# Optimizing a Trainium2 kernel written in Bass

```python
import numpy as np
import jax
import jax.numpy as jnp

def _softmax(x, axis=-1):
    return jax.nn.softmax(x, axis=axis)

def _gelu(x):
    return jax.nn.gelu(x, approximate=True)

def _silu(x):
    return jax.nn.silu(x)

def _sigmoid(x):
    return jax.nn.sigmoid(x)

def _layernorm(x, axis=-1, eps=1e-05):
    m = jnp.mean(x, axis=axis, keepdims=True)
    v = jnp.var(x, axis=axis, keepdims=True)
    return (x - m) / jnp.sqrt(v + eps)

def _scatter_add(tgt, idx, src, axis=0):
    return tgt.at[idx].add(src)

def _segment_sum(src, seg, n):
    return jax.ops.segment_sum(src, seg, n)
kernel_name = 'mk_early_fusion_d2_tok_img512_r4_6f2d3e'

def setup_inputs(seed: int=0):
    np.random.seed(seed)
    _w = jnp.asarray

    def _rec_inputs():
        import jax
        import jax.numpy as jnp
        _rk = jax.random.key(seed)
        x = -0.000392918 + 0.999932 * jax.random.normal(jax.random.fold_in(_rk, 1), (32, 1, 128, 128), jnp.float32)
        txt = 0.229487 + 0.681011 * jax.random.normal(jax.random.fold_in(_rk, 2), (32, 77, 128), jnp.float32)
        return (x, txt)
    x, txt = _rec_inputs()

    def _L0_tok_setup():
        import math
        import jax, jax.numpy as jnp
        import numpy as np
        PW = PH = 16
        EMB = 128
        HID = 128
        B, H, W = (64, 128, 128)
        L = H // PW * (W // PH)
        SIGMA_ZERO = 0.1

        def _f_noise(x):
            return jnp.sign(x) * jnp.sqrt(jnp.abs(x))

        def _noisy_linear(x, w, b, sw, sb, eps_in, eps_out):
            ei = _f_noise(eps_in)
            eo = _f_noise(eps_out)
            w_n = w + sw * (eo[:, None] * ei[None, :])
            b_n = b + sb * eo
            return x @ w_n.T + b_n

        def _unfold_patches(x):
            b = x.shape[0]
            p = x.reshape(b, H // PW, PW, W // PH, PH)
            p = p.transpose(0, 1, 3, 2, 4)
            return p.reshape(b, L, PW * PH)

        def _pos_encoding(x):
            pos = jnp.arange(L, dtype=jnp.float32)[:, None]
            div = jnp.exp(jnp.arange(0, EMB, 2, dtype=jnp.float32) * (-math.log(10000.0) / EMB))
            ang = pos * div
            pe = jnp.stack([jnp.sin(ang), jnp.cos(ang)], axis=-1).reshape(L, EMB)
            return x + pe[None, :, :]
        key = jax.random.key(seed)
        ks = jax.random.split(key, 12)
        in_f = PW * PH
        sig = SIGMA_ZERO / math.sqrt(in_f)
        bnd1 = 1.0 / math.sqrt(in_f)
        bnd3 = 1.0 / math.sqrt(HID)
        u = lambda k, shape, bnd: jax.random.uniform(k, shape, jnp.float32, -bnd, bnd)
        return {'inputs': jax.random.normal(ks[0], (B, 1, H, W), jnp.float32), 'W1_w': u(ks[1], (HID, in_f), bnd1), 'W1_b': u(ks[2], (HID,), bnd1), 'W1_sw': jnp.full((HID, in_f), sig, jnp.float32), 'W1_sb': jnp.full((HID,), sig, jnp.float32), 'W2_w': u(ks[3], (HID, in_f), bnd1), 'W2_b': u(ks[4], (HID,), bnd1), 'W2_sw': jnp.full((HID, in_f), sig, jnp.float32), 'W2_sb': jnp.full((HID,), sig, jnp.float32), 'W3_w': u(ks[5], (EMB, HID), bnd3), 'W3_b': u(ks[6], (EMB,), bnd3), 'eps_in1': jax.random.normal(ks[7], (in_f,), jnp.float32), 'eps_out1': jax.random.normal(ks[8], (HID,), jnp.float32), 'eps_in2': jax.random.normal(ks[9], (in_f,), jnp.float32), 'eps_out2': jax.random.normal(ks[10], (HID,), jnp.float32)}
    _L0_tok_all = _L0_tok_setup()
    _L0_tok_in = {k: v for k, v in _L0_tok_all.items() if k in ('W1_w', 'W1_b', 'W1_sw', 'W1_sb', 'W2_w', 'W2_b', 'W2_sw', 'W2_sb', 'W3_w', 'W3_b', 'eps_in1', 'eps_out1', 'eps_in2', 'eps_out2')}
    del _L0_tok_all

    def _L0_attn_setup():
        import jax, jax.numpy as jnp
        import numpy as np
        DIM = 128
        IN_DIM = 128
        SCALE = 1.0 / float(np.sqrt(DIM))
        key = jax.random.key(seed)
        k1, k2, k3 = jax.random.split(key, 3)
        B, N = (8, 1024)
        x = jax.random.normal(k1, (B, N, DIM), dtype=jnp.float32)
        w_qkv = jax.random.normal(k2, (3 * IN_DIM, DIM), dtype=jnp.float32) * 0.02
        w_proj = jax.random.normal(k3, (IN_DIM, IN_DIM), dtype=jnp.float32) * 0.02
        b_proj = jnp.zeros((IN_DIM,), dtype=jnp.float32)
        return {'x': x, 'w_qkv': w_qkv, 'w_proj': w_proj, 'b_proj': b_proj}
    _L0_attn_all = _L0_attn_setup()
    _L0_attn_in = {k: v for k, v in _L0_attn_all.items() if k in ('w_qkv', 'w_proj', 'b_proj')}
    del _L0_attn_all

    def _L0_ffn_setup():
        import jax, jax.numpy as jnp
        import numpy as np
        B, S, D, F, E = (8, 1024, 128, 512, 8)
        INIT_LAMBDA = 0.2
        LN_EPS = 1e-05
        LN_MERGE = 0.03
        key = jax.random.key(seed)
        ks = jax.random.split(key, 12)
        n = lambda k, shp, s=1.0: jax.random.normal(k, shp, dtype=jnp.float32) * s
        return {'hidden_states': n(ks[0], (B, S, D)), 'gfc1_w': n(ks[1], (D, D), 0.01), 'gfc1_b': jnp.zeros((D,), jnp.float32), 'gfc2_w': n(ks[2], (E, D), 0.01), 'gfc2_b': jnp.full((E,), INIT_LAMBDA, dtype=jnp.float32), 'W1': n(ks[3], (F, D), 0.02), 'b1': jnp.zeros((F,), jnp.float32), 'W2': n(ks[4], (D, F), 0.02), 'b2': jnp.zeros((D,), jnp.float32), 'ln_g': jnp.ones((D,), jnp.float32), 'ln_b': jnp.zeros((D,), jnp.float32), 'tv_W1': n(ks[5], (E, F, D), 0.02), 'tv_b1': n(ks[6], (E, F), 0.02), 'tv_W2': n(ks[7], (E, D, F), 0.02), 'tv_b2': n(ks[8], (E, D), 0.02), 'tv_ln_g': n(ks[9], (E, D), 0.02), 'tv_ln_b': n(ks[10], (E, D), 0.02)}
    _L0_ffn_all = _L0_ffn_setup()
    _L0_ffn_in = {k: v for k, v in _L0_ffn_all.items() if k in ('gfc1_w', 'gfc1_b', 'gfc2_w', 'gfc2_b', 'W1', 'b1', 'W2', 'b2', 'ln_g', 'ln_b', 'tv_W1', 'tv_b1', 'tv_W2', 'tv_b2', 'tv_ln_g', 'tv_ln_b')}
    del _L0_ffn_all

    def _L1_attn_setup():
        import jax, jax.numpy as jnp
        import numpy as np
        EMB = 128
        HEADS = 8
        HEAD_DIM = EMB // HEADS

        def _split_heads(t):
            b, n, _ = t.shape
            return t.reshape(b, n, HEADS, HEAD_DIM).transpose(0, 2, 1, 3)
        key = jax.random.key(seed)
        ks = jax.random.split(key, 9)
        s = 1.0 / np.sqrt(EMB)
        return {'x': jax.random.normal(ks[0], (4, 512, EMB), dtype=jnp.float32), 'Wq': jax.random.uniform(ks[1], (EMB, EMB), jnp.float32, -s, s), 'bq': jax.random.uniform(ks[2], (EMB,), jnp.float32, -s, s), 'Wk': jax.random.uniform(ks[3], (EMB, EMB), jnp.float32, -s, s), 'bk': jax.random.uniform(ks[4], (EMB,), jnp.float32, -s, s), 'Wv': jax.random.uniform(ks[5], (EMB, EMB), jnp.float32, -s, s), 'bv': jax.random.uniform(ks[6], (EMB,), jnp.float32, -s, s), 'Wp': jax.random.uniform(ks[7], (EMB, EMB), jnp.float32, -s, s), 'bp': jax.random.uniform(ks[8], (EMB,), jnp.float32, -s, s)}
    _L1_attn_all = _L1_attn_setup()
    _L1_attn_in = {k: v for k, v in _L1_attn_all.items() if k in ('Wq', 'bq', 'Wk', 'bk', 'Wv', 'bv', 'Wp', 'bp')}
    del _L1_attn_all

    def _L1_ffn_setup():
        import jax, jax.numpy as jnp
        import numpy as np
        DIM = 128
        HID = 256
        E = 8
        K = 2
        B, S = (4, 512)
        key = jax.random.key(seed)
        ks = jax.random.split(key, 10)
        sd = DIM ** (-0.5)
        sh = HID ** (-0.5)
        return {'x': jax.random.normal(ks[0], (B, S, DIM), dtype=jnp.float32), 'gate_w': jax.random.normal(ks[1], (E, DIM), dtype=jnp.float32) * sd, 'biases': jnp.zeros((E,), dtype=jnp.float32), 'w1': jax.random.normal(ks[2], (E, DIM, HID), dtype=jnp.float32) * sd, 'w3': jax.random.normal(ks[3], (E, DIM, HID), dtype=jnp.float32) * sd, 'w2': jax.random.normal(ks[4], (E, HID, DIM), dtype=jnp.float32) * sh, 'sw1': jax.random.normal(ks[5], (DIM, HID), dtype=jnp.float32) * sd, 'sw3': jax.random.normal(ks[6], (DIM, HID), dtype=jnp.float32) * sd, 'sw2': jax.random.normal(ks[7], (HID, DIM), dtype=jnp.float32) * sh}
    _L1_ffn_all = _L1_ffn_setup()
    _L1_ffn_in = {k: v for k, v in _L1_ffn_all.items() if k in ('gate_w', 'biases', 'w1', 'w3', 'w2', 'sw1', 'sw3', 'sw2')}
    del _L1_ffn_all
    return {'x': x, 'txt': txt, 'L0_tok_W1_w': _L0_tok_in['W1_w'], 'L0_tok_W1_b': _L0_tok_in['W1_b'], 'L0_tok_W1_sw': _L0_tok_in['W1_sw'], 'L0_tok_W1_sb': _L0_tok_in['W1_sb'], 'L0_tok_W2_w': _L0_tok_in['W2_w'], 'L0_tok_W2_b': _L0_tok_in['W2_b'], 'L0_tok_W2_sw': _L0_tok_in['W2_sw'], 'L0_tok_W2_sb': _L0_tok_in['W2_sb'], 'L0_tok_W3_w': _L0_tok_in['W3_w'], 'L0_tok_W3_b': _L0_tok_in['W3_b'], 'L0_tok_eps_in1': _L0_tok_in['eps_in1'], 'L0_tok_eps_out1': _L0_tok_in['eps_out1'], 'L0_tok_eps_in2': _L0_tok_in['eps_in2'], 'L0_tok_eps_out2': _L0_tok_in['eps_out2'], 'L0_attn_w_qkv': _L0_attn_in['w_qkv'], 'L0_attn_w_proj': _L0_attn_in['w_proj'], 'L0_attn_b_proj': _L0_attn_in['b_proj'], 'L0_ffn_gfc1_w': _L0_ffn_in['gfc1_w'], 'L0_ffn_gfc1_b': _L0_ffn_in['gfc1_b'], 'L0_ffn_gfc2_w': _L0_ffn_in['gfc2_w'], 'L0_ffn_gfc2_b': _L0_ffn_in['gfc2_b'], 'L0_ffn_W1': _L0_ffn_in['W1'], 'L0_ffn_b1': _L0_ffn_in['b1'], 'L0_ffn_W2': _L0_ffn_in['W2'], 'L0_ffn_b2': _L0_ffn_in['b2'], 'L0_ffn_ln_g': _L0_ffn_in['ln_g'], 'L0_ffn_ln_b': _L0_ffn_in['ln_b'], 'L0_ffn_tv_W1': _L0_ffn_in['tv_W1'], 'L0_ffn_tv_b1': _L0_ffn_in['tv_b1'], 'L0_ffn_tv_W2': _L0_ffn_in['tv_W2'], 'L0_ffn_tv_b2': _L0_ffn_in['tv_b2'], 'L0_ffn_tv_ln_g': _L0_ffn_in['tv_ln_g'], 'L0_ffn_tv_ln_b': _L0_ffn_in['tv_ln_b'], 'L1_attn_Wq': _L1_attn_in['Wq'], 'L1_attn_bq': _L1_attn_in['bq'], 'L1_attn_Wk': _L1_attn_in['Wk'], 'L1_attn_bk': _L1_attn_in['bk'], 'L1_attn_Wv': _L1_attn_in['Wv'], 'L1_attn_bv': _L1_attn_in['bv'], 'L1_attn_Wp': _L1_attn_in['Wp'], 'L1_attn_bp': _L1_attn_in['bp'], 'L1_ffn_gate_w': _L1_ffn_in['gate_w'], 'L1_ffn_biases': _L1_ffn_in['biases'], 'L1_ffn_w1': _L1_ffn_in['w1'], 'L1_ffn_w3': _L1_ffn_in['w3'], 'L1_ffn_w2': _L1_ffn_in['w2'], 'L1_ffn_sw1': _L1_ffn_in['sw1'], 'L1_ffn_sw3': _L1_ffn_in['sw3'], 'L1_ffn_sw2': _L1_ffn_in['sw2']}

def reference(x, txt, L0_tok_W1_w, L0_tok_W1_b, L0_tok_W1_sw, L0_tok_W1_sb, L0_tok_W2_w, L0_tok_W2_b, L0_tok_W2_sw, L0_tok_W2_sb, L0_tok_W3_w, L0_tok_W3_b, L0_tok_eps_in1, L0_tok_eps_out1, L0_tok_eps_in2, L0_tok_eps_out2, L0_attn_w_qkv, L0_attn_w_proj, L0_attn_b_proj, L0_ffn_gfc1_w, L0_ffn_gfc1_b, L0_ffn_gfc2_w, L0_ffn_gfc2_b, L0_ffn_W1, L0_ffn_b1, L0_ffn_W2, L0_ffn_b2, L0_ffn_ln_g, L0_ffn_ln_b, L0_ffn_tv_W1, L0_ffn_tv_b1, L0_ffn_tv_W2, L0_ffn_tv_b2, L0_ffn_tv_ln_g, L0_ffn_tv_ln_b, L1_attn_Wq, L1_attn_bq, L1_attn_Wk, L1_attn_bk, L1_attn_Wv, L1_attn_bv, L1_attn_Wp, L1_attn_bp, L1_ffn_gate_w, L1_ffn_biases, L1_ffn_w1, L1_ffn_w3, L1_ffn_w2, L1_ffn_sw1, L1_ffn_sw3, L1_ffn_sw2):
    import jax
    import jax.numpy as jnp

    def _L0_tok_ref(inputs, W1_w, W1_b, W1_sw, W1_sb, W2_w, W2_b, W2_sw, W2_sb, W3_w, W3_b, eps_in1, eps_out1, eps_in2, eps_out2):
        import math
        import jax, jax.numpy as jnp
        import numpy as np
        PW = PH = 16
        EMB = 128
        HID = 128
        B, H, W = (64, 128, 128)
        L = H // PW * (W // PH)
        SIGMA_ZERO = 0.1

        def _f_noise(x):
            return jnp.sign(x) * jnp.sqrt(jnp.abs(x))

        def _noisy_linear(x, w, b, sw, sb, eps_in, eps_out):
            ei = _f_noise(eps_in)
            eo = _f_noise(eps_out)
            w_n = w + sw * (eo[:, None] * ei[None, :])
            b_n = b + sb * eo
            return x @ w_n.T + b_n

        def _unfold_patches(x):
            b = x.shape[0]
            p = x.reshape(b, H // PW, PW, W // PH, PH)
            p = p.transpose(0, 1, 3, 2, 4)
            return p.reshape(b, L, PW * PH)

        def _pos_encoding(x):
            pos = jnp.arange(L, dtype=jnp.float32)[:, None]
            div = jnp.exp(jnp.arange(0, EMB, 2, dtype=jnp.float32) * (-math.log(10000.0) / EMB))
            ang = pos * div
            pe = jnp.stack([jnp.sin(ang), jnp.cos(ang)], axis=-1).reshape(L, EMB)
            return x + pe[None, :, :]
        x = _unfold_patches(inputs)
        g = _noisy_linear(x, W1_w, W1_b, W1_sw, W1_sb, eps_in1, eps_out1)
        x_gate = g * jnp.tanh(jax.nn.softplus(g))
        x_inner = _noisy_linear(x, W2_w, W2_b, W2_sw, W2_sb, eps_in2, eps_out2)
        x = x_gate * x_inner
        x = x @ W3_w.T + W3_b
        return _pos_encoding(x)

    def _L0_attn_ref(x, w_qkv, w_proj, b_proj):
        import jax, jax.numpy as jnp
        import numpy as np
        DIM = 128
        IN_DIM = 128
        SCALE = 1.0 / float(np.sqrt(DIM))
        qkv = jnp.einsum('bnc,fc->bnf', x, w_qkv)
        B, N, _ = qkv.shape
        qkv = qkv.reshape(B, N, 3, IN_DIM)
        q, k, v = (qkv[:, :, 0], qkv[:, :, 1], qkv[:, :, 2])
        attn = jax.nn.softmax(jnp.einsum('bnd,bmd->bnm', q, k) * SCALE, axis=-1)
        o = jnp.einsum('bnm,bmd->bnd', attn, v)
        o = jnp.einsum('bnd,ed->bne', o, w_proj) + b_proj
        return v + o

    def _L0_ffn_ref(hidden_states, gfc1_w, gfc1_b, gfc2_w, gfc2_b, W1, b1, W2, b2, ln_g, ln_b, tv_W1, tv_b1, tv_W2, tv_b2, tv_ln_g, tv_ln_b):
        import jax, jax.numpy as jnp
        import numpy as np
        B, S, D, F, E = (8, 1024, 128, 512, 8)
        INIT_LAMBDA = 0.2
        LN_EPS = 1e-05
        LN_MERGE = 0.03
        x = hidden_states
        gh = jax.nn.relu(jnp.einsum('bsd,hd->bsh', x, gfc1_w) + gfc1_b)
        g = (jnp.einsum('bsh,eh->bse', gh, gfc2_w) + gfc2_b).mean(axis=1)
        W1m = W1 + jnp.einsum('be,efd->bfd', g, tv_W1)
        b1m = b1 + g @ tv_b1
        W2m = W2 + jnp.einsum('be,edf->bdf', g, tv_W2)
        b2m = b2 + g @ tv_b2
        lng = ln_g + LN_MERGE * (tv_ln_g - ln_g).sum(axis=0)
        lnb = ln_b + LN_MERGE * (tv_ln_b - ln_b).sum(axis=0)
        h = jax.nn.relu(jnp.einsum('bsd,bfd->bsf', x, W1m) + b1m[:, None, :])
        out = jnp.einsum('bsf,bdf->bsd', h, W2m) + b2m[:, None, :]
        res = x + out
        mu = res.mean(axis=-1, keepdims=True)
        var = res.var(axis=-1, keepdims=True)
        return (res - mu) * jax.lax.rsqrt(var + LN_EPS) * lng + lnb

    def _L1_attn_ref(x, Wq, bq, Wk, bk, Wv, bv, Wp, bp):
        import jax, jax.numpy as jnp
        import numpy as np
        EMB = 128
        HEADS = 8
        HEAD_DIM = EMB // HEADS

        def _split_heads(t):
            b, n, _ = t.shape
            return t.reshape(b, n, HEADS, HEAD_DIM).transpose(0, 2, 1, 3)
        q = _split_heads(x @ Wq.T + bq)
        k = _split_heads(x @ Wk.T + bk)
        v = _split_heads(x @ Wv.T + bv)
        energy = jnp.einsum('bhqd,bhkd->bhqk', q, k)
        att = jax.nn.softmax(energy, axis=-1) / jnp.sqrt(jnp.float32(EMB))
        out = jnp.einsum('bhqk,bhkd->bhqd', att, v)
        b, h, n, d = out.shape
        out = out.transpose(0, 2, 1, 3).reshape(b, n, h * d)
        return out @ Wp.T + bp

    def _L1_ffn_ref(x, gate_w, biases, w1, w3, w2, sw1, sw3, sw2):
        import jax, jax.numpy as jnp
        import numpy as np
        DIM = 128
        HID = 256
        E = 8
        K = 2
        B, S = (4, 512)
        Bb, Ss, D = x.shape
        xt = x.reshape(Bb * Ss, D)
        shared = jax.nn.silu(xt @ sw1) * (xt @ sw3) @ sw2
        scores = xt @ gate_w.T
        _, idx = jax.lax.top_k(scores + biases, K)
        topv, _ = jax.lax.top_k(scores, K)
        p = jax.nn.sigmoid(topv)
        p = p / jnp.sum(p, axis=-1, keepdims=True)
        h = jax.nn.silu(jnp.einsum('td,edh->eth', xt, w1)) * jnp.einsum('td,edh->eth', xt, w3)
        y = jnp.einsum('eth,ehd->etd', h, w2)
        onehot = jax.nn.one_hot(idx, E, dtype=xt.dtype)
        comb = jnp.einsum('tk,tke->te', p, onehot)
        out = jnp.einsum('te,etd->td', comb, y) + shared
        return out.reshape(Bb, Ss, D)
    h = _L0_tok_ref(x, L0_tok_W1_w, L0_tok_W1_b, L0_tok_W1_sw, L0_tok_W1_sb, L0_tok_W2_w, L0_tok_W2_b, L0_tok_W2_sw, L0_tok_W2_sb, L0_tok_W3_w, L0_tok_W3_b, L0_tok_eps_in1, L0_tok_eps_out1, L0_tok_eps_in2, L0_tok_eps_out2)
    h = jnp.concatenate([h, txt], axis=1)
    h = h + _L0_attn_ref(_layernorm(h, axis=-1), L0_attn_w_qkv, L0_attn_w_proj, L0_attn_b_proj)
    h = h + _L0_ffn_ref(_layernorm(h, axis=-1), L0_ffn_gfc1_w, L0_ffn_gfc1_b, L0_ffn_gfc2_w, L0_ffn_gfc2_b, L0_ffn_W1, L0_ffn_b1, L0_ffn_W2, L0_ffn_b2, L0_ffn_ln_g, L0_ffn_ln_b, L0_ffn_tv_W1, L0_ffn_tv_b1, L0_ffn_tv_W2, L0_ffn_tv_b2, L0_ffn_tv_ln_g, L0_ffn_tv_ln_b)
    h = h + _L1_attn_ref(_layernorm(h, axis=-1), L1_attn_Wq, L1_attn_bq, L1_attn_Wk, L1_attn_bk, L1_attn_Wv, L1_attn_bv, L1_attn_Wp, L1_attn_bp)
    h = h + _L1_ffn_ref(_layernorm(h, axis=-1), L1_ffn_gate_w, L1_ffn_biases, L1_ffn_w1, L1_ffn_w3, L1_ffn_w2, L1_ffn_sw1, L1_ffn_sw3, L1_ffn_sw2)
    return h

_drawn_inputs = setup_inputs


def setup_inputs(seed=0):
    import zlib

    import numpy as np

    out = dict(_drawn_inputs(seed))
    spreads = {'L0_tok_W1_sw': (0.0062500000931322575, 0.6),
     'L0_tok_W1_sb': (0.0062500000931322575, 0.6),
     'L0_tok_W2_sw': (0.0062500000931322575, 0.6),
     'L0_tok_W2_sb': (0.0062500000931322575, 0.6),
     'L0_attn_b_proj': (0.0, 0.1),
     'L0_ffn_gfc1_b': (0.0, 0.614),
     'L0_ffn_gfc2_b': (0.20000000298023224, 0.6),
     'L0_ffn_b1': (0.0, 0.1),
     'L0_ffn_b2': (0.0, 0.1),
     'L0_ffn_ln_g': (1.0, 0.2),
     'L0_ffn_ln_b': (0.0, 0.1),
     'L1_ffn_biases': (0.0, 0.1)}
    factors = {'L0_ffn_gfc1_w': 8.0,
     'L0_ffn_gfc2_w': 5.448,
     'L0_ffn_tv_b1': 5.058,
     'L0_ffn_tv_b2': 2.994,
     'L0_ffn_tv_ln_g': 5.555,
     'L0_ffn_tv_ln_b': 8.0,
     'L1_attn_Wq': 2.965,
     'L1_attn_bq': 8.0,
     'L1_attn_Wk': 3.24,
     'L1_attn_bk': 8.0,
     'L1_attn_Wv': 2.748,
     'L1_attn_bv': 5.58,
     'L1_attn_Wp': 2.873}
    for name, (base, spread) in spreads.items():
        noise = np.random.default_rng([zlib.crc32(name.encode()), seed]).standard_normal(out[name].shape)
        drawn = base * np.exp(spread * noise) if base else spread * noise
        out[name] = jnp.asarray(drawn.astype(out[name].dtype))
    for name, factor in factors.items():
        out[name] = (out[name] * factor).astype(out[name].dtype)
    return out
```

```python
from contextlib import ExitStack

import concourse.bass as bass
from concourse import mybir

P = 128
B, NP_, NT, D = 32, 64, 77, 128
N = NP_ + NT
T = B * N
NTAIL = N - P
CH = 376
NCH = T // CH
SUB = 94
NSUB = CH // SUB
H, HD = 8, 16
HT = H * NTAIL
E = 8
F = 512
HID = 256
FW = F + 5
GB = 2 * N
LN_EPS = 1e-5
LN_MERGE = 0.03
BIG = 3.0e38

ALU = mybir.AluOpType
ACT = mybir.ActivationFunctionType
AX = mybir.AxisListType.X
F32 = mybir.dt.float32

CONST = {}
_at = 0
for _name, _n in (("ident", 128), ("centre", 128), ("average", 128), ("pos", NP_), ("jmask", 8),
                  ("hmask", H), ("vmask", 128), ("tmask", HT), ("dsel", NTAIL), ("rep", 72),
                  ("select", E * 128), ("rank", E)):
    CONST[_name] = (_at, _n)
    _at += _n
NCONST = _at

VECS = ["W1_b", "W1_sb", "W2_b", "W2_sb", "eps_out1", "eps_out2", "W3_b", "b_proj", "gfc1_b", "b2",
        "ln_g", "ln_b", "bq", "bk", "bv", "bp", "b1n", "b2n", "eo1", "eo2", "lng", "lnb", "bpn",
        "eps", "tmp0", "tmp1", "b3", "spare"]
VEC = {n: i for i, n in enumerate(VECS)}

SLOT = {n: i for i, n in enumerate(["W3", "gfc1", "proj", "v0", "Wq", "Wk", "Wv", "Wp",
                                    "n1a", "n1b", "n2a", "n2b", "gfc2", "gate", "tvg", "tvs"])}


PHASES = ["ln1", "attn0", "ln2", "ffn", "lnf", "lna", "attn1", "lnm", "gate", "moe"]
NORMS = ["ln1", "ln2", "lnf", "lna", "lnm"]


def is_known(u):
    return isinstance(u, int)


def reuse(eng, sem, u, depth):
    if is_known(u):
        if u >= depth:
            eng.wait_ge(sem, u - depth + 1)
    else:
        eng.wait_ge(sem, u - depth + 1)


def reuse3(eng, sem, u):
    if not is_known(u) or u >= 2:
        eng.wait_ge(sem, u * 3 - 3)


def run_steps(eng, units, lag, body, head):
    total = units + lag
    rounds = (units - head) // 2
    for t in range(head):
        body(t, t % 2)
    with eng.Fori(0, rounds) as i:
        for r in range(2):
            body(i * 2 + (head + r), r)
    for t in range(head + 2 * rounds, total):
        body(t, t % 2)


def live(t, k, units):
    return not is_known(t) or 0 <= t - k < units


def early_fusion(nc, x, txt, tok, attn0, ffn, attn1, moe, const, out, stop=99):
    with ExitStack() as ctx:
        def sb(name, shape):
            return ctx.enter_context(nc.sbuf_tensor(name, shape, F32))

        sems = {}

        def S(name):
            if name not in sems:
                sems[name] = ctx.enter_context(nc.semaphore(name))
            return sems[name]

        ps = [ctx.enter_context(nc.psum_tensor(f"ps{i}", [P, 512], F32)) for i in range(2)]
        ps3a = ctx.enter_context(nc.psum_tensor("ps3a", [P, 3, 512], F32))
        ps3b = ctx.enter_context(nc.psum_tensor("ps3b", [P, 3, 512], F32))
        bank = [ps[0][:, :], ps[1][:, :]] + [ps3a[:, i, :] for i in range(3)] + [ps3b[:, i, :] for i in range(3)]

        hT = sb("hT", [P, T])
        xn = sb("xn", [P, T])
        cst = sb("cst", [P, NCONST])
        vec = sb("vec", [P, len(VECS)])
        wT = sb("wT", [P, len(SLOT), P])
        pq = sb("pq", [P, 2, P])
        small = sb("small", [P, 64])
        arena = sb("arena", [P, B * FW + B * F])

        def C(name, rows=P):
            a, n = CONST[name]
            return cst[0:rows, a:a + n]

        def V(name, rows=P):
            return vec[0:rows, VEC[name]:VEC[name] + 1]

        def W(name):
            return wT[:, SLOT[name], :]

        used = [0]

        def take(n):
            a = used[0]
            used[0] += n
            assert used[0] <= B * FW + B * F, used[0]
            return arena[:, a:a + n]

        ident = C("ident")

        xp = take(2 * 2048).rearrange("p (t r w c) -> p t r w c", t=2, r=16, w=8)
        xq = take(2 * 2048).rearrange("p (t w n) -> p t w n", t=2, w=8)
        xT = take(2 * 2048).rearrange("p (k n) -> p k n", k=2)
        wN = take(len(SLOT) * P).rearrange("p (s c) -> p s c", s=len(SLOT))
        wqk = take(2 * P).rearrange("p (s c) -> p s c", s=2)
        txn = take(B * D).rearrange("p (b d) -> p b d", b=B)
        sw = take(2 * 256).rearrange("p (k n) -> p k n", k=2)
        wraw = take(2 * 256).rearrange("p (k n) -> p k n", k=2)
        ei = take(2 * 256).rearrange("p (k n) -> p k n", k=2)
        ea = take(2 * 256).rearrange("p (k n) -> p k n", k=2)
        mish = take(6 * 512).rearrange("p (k n) -> p k n", k=6)
        tokx = take(2 * 512).rearrange("p (k n) -> p k n", k=2)
        tvln = sb("tvln", [P, 2, E])
        LNW = 4 * CH
        ln_a = arena[:, B * (FW + F) - LNW:B * (FW + F)].rearrange("p (k n) -> p k n", k=4)
        used[0] = 0
        a_u = take(2 * N).rearrange("p (k n) -> p k n", k=2)
        a_x = take(2 * N).rearrange("p (k n) -> p k n", k=2)
        a_v = take(2 * 2 * P).rearrange("p (k m n) -> p k m n", k=2, m=2)
        a_e = take(2 * 2 * N).rearrange("p (k m n) -> p k m n", k=2, m=2)
        a_t = take(2 * 2 * N).rearrange("p (k m n) -> p k m n", k=2, m=2)
        a_m = take(2 * 6).rearrange("p (k m) -> p k m", k=2)
        used[0] = 0
        w1m = take(B * FW).rearrange("p (b f) -> p b f", b=B)
        w2m = take(B * F).rearrange("p (b f) -> p b f", b=B)
        tvc = sb("tvc", [72, 2, 1024])
        tvb = sb("tvb", [E + 1, F + D])
        g9 = sb("g9", [E + 1, B + 1])
        gblk = sb("gblk", [72, 8, B])
        gcol = sb("gcol", [72, B])
        ghm = sb("ghm", [P, B])
        wst = sb("wst", [P, 2, FW + F])
        hbuf = sb("hbuf", [P, 2, 4, N])
        used[0] = 0
        b_x = take(2 * N).rearrange("p (k n) -> p k n", k=2)
        b_xt = take(2 * HT).rearrange("p (k n) -> p k n", k=2)
        b_ek = take(2 * HT).rearrange("p (k n) -> p k n", k=2)
        b_q = take(2 * N).rearrange("p (k n) -> p k n", k=2)
        b_k = take(2 * N).rearrange("p (k n) -> p k n", k=2)
        b_km = take(2 * H * N).rearrange("p (k h n) -> p k h n", k=2, h=H)
        b_qm = take(2 * HT).rearrange("p (k h n) -> p k h n", k=2, h=H)
        b_v = take(2 * H * P).rearrange("p (k h n) -> p k h n", k=2, h=H)
        b_vt = take(2 * P).rearrange("p (k n) -> p k n", k=2)
        b_nm = take(2 * 9).rearrange("p (k h) -> p k h", k=2)
        b_s = take(2 * 9).rearrange("p (k h) -> p k h", k=2)
        b_r = take(2 * 9).rearrange("p (k h) -> p k h", k=2)
        b_e = take(2 * 9 * N).rearrange("p (k h n) -> p k h n", k=2, h=9)
        b_tt = take(2 * HT).rearrange("p (k n) -> p k n", k=2)
        b_et = take(2 * H * N).rearrange("p (k h n) -> p k h n", k=2, h=H)
        b_ett = take(2 * N).rearrange("p (k n) -> p k n", k=2)
        b_o = take(2 * N).rearrange("p (k n) -> p k n", k=2)
        used[0] = 13600
        m_w1 = take((E + 1) * HID).rearrange("p (e h) -> p e h", e=E + 1)
        m_w3 = take((E + 1) * HID).rearrange("p (e h) -> p e h", e=E + 1)
        m_w2 = take((E + 1) * HID).rearrange("p (e k d) -> p e k d", e=E + 1, k=2)
        m_bias = take(E)
        assert used[0] <= B * (FW + F) - LNW
        used[0] = 0
        m_sc = take(2 * CH).rearrange("p (k n) -> p k n", k=2)
        m_s = take(NCH * NSUB * E).rearrange("p (s e) -> p s e", e=E)
        m_t = [take(NCH * NSUB * E).rearrange("p (s e) -> p s e", e=E) for _ in range(4)]
        m_1 = [take(NCH * NSUB) for _ in range(5)]
        m_ct = take(T)
        m_cb = take(2 * CH).rearrange("p (k n) -> p k n", k=2)
        m_a = take(3 * CH).rearrange("p (k n) -> p k n", k=3)
        m_g = take(3 * CH).rearrange("p (k n) -> p k n", k=3)
        m_h = take(3 * CH).rearrange("p (k n) -> p k n", k=3)
        m_f = take(2 * CH).rearrange("p (k n) -> p k n", k=2)
        m_o = take(2 * NSUB * D).rearrange("p (k s d) -> p k s d", k=2, s=NSUB)


        assert used[0] <= 13600

        def chunk(buf, c, n=CH):
            return buf[:, bass.ds(c * n, n)]

        def sample(buf, b):
            return buf[:, bass.ds(b * N, N)]

        def meet(eng, phase):
            eng.drain().then_inc(S("phases_met"), 1)
            eng.wait_ge(S("phases_met"), 5 * (PHASES.index(phase) + 1))

        def merged_dst(w, c, s):
            if w == 0:
                return w1m[:, :, 0:F].rearrange("p b (j g) -> p g j b", j=8)[:, bass.ds(c * 8 + 2 * s, 2)]
            v = w2m[:, :, :].rearrange("p b (k j g) -> p g k j b", k=4, j=8)
            return v[:, bass.ds(c * 2 + s // 2, 1), 2 * (s % 2):2 * (s % 2) + 2].rearrange("p a k j b -> p (a k) j b")

        turns = []
        for t in range(2):
            for k in range(2):
                for half in range(2):
                    turns.append(("x", [(xq[:, t, 4 * half + i, k * P:(k + 1) * P], P) for i in range(4)],
                                  xT[:, k, t * 1024:(t + 1) * 1024].rearrange("p (q w) -> p w q", w=8)[:, 4 * half:4 * half + 4, :], P))
        for g in range(4):
            n = min(4, len(SLOT) - 4 * g)
            rows = P if g < 3 else E
            turns.append(("w" if g == 2 else "n",
                          [(wN[0:rows, 4 * g + i, :], rows) for i in range(n)],
                          wT[:, 4 * g:4 * g + n, 0:rows], rows))
        for g in range(8):
            turns.append(("t", [(txn[0:NT, 4 * g + i, :], NT) for i in range(4)],
                          hT[:, 4 * g * N:(4 * g + 4) * N].rearrange("p (b n) -> p b n", n=N)[:, :, NP_:N], NT))

        block = ctx.enter_context(nc.Block())

        @block.sync
        def _(sp):
            sp.dma_start(cst[:, :], const).then_inc(S("const_in"), 16)
            for t in range(2):
                sp.dma_start(xp[:, t].rearrange("p r w c -> p (r w c)"),
                             x[16 * t:16 * t + 16].rearrange("b o (q r) w -> (b o q) (r w)", q=8)).then_inc(S(f"x_in{t}"), 16)
            for k, n in enumerate(("1", "2")):
                sp.dma_start(wraw[:, k, :], tok[f"W{n}_w"]).then_inc(S("noise_in"), 16)
                sp.dma_start(sw[:, k, :], tok[f"W{n}_sw"]).then_inc(S("noise_in"), 16)
                sp.dma_start(ei[:, k, :], tok[f"eps_in{n}"].unsqueeze(0).to_broadcast([P, 256])).then_inc(S("noise_in"), 16)
            vsrc = {"W1_b": tok["W1_b"], "W1_sb": tok["W1_sb"], "W2_b": tok["W2_b"], "W2_sb": tok["W2_sb"],
                    "eps_out1": tok["eps_out1"], "eps_out2": tok["eps_out2"], "W3_b": tok["W3_b"],
                    "b_proj": attn0["b_proj"], "gfc1_b": ffn["gfc1_b"], "b2": ffn["b2"], "ln_g": ffn["ln_g"],
                    "ln_b": ffn["ln_b"], "bq": attn1["bq"], "bk": attn1["bk"], "bv": attn1["bv"], "bp": attn1["bp"]}
            for n, a in vsrc.items():
                sp.dma_start(V(n), a.unsqueeze(1)).then_inc(S("vec_in"), 16)
            nat = {"W3": tok["W3_w"], "gfc1": ffn["gfc1_w"], "proj": attn0["w_proj"], "v0": attn0["w_qkv"][256:384],
                   "Wq": attn1["Wq"], "Wk": attn1["Wk"], "Wv": attn1["Wv"], "Wp": attn1["Wp"]}
            for n, a in nat.items():
                sp.dma_start(wN[:, SLOT[n], :], a).then_inc(S("nat_in"), 16)
            sp.dma_start(wN[0:E, SLOT["gfc2"], :], ffn["gfc2_w"]).then_inc(S("nat_in"), 16)
            sp.dma_start(wN[0:E, SLOT["gate"], :], moe["gate_w"]).then_inc(S("nat_in"), 16)
            sp.dma_start(wN[0:E, SLOT["tvg"], :], ffn["tv_ln_g"]).then_inc(S("nat_in"), 16)
            sp.dma_start(wN[0:E, SLOT["tvs"], :], ffn["tv_ln_b"]).then_inc(S("nat_in"), 16)
            for k in range(2):
                sp.dma_start(wqk[:, k, :], attn0["w_qkv"][128 * k:128 * k + 128]).then_inc(S("nat_in"), 16)
            sp.dma_start(txn[0:NT, :, :], txt.rearrange("b n d -> n b d")).then_inc(S("txt_in"), 16)
            sp.dma_start(tvb[0:E, 0:F], ffn["tv_b1"]).then_inc(S("tvb_in"), 16)
            sp.dma_start(tvb[0:E, F:F + D], ffn["tv_b2"]).then_inc(S("tvb_in"), 16)
            sp.dma_start(tvb[E:E + 1, 0:F], ffn["b1"].unsqueeze(0)).then_inc(S("tvb_in"), 16)
            sp.dma_start(tvb[E:E + 1, F:F + D], ffn["b2"].unsqueeze(0)).then_inc(S("tvb_in"), 16)
            sp.wait_ge(S("g9_ones"), 1)
            sp.dma_start(g9[0:E, B:B + 1], ffn["gfc2_b"].unsqueeze(1)).then_inc(S("g9_in"), 16)
            for ph in ("ln1", "attn0", "ln2", "ffn"):
                meet(sp, ph)
            for w, (tv, base) in enumerate((("tv_W1", "W1"), ("tv_W2", "W2")) if stop > 4 else ()):
                tvr = ffn[tv].rearrange("e (j g) c -> (e j) (g c)", j=8)
                bsr = ffn[base].rearrange("(j g) c -> j (g c)", j=8)

                def load(n, r):
                    if not (is_known(n) and n == 0):
                        sp.wait_ge(S("mg_mm"), n * 8 + (4 * r - 4))
                    at = (n * 2 + (r - 8 * w)) * 1024
                    sp.dma_start(tvc[0:64, r, :], tvr[:, bass.ds(at, 1024)]).then_inc(S(f"tv_in{r}"), 16)
                    sp.dma_start(tvc[64:72, r, :], bsr[:, bass.ds(at, 1024)]).then_inc(S(f"tv_in{r}"), 16)
                if w == 0:
                    load(0, 0)
                    load(0, 1)
                with sp.Fori(1 if w == 0 else 4, 4 if w == 0 else 8) as n:
                    for r in range(2):
                        load(n, r)
            meet(sp, "lnf")
            meet(sp, "lna")
            for dst, src in ((m_w1, "w1"), (m_w3, "w3")):
                sp.dma_start(dst[:, 0:E, :], moe[src].rearrange("e d h -> d e h")).then_inc(S("moe_in"), 16)
                sp.dma_start(dst[:, E, :], moe["s" + src]).then_inc(S("moe_in"), 16)
            for k in range(2):
                sp.dma_start(m_w2[:, 0:E, k, :], moe["w2"].rearrange("e (k h) d -> k h e d", k=2)[k]).then_inc(S("moe_in"), 16)
                sp.dma_start(m_w2[:, E, k, :], moe["sw2"].rearrange("(k h) d -> k h d", k=2)[k]).then_inc(S("moe_in"), 16)
            sp.dma_start(m_bias[0:SUB, :], moe["biases"].unsqueeze(0).to_broadcast([SUB, E])).then_inc(S("moe_in"), 16)
            for ph in ("attn1", "lnm", "gate", "moe"):
                meet(sp, ph)
            o = out.rearrange("b n d -> (b n) d").rearrange("(c s p) d -> c p s d", s=NSUB, p=SUB)

            if stop > 8:
                sp.sem_inc(S("stored"), 16)
                with sp.Fori(0, NCH) as c:
                    sp.wait_ge(S("out_copied"), c + 1)
                    sp.dma_start(o[bass.ds(c, 1)].rearrange("a p s d -> (a p) s d"), m_o[0:SUB, 0]).then_inc(S("stored"), 16)
                sp.wait_ge(S("stored"), 16 * (NCH + 1))
            else:
                for n, v in (("tvb_in", 64), ("g9_in", 16), ("moe_in", 144)):
                    sp.wait_ge(S(n), v)
                sp.dma_start(out.rearrange("b n d -> (b n d)").rearrange("(p t) -> p t", p=P), hT[:, :]).then_inc(S("stored"), 16)
                sp.wait_ge(S("stored"), 16)

        def ln_pe(pe, name):
            done = NCH * NORMS.index(name)
            src = xn if name == "lnf" else hT

            def body(t, r):
                if live(t, 0, NCH):
                    if not is_known(t) or t >= 4:
                        pe.wait_ge(S("ln_out"), t + (done - 3))
                    pe.matmul(bank[r][:, 0:CH], C("centre"), chunk(src, t), start=True, stop=True).then_inc(S("ln_cen"), 1)
                if live(t, 2, NCH):
                    q = (r - 2) % 4
                    pe.wait_ge(S("ln_sq"), t + (done - 1))
                    if not is_known(t) or t >= 6:
                        pe.wait_ge(S("ln_var_read"), t + (done - 5))
                    pe.matmul(bank[4 + q][:, 0:CH], C("average"), ln_a[:, q, :], start=True, stop=True).then_inc(S("ln_var"), 1)
            for t in range(NCH + 2):
                body(t, t % 4)

        def ln_act(act, name):
            done = NCH * NORMS.index(name)

            def body(t, r):
                if live(t, 0, NCH):
                    act.wait_ge(S("ln_cen"), t + (done + 1))
                    if not is_known(t) or t >= 4:
                        act.wait_ge(S("ln_out"), t + (done - 3))
                    act.activation(ln_a[:, r, :], bank[r][:, 0:CH], ACT.Square).then_inc(S("ln_sq"), 1)
                if live(t, 2, NCH):
                    q = (r - 2) % 4
                    act.wait_ge(S("ln_var"), t + (done - 1))
                    act.activation(ln_a[:, q, :], bank[4 + q][:, 0:CH], ACT.Ln, bias=V("eps")).then_inc(S("ln_var_read"), 1)
                    act.wait_ge(S("ln_var_read"), t + (done - 1))
                    act.activation(ln_a[:, q, :], ln_a[:, q, :], ACT.Exp, scale=-0.5).then_inc(S("ln_rs"), 1)
            for t in range(NCH + 2):
                body(t, t % 4)

        def ln_dve(dve, name):
            done = NCH * NORMS.index(name)

            def body(t, r):
                dve.wait_ge(S("ln_rs"), t + (done + 1))
                dve.tensor_tensor(chunk(xn, t), bank[r][:, 0:CH], ln_a[:, r, :], ALU.mult).then_inc(S("ln_out"), 1)
                if name == "lnf":
                    dve.wait_ge(S("ln_out"), t + (done + 1))
                    dve.tensor_scalar(chunk(xn, t), chunk(xn, t), V("lng"), V("lnb"), ALU.mult, ALU.add).then_inc(S("lnf_aff"), 1)
                    dve.wait_ge(S("lnf_aff"), t + 1)
                    dve.tensor_tensor(chunk(hT, t), chunk(hT, t), chunk(xn, t), ALU.add)
            for t in range(NCH):
                body(t, t % 4)

        @block.gpsimd
        def _(pool):
            pool.memset(V("eps"), LN_EPS).then_inc(S("eps_set"), 1)
            pool.memset(g9[:, B:B + 1], 1.0).then_inc(S("g9_ones"), 1)
            for ph in ("ln1", "attn0"):
                meet(pool, ph)

            def stage0(t, r):
                reuse(pool, S("a_v_done"), t, 2)
                pool.tensor_copy(a_x[:, r, :], sample(xn, t)).then_inc(S("a_x_ready"), 1)
            if stop > 2:
                run_steps(pool, B, 0, stage0, 2)
            for ph in ("ln2", "ffn"):
                meet(pool, ph)
            if stop > 4:
                pool.wait_ge(S("mg_act"), 32)
                pool.wait_ge(S("mg_dve"), 32)

                def stage_w(t, r):
                    reuse(pool, S("f_y"), t, 2)
                    pool.tensor_copy(wst[:, r, FW:FW + F], w2m[:, bass.ds(t, 1), :].rearrange("p a f -> p (a f)")).then_inc(S("f_w2"), 1)
                run_steps(pool, B, 0, stage_w, 2)
            meet(pool, "lnf")
            meet(pool, "lna")
            if stop > 6:
                pool.memset(b_v[:, :, :, :], 0.0).then_inc(S("b_v_zero"), 1)
            meet(pool, "attn1")

            def masked_keys(t, r):
                reuse(pool, S("b_v_done"), t, 2)
                pool.tensor_copy(b_x[:, r, :], sample(xn, t))
                pool.tensor_copy(b_xt[:, r, :].rearrange("p (h n) -> p h n", h=H),
                                 xn[:, bass.ds(t * N + P, NTAIL)].unsqueeze(1).to_broadcast([P, H, NTAIL])).then_inc(S("b_x_ready"), 1)
                pool.wait_ge(S("b_k_ready"), t + 1)
                reuse3(pool, S("b_s_done"), t)
                pool.tensor_tensor(b_km[:, r], b_k[:, r, :].unsqueeze(1).to_broadcast([P, H, N]),
                                   C("hmask").unsqueeze(2).to_broadcast([P, H, N]), ALU.mult).then_inc(S("b_km_ready"), 1)
            if stop > 6:
                run_steps(pool, B, 0, masked_keys, 2)
            for ph in ("lnm", "gate", "moe"):
                meet(pool, ph)

        @block.tensor
        def _(pe):
            pe.wait_ge(S("const_in"), 16)
            pe.wait_ge(S("psum_zero"), 8)
            for u, (kind, srcs, _, rows) in enumerate(turns):
                if kind == "x":
                    pe.wait_ge(S("xq_ready"), u // 4 + 1)
                if kind == "n":
                    pe.wait_ge(S("nat_in"), 16 * 14)
                if kind == "w":
                    pe.wait_ge(S("noisy"), 2)
                if kind == "t":
                    pe.wait_ge(S("txt_in"), 16)
                if u >= 4:
                    pe.wait_ge(S("turned_act" if u % 2 == 0 else "turned_dve"), (u - 4) // 2 + 1)
                for i, (src, rows) in enumerate(srcs):
                    mm = pe.transpose(bank[u % 4][:, i * rows:(i + 1) * rows], src, ident[0:rows, 0:rows])
                mm.then_inc(S("turned"), 1)
            pe.wait_ge(S("turned_act"), len(turns) // 2)
            pe.wait_ge(S("turned_dve"), len(turns) // 2)
            pe.matmul(bank[4][:, 0:P], wqk[:, 0, :], wqk[:, 1, :], start=True, stop=True)
            pe.matmul(bank[4][:, P:2 * P], wN[:, SLOT["v0"], :], W("proj"), start=True, stop=True)
            pe.wait_ge(S("wp_scaled"), 1)
            pe.matmul(bank[4][:, 2 * P:2 * P + 1], W("Wp"), V("bv"), start=True, stop=True).then_inc(S("wprod"), 1)
            for c in range(4):
                cols = slice(512 * c, 512 * c + 512)
                if c:
                    pe.wait_ge(S("tok_x"), c)
                for k in range(2):
                    pe.matmul(bank[0], W("n1a" if k == 0 else "n1b"), xT[:, k, cols], start=k == 0, stop=k == 1)
                for k in range(2):
                    mm = pe.matmul(bank[1], W("n2a" if k == 0 else "n2b"), xT[:, k, cols], start=k == 0, stop=k == 1)
                mm.then_inc(S("tok_g"), 1)
                pe.wait_ge(S("tok_x"), c + 1)
                if c >= 2:
                    pe.wait_ge(S("tok_h"), c - 1)
                pe.matmul(bank[2 + c % 2], W("W3"), tokx[:, c % 2, :], start=True, stop=True).then_inc(S("tok_y"), 1)
            meet(pe, "ln1")
            if stop > 1:
                ln_pe(pe, "ln1")
            meet(pe, "attn0")

            def attn0_step(t, r):
                if live(t, 0, B):
                    reuse(pe, S("a_u_ready"), t, 1)
                    pe.matmul(bank[0][:, 0:N], pq[:, 0, :], sample(xn, t), start=True, stop=True).then_inc(S("a_u_done"), 1)
                if live(t, 2, B):
                    q = r
                    pe.wait_ge(S("a_a_ready"), t - 1)
                    reuse(pe, S("a_t_ready"), t - 2, 2)
                    tp = bank[5 + q]
                    pe.transpose(tp[:, 0:P], a_e[:, q, 0, 0:P], ident)
                    pe.transpose(tp[:, P:N], a_e[0:NTAIL, q, 1, 0:P], ident[0:NTAIL, 0:NTAIL])
                    pe.transpose(tp[0:NTAIL, N:N + P], a_e[:, q, 0, P:N], ident)
                    pe.transpose(tp[0:NTAIL, N + P:2 * N], a_e[0:NTAIL, q, 1, P:N], ident[0:NTAIL, 0:NTAIL]).then_inc(S("a_t_done"), 1)
                if live(t, 1, B):
                    q = (r - 1) % 2
                    pe.wait_ge(S("a_u_ready"), t)
                    reuse(pe, S("a_e_ready"), t - 1, 2)
                    sc = bank[1 + q]
                    pe.matmul(sc[:, 0:N], a_u[:, q, 0:P], sample(xn, t - 1), start=True, stop=True)
                    pe.matmul(sc[0:NTAIL, N:2 * N], a_u[:, q, P:N], sample(xn, t - 1), start=True, stop=True, skip_group_check=True).then_inc(S("a_s_done"), 1)
                if live(t, 2, B):
                    pe.wait_ge(S("a_x_ready"), t - 1)
                    reuse(pe, S("a_v_ready"), t - 2, 1)
                    pe.matmul(bank[7][:, 0:P], a_x[:, r, 0:P], pq[:, 1, :], start=True, stop=True)
                    pe.matmul(bank[7][0:NTAIL, P:2 * P], a_x[:, r, P:N], pq[:, 1, :], start=True, stop=True, skip_group_check=True).then_inc(S("a_v_done"), 1)
                if live(t, 3, B):
                    q = (r - 3) % 2
                    pe.wait_ge(S("a_v_ready"), t - 2)
                    pe.wait_ge(S("a_t_ready"), t - 2)
                    reuse(pe, S("a_h"), t - 3, 2)
                    o = bank[3 + q][:, 0:N]
                    pe.matmul(o, W("v0"), sample(xn, t - 3), start=True, stop=False)
                    pe.matmul(o, a_v[:, q, 0, :], a_t[:, q, 0, :], start=False, stop=False)
                    pe.matmul(o, a_v[0:NTAIL, q, 1, :], a_t[0:NTAIL, q, 1, :], start=False, stop=True).then_inc(S("a_o_done"), 1)
            if stop > 2:
                run_steps(pe, B, 3, attn0_step, 6)
            meet(pe, "ln2")
            if stop > 3:
                ln_pe(pe, "ln2")
            meet(pe, "ffn")
            if stop > 4:
                def gate_step(t, r):
                    reuse(pe, S("gh_done"), t, 2)
                    pe.matmul(bank[r][:, 0:GB], W("gfc1"), chunk(xn, t, GB), start=True, stop=True).then_inc(S("gh_mm"), 1)
                run_steps(pe, B // 2, 0, gate_step, 2)
                pe.wait_ge(S("gh_sum"), B // 2)
                pe.matmul(bank[2][0:E, 0:B], W("gfc2")[:, 0:E], ghm[:, :], start=True, stop=True).then_inc(S("g_mm"), 1)
                pe.wait_ge(S("g9_ready"), 2)
                pe.matmul(bank[3][0:72, 0:B], C("rep", E + 1), g9[:, 0:B], start=True, stop=True).then_inc(S("grep_mm"), 1)
                pe.wait_ge(S("tvb_in"), 64)
                for k in range(5):
                    mm = pe.matmul(bank[4][:, k * B:(k + 1) * B], tvb[:, k * P:(k + 1) * P], g9[:, 0:B], start=True, stop=True, skip_group_check=True)
                mm.then_inc(S("bm_mm"), 1)
                pe.wait_ge(S("gblk_ready"), 1)
                def merge(n, r):
                    pe.wait_ge(S(f"tv_in{r}"), n * 32 + 32)
                    for s in range(4):
                        if not (is_known(n) and n == 0):
                            pe.wait_ge(S("mg_act" if s % 2 == 0 else "mg_dve"), n * 4 + (2 * r + s // 2 - 3))
                        for k in range(2):
                            mm = pe.matmul(bank[4 * r + s][:, k * 256:(k + 1) * 256], tvc[:, r, (2 * s + k) * P:(2 * s + k + 1) * P],
                                           gblk[:, :, :].rearrange("p j b -> p (j b)"), start=True, stop=True, skip_group_check=True)
                        mm.then_inc(S("mg_mm"), 1)
                pe.wait_ge(S("bm_copied"), 1)
                for r in range(2):
                    merge(0, r)
                with pe.Fori(1, 8) as n:
                    for r in range(2):
                        merge(n, r)
                pe.wait_ge(S("mg_act"), 32)
                pe.wait_ge(S("mg_dve"), 32)

                def ffn_step(t, r):
                    if live(t, 0, B):
                        pe.wait_ge(S("f_w1"), t + 1)
                        reuse(pe, S("f_h_act"), t, 2)
                        reuse(pe, S("f_h_dve"), t, 2)
                        for k in range(4):
                            mm = pe.matmul(bank[2 * r + k // 2][:, (k % 2) * N:(k % 2) * N + N], wst[:, r, k * P:(k + 1) * P],
                                           sample(xn, t), start=True, stop=True, skip_group_check=True)
                        mm.then_inc(S("f_mm"), 1)
                    if live(t, 1, B):
                        q = (r - 1) % 2
                        pe.wait_ge(S("f_w2"), t)
                        pe.wait_ge(S("f_h_act"), t)
                        pe.wait_ge(S("f_h_dve"), t)
                        reuse(pe, S("f_res"), t - 1, 2)
                        for k in range(4):
                            mm = pe.matmul(bank[4 + q][:, 0:N], wst[:, q, FW + k * P:FW + (k + 1) * P], hbuf[:, q, k, :],
                                           start=k == 0, stop=k == 3)
                        mm.then_inc(S("f_y"), 1)
                run_steps(pe, B, 1, ffn_step, 4)
            meet(pe, "lnf")
            if stop > 5:
                ln_pe(pe, "lnf")
            meet(pe, "lna")
            if stop > 6:
                ln_pe(pe, "lna")
            meet(pe, "attn1")

            def attn1_step(t, r):
                if live(t, 0, B):
                    reuse(pe, S("b_vm_ready"), t, 1)
                    xs = sample(xn, t)
                    pe.matmul(bank[0][:, 0:N], W("Wq"), xs, start=True, stop=True)
                    pe.matmul(bank[0][:, N:2 * N], W("Wk"), xs, start=True, stop=True, skip_group_check=True).then_inc(S("b_qk_done"), 1)
                if live(t, 2, B):
                    pe.wait_ge(S("b_en_ready"), t - 1)
                    pe.wait_ge(S("b_tt_ready"), t - 1)
                    reuse(pe, S("b_et_act"), t - 2, 1)
                    reuse(pe, S("b_et_dve"), t - 2, 1)
                    ee = b_e[:, r]
                    for h in range(H):
                        pe.transpose(bank[5 + h // 4][:, (h % 4) * P:(h % 4) * P + P], ee[:, h, 0:P], ident)
                    pe.transpose(bank[7][:, 0:HT], ee[0:HT, 8, 0:P], ident[0:HT, 0:HT])
                    pe.transpose(bank[7][0:HT, HT:HT + P], b_ek[:, r, :], ident)
                    pe.matmul(bank[7][0:HT, HT + P:HT + N], b_tt[0:HT, r, :], C("dsel", HT), start=True, stop=True, skip_group_check=True).then_inc(S("b_t_done"), 1)
                if live(t, 1, B):
                    q = (r - 1) % 2
                    pe.wait_ge(S("b_km_ready"), t)
                    pe.wait_ge(S("b_qm_ready"), t)
                    for g in range(3):
                        if not (is_known(t) and t == 1):
                            pe.wait_ge(S("b_e_ready"), (t - 2) * 3 + (g + 1))
                        n = 3 if g < 2 else 2
                        mm = pe.matmul(ps3a[:, g, 0:n * N], b_q[:, q, 0:P], b_km[:, q, 3 * g:3 * g + n, :].rearrange("p h n -> p (h n)"), start=True, stop=True)
                        if g == 2:
                            mm = pe.matmul(ps3a[0:HT, 2, 2 * N:3 * N], b_qm[:, q].rearrange("p h n -> p (h n)"), b_k[:, q, :], start=True, stop=True, skip_group_check=True)
                        mm.then_inc(S("b_s_done"), 1)
                if live(t, 2, B):
                    pe.wait_ge(S("b_et_act"), t - 1)
                    pe.wait_ge(S("b_et_dve"), t - 1)
                    reuse(pe, S("b_h"), t - 2, 1)
                    o = bank[1][:, 0:N]
                    for h in range(H):
                        pe.matmul(o, b_v[:, r, h, :], b_et[:, r, h, :], start=h == 0, stop=False)
                    pe.matmul(o, b_vt[0:HT, r, :], b_ett[0:HT, r, :], start=False, stop=True).then_inc(S("b_o_done"), 1)
                if live(t, 0, B):
                    pe.wait_ge(S("b_x_ready"), t + 1)
                    pe.wait_ge(S("b_k_ready"), t + 1)
                    pe.matmul(bank[0][:, 0:P], b_x[:, r, 0:P], W("Wv"), start=True, stop=True)
                    pe.matmul(bank[0][0:HT, P:2 * P], b_xt[:, r, :], W("Wv"),
                              start=True, stop=True, skip_group_check=True).then_inc(S("b_v_done"), 1)
                if live(t, 2, B):
                    pe.wait_ge(S("b_o_ready"), t - 1)
                    pe.matmul(bank[1][:, 256:256 + N], W("Wp"), b_o[:, r, :], start=True, stop=True).then_inc(S("b_y_done"), 1)
            if stop > 6:
                run_steps(pe, B, 2, attn1_step, 4)
            meet(pe, "lnm")
            if stop > 7:
                ln_pe(pe, "lnm")
            meet(pe, "gate")
            if stop > 8:
                pe.wait_ge(S("moe_in"), 16 * 9)

                def route_step(t, r):
                    if live(t, 1, NCH):
                        pe.wait_ge(S("r_sc"), t)
                        reuse(pe, S("r_s"), t - 1, 2)
                    if live(t, 0, NCH):
                        reuse(pe, S("r_sc"), t, 2)
                        pe.matmul(bank[r][0:E, 0:CH], W("gate")[:, 0:E], chunk(xn, t), start=True, stop=True).then_inc(S("r_mm"), 1)
                    if live(t, 1, NCH):
                        q = (r - 1) % 2
                        for s in range(NSUB):
                            mm = pe.transpose(bank[2 + q][0:SUB, s * E:(s + 1) * E], m_sc[0:E, q, s * SUB:(s + 1) * SUB], ident[0:E, 0:E])
                        mm.then_inc(S("r_tr"), 1)
                run_steps(pe, NCH, 1, route_step, 4)
                pe.wait_ge(S("comb"), 1)
                for c in range(NCH):
                    if c >= 4:
                        pe.wait_ge(S("ct"), c - 3)
                    for s in range(NSUB):
                        mm = pe.transpose(bank[4 + c % 4][0:E, s * SUB:(s + 1) * SUB], m_t[3][0:SUB, c * NSUB + s, :], ident[0:SUB, 0:SUB])
                    mm.then_inc(S("ct_tr"), 1)
            meet(pe, "moe")
            if stop > 8:
                pe.sem_inc(S("m_y"), 3)

                def turn_out(cb):
                    pe.wait_ge(S("cb_taken"), cb + 1)
                    for s in range(NSUB):
                        mm = pe.transpose(bank[7][0:SUB, s * P:(s + 1) * P], m_f[:, 0, s * SUB:(s + 1) * SUB], ident)
                    mm.then_inc(S("m_tr"), 1)

                def chunk_pe(c):
                    later = not is_known(c)
                    for v in range(UN + 1):
                        e, k, s = v // 2, v % 2, v % 3
                        if v == 6 and later:
                            pe.wait_ge(S("m_f"), c + 1)
                            turn_out(c * E + 3)
                        if v < UN:
                            if k == 0 and e < E:
                                pe.wait_ge(S("cb_taken"), c * E + (e + 1))
                                if v == 6 and later:
                                    pe.wait_ge(S("out_copied"), c)
                            pe.wait_ge(S("m_h"), c * UN + (v + 1))
                            pe.matmul(bank[2 * s][:, 0:CH], m_w1[:, e, k * P:(k + 1) * P], chunk(xn, c), start=True, stop=True)
                            pe.matmul(bank[2 * s + 1][:, 0:CH], m_w3[:, e, k * P:(k + 1) * P], chunk(xn, c), start=True, stop=True).then_inc(S("m_ab"), 1)
                            if k == 0 and e < E:
                                pe.matmul(bank[7][:, 0:CH], C("select", E)[:, e * P:(e + 1) * P], m_ct[0:E, bass.ds(c * CH, CH)],
                                          start=True, stop=True).then_inc(S("cb_mm"), 1)
                        if v >= 1:
                            w = v - 1
                            if w == 0:
                                pe.wait_ge(S("m_f"), c + 1)
                            pe.wait_ge(S("m_h"), c * UN + (w + 4))
                            pe.matmul(bank[6][:, 0:CH], m_w2[:, w // 2, w % 2, :], m_h[:, w % 3, :], start=w == 0, stop=w == UN - 1).then_inc(S("m_y"), 1)
                chunk_pe(0)
                with pe.Fori(1, NCH) as c:
                    chunk_pe(c)
                pe.wait_ge(S("m_f"), NCH + 1)
                turn_out(NCH * E)

        @block.scalar
        def _(act):
            act.wait_ge(S("noise_in"), 96)
            act.wait_ge(S("vec_in"), 16 * 16)
            act.activation(ea[:, :, :], ei[:, :, :], ACT.Abs).then_inc(S("f_abs"), 1)
            act.activation(V("tmp0"), V("eps_out1"), ACT.Abs).then_inc(S("f_abs"), 1)
            act.activation(V("tmp1"), V("eps_out2"), ACT.Abs).then_inc(S("f_abs"), 1)
            act.activation(ei[:, :, :], ei[:, :, :], ACT.Sign).then_inc(S("f_sign"), 1)
            act.activation(V("eps_out1"), V("eps_out1"), ACT.Sign).then_inc(S("f_sign"), 1)
            act.activation(V("eps_out2"), V("eps_out2"), ACT.Sign).then_inc(S("f_sign"), 1)
            act.wait_ge(S("f_abs"), 3)
            act.wait_ge(S("f_sign"), 3)
            act.activation(ea[:, :, :], ea[:, :, :], ACT.Sqrt).then_inc(S("f_sqrt"), 1)
            act.activation(V("eo1"), V("tmp0"), ACT.Sqrt).then_inc(S("f_sqrt"), 1)
            act.activation(V("eo2"), V("tmp1"), ACT.Sqrt).then_inc(S("f_sqrt"), 1)
            for u, (kind, srcs, dst, rows) in enumerate(turns):
                if u % 2 == 0:
                    act.wait_ge(S("turned"), u + 1)
                    act.copy(dst, bank[u % 4][:, 0:len(srcs) * rows].rearrange("p (a b) -> p a b", a=len(srcs))).then_inc(S("turned_act"), 1)
            act.wait_ge(S("wprod"), 1)
            act.copy(pq[:, :, :], bank[4][:, 0:2 * P].rearrange("p (a b) -> p a b", a=2)).then_inc(S("pq_ready"), 1)
            act.activation(V("bpn"), bank[4][:, 2 * P:2 * P + 1], ACT.Identity, bias=V("bp")).then_inc(S("pq_ready"), 1)
            for c in range(4):
                act.wait_ge(S("tok_m"), c + 1)
                act.activation(mish[:, 1, :], mish[:, 0, :], ACT.Exp).then_inc(S("tok_e"), 1)
            meet(act, "ln1")
            act.preload_act_table_set("natural_log_exp_and_others")
            if stop > 1:
                ln_act(act, "ln1")
            meet(act, "attn0")

            def attn0_step(t, r):
                if live(t, 0, B):
                    act.wait_ge(S("a_u_done"), t + 1)
                    reuse(act, S("a_s_done"), t, 2)
                    act.copy(a_u[:, r, :], bank[0][:, 0:N]).then_inc(S("a_u_ready"), 1)
                if live(t, 1, B):
                    q = (r - 1) % 2
                    act.wait_ge(S("a_m_ready"), t)
                    reuse(act, S("a_t_done"), t - 1, 2)
                    act.activation(a_e[:, q, 0, :], bank[1 + q][:, 0:N], ACT.Exp, bias=a_m[:, q, 0:1], scale=D ** -0.5, accum_out=a_m[:, q, 2:3])
                    act.activation(a_e[0:NTAIL, q, 1, :], bank[1 + q][0:NTAIL, N:2 * N], ACT.Exp, bias=a_m[0:NTAIL, q, 1:2], scale=D ** -0.5,
                                   accum_out=a_m[0:NTAIL, q, 3:4]).then_inc(S("a_e_ready"), 1)
                if live(t, 2, B):
                    act.wait_ge(S("a_v_done"), t - 1)
                    reuse(act, S("a_o_done"), t - 2, 2)
                    act.copy(a_v[:, r].rearrange("p m n -> p (m n)"), bank[7][:, 0:2 * P]).then_inc(S("a_v_ready"), 1)
            if stop > 2:
                run_steps(act, B, 2, attn0_step, 4)
            meet(act, "ln2")
            if stop > 3:
                ln_act(act, "ln2")
            meet(act, "ffn")
            if stop > 4:
                def gate_step(t, r):
                    act.wait_ge(S("gh_mm"), t + 1)
                    reuse(act, S("gh_sum"), t, 2)
                    act.activation(hbuf[:, r, 0:2, :].rearrange("p a n -> p (a n)"), bank[r][:, 0:GB], ACT.Relu, bias=V("gfc1_b")).then_inc(S("gh_done"), 1)
                run_steps(act, B // 2, 0, gate_step, 2)

                for w in range(2):
                    with act.Fori(4 * w, 4 * w + 4) as n:
                        for r in range(2):
                            for s in (0, 2):
                                act.wait_ge(S("mg_mm"), n * 8 + (4 * r + s + 1))
                                act.copy(merged_dst(w, n * 2 + (r - 8 * w), s),
                                         bank[4 * r + s].rearrange("p (g j b) -> p g j b", g=2, j=8)).then_inc(S("mg_act"), 1)
                act.wait_ge(S("bm_copied"), 1)
                act.wait_ge(S("mg_act"), 32)
                act.wait_ge(S("mg_dve"), 32)

                def ffn_step(t, r):
                    if live(t, 0, B):
                        reuse(act, S("f_mm"), t, 2)
                        reuse(act, S("f_res"), t, 2)
                        act.copy(wst[:, r, 0:FW], w1m[:, bass.ds(t, 1), :].rearrange("p a f -> p (a f)")).then_inc(S("f_w1"), 1)
                    if live(t, 1, B):
                        q = (r - 1) % 2
                        act.wait_ge(S("f_mm"), t)
                        reuse(act, S("f_y"), t - 1, 2)
                        act.activation(hbuf[:, q, 0, :], bank[2 * q][:, 0:N], ACT.Relu, bias=wst[:, q, F:F + 1])
                        act.activation(hbuf[:, q, 1, :], bank[2 * q][:, N:2 * N], ACT.Relu, bias=wst[:, q, F + 1:F + 2]).then_inc(S("f_h_act"), 1)
                run_steps(act, B, 1, ffn_step, 4)
            meet(act, "lnf")
            if stop > 5:
                ln_act(act, "lnf")
            meet(act, "lna")
            if stop > 6:
                ln_act(act, "lna")
            meet(act, "attn1")

            def attn1_step(t, r):
                if live(t, 2, B):
                    act.wait_ge(S("b_t_done"), t - 1)
                    reuse(act, S("b_o_done"), t - 2, 2)
                    act.copy(b_et[:, r, 0:4, 0:P], bank[5].rearrange("p (h n) -> p h n", h=4)).then_inc(S("b_et_act"), 1)
                if live(t, 0, B):
                    act.wait_ge(S("b_qk_done"), t + 1)
                    reuse3(act, S("b_s_done"), t)
                    act.activation(b_q[:, r, :], bank[0][:, 0:N], ACT.Identity, bias=V("bq")).then_inc(S("b_q_ready"), 1)
                    reuse(act, S("b_km_ready"), t, 2)
                    act.activation(b_k[:, r, :], bank[0][:, N:2 * N], ACT.Identity, bias=V("bk")).then_inc(S("b_k_ready"), 1)
                if live(t, 1, B):
                    q = (r - 1) % 2
                    reuse(act, S("b_t_done"), t - 1, 2)
                    for h in range(9):
                        if h % 3 == 0:
                            act.wait_ge(S("b_nm_ready"), (t - 1) * 3 + (h // 3 + 1))
                        rows = P if h < 8 else HT
                        ins = act.activation(b_e[0:rows, q, h, :], ps3a[0:rows, h // 3, (h % 3) * N:(h % 3) * N + N], ACT.Exp,
                                             bias=b_nm[0:rows, q, h:h + 1], accum_out=b_s[0:rows, q, h:h + 1])
                        if h % 3 == 2:
                            ins.then_inc(S("b_e_ready"), 1)
            if stop > 6:
                run_steps(act, B, 2, attn1_step, 4)
            meet(act, "lnm")
            if stop > 7:
                ln_act(act, "lnm")
            meet(act, "gate")
            if stop > 8:
                def route_step(t, r):
                    act.wait_ge(S("r_mm"), t + 1)
                    reuse(act, S("r_tr"), t, 2)
                    act.copy(m_sc[0:E, r, :], bank[r][0:E, 0:CH]).then_inc(S("r_sc"), 1)
                run_steps(act, NCH, 0, route_step, 2)
                act.wait_ge(S("top_ready"), 2)
                for k in range(2):
                    act.activation(m_1[k][0:SUB, :], m_1[k][0:SUB, :], ACT.Exp, scale=-1.0).then_inc(S("top_exp"), 1)
                for c in range(NCH):
                    act.wait_ge(S("ct_tr"), c + 1)
                    act.copy(m_ct[0:E, c * CH:(c + 1) * CH], bank[4 + c % 4][0:E, 0:CH]).then_inc(S("ct"), 1)
            meet(act, "moe")
            if stop > 8:
                act.sem_inc(S("cb_taken"), 1)

                def out_act(n):
                    act.wait_ge(S("m_tr"), n)
                    act.wait_ge(S("stored"), n * 16)
                    act.copy(m_o[0:SUB, 0], bank[7][0:SUB].rearrange("p (s d) -> p s d", s=NSUB)).then_inc(S("out_copied"), 1)

                def chunk_act(c):
                    for v in range(UN):
                        e, k, s = v // 2, v % 2, v % 3
                        if v == 6 and not is_known(c):
                            out_act(c)
                        if k == 0 and e < E:
                            act.wait_ge(S("cb_mm"), c * E + (e + 1))
                            act.wait_ge(S("cb_used"), c * E + (e + 1))
                            act.copy(m_cb[:, e % 2, :], bank[7][:, 0:CH]).then_inc(S("cb_taken"), 1)
                        act.wait_ge(S("m_ab"), c * UN + (v + 1))
                        act.wait_ge(S("m_h"), c * UN + (v + 1))
                        act.activation(m_a[:, s, :], bank[2 * s][:, 0:CH], ACT.Silu).then_inc(S("m_silu"), 1)
                chunk_act(0)
                with act.Fori(1, NCH) as c:
                    chunk_act(c)
                out_act(NCH)

        @block.vector
        def _(dve):
            for i in range(8):
                dve.memset(bank[i], 0.0).then_inc(S("psum_zero"), 1)
            for t in range(2):
                dve.wait_ge(S(f"x_in{t}"), 16)
                dve.tensor_copy(xq[:, t].rearrange("p w (r c) -> p w r c", c=16), xp[:, t].rearrange("p r w c -> p w r c")).then_inc(S("xq_ready"), 1)
            dve.wait_ge(S("f_sqrt"), 3)
            dve.tensor_tensor(ei[:, :, :], ei[:, :, :], ea[:, :, :], ALU.mult).then_inc(S("n_f"), 1)
            dve.tensor_tensor(V("eo1"), V("eo1"), V("eps_out1"), ALU.mult).then_inc(S("n_f"), 1)
            dve.tensor_tensor(V("eo2"), V("eo2"), V("eps_out2"), ALU.mult).then_inc(S("n_f"), 1)
            dve.wait_ge(S("n_f"), 3)
            for k in range(2):
                dve.scalar_tensor_tensor(ea[:, k, :], ei[:, k, :], V(f"eo{k + 1}"), sw[:, k, :], ALU.mult, ALU.mult).then_inc(S("n_sw"), 1)
                dve.tensor_scalar(V(f"b{k + 1}n"), V(f"W{k + 1}_sb"), V(f"eo{k + 1}"), V(f"W{k + 1}_b"), ALU.mult, ALU.add).then_inc(S("n_b"), 1)
            dve.wait_ge(S("n_sw"), 2)
            for k in range(2):
                s0 = SLOT["n1a"] + 2 * k
                dve.tensor_tensor(wN[:, s0:s0 + 2, :], ea[:, k, :].rearrange("p (a c) -> p a c", a=2),
                                  wraw[:, k, :].rearrange("p (a c) -> p a c", a=2), ALU.add).then_inc(S("noisy"), 1)
            for u, (kind, srcs, dst, rows) in enumerate(turns):
                if u % 2 == 1:
                    dve.wait_ge(S("turned"), u + 1)
                    dve.tensor_copy(dst, bank[u % 4][0:dst.shape[0], 0:len(srcs) * rows].rearrange("p (a b) -> p a b", a=len(srcs))).then_inc(S("turned_dve"), 1)
            dve.wait_ge(S("turned_dve"), len(turns) // 2)
            dve.tensor_scalar(W("Wp"), W("Wp"), D ** -0.5, None, ALU.mult).then_inc(S("wp_scaled"), 1)
            dve.wait_ge(S("turned_act"), len(turns) // 2)
            for k, (v, n) in enumerate((("ln_g", "lng"), ("ln_b", "lnb"))):
                dve.tensor_scalar(tvln[:, k, :], W("tvg" if k == 0 else "tvs")[:, 0:E], V(v), None, ALU.subtract).then_inc(S("ln_d"), 1)
                dve.wait_ge(S("ln_d"), 3 * k + 1)
                dve.tensor_reduce(V(n), tvln[:, k, :], AX, ALU.add).then_inc(S("ln_d"), 1)
                dve.wait_ge(S("ln_d"), 3 * k + 2)
                dve.tensor_scalar(V(n), V(n), LN_MERGE, V(v), ALU.mult, ALU.add).then_inc(S("ln_d"), 1)
            dve.wait_ge(S("n_b"), 2)
            for c in range(4):
                dve.wait_ge(S("tok_g"), c + 1)
                dve.tensor_scalar(mish[:, 0, :], bank[0], V("b1n"), 30.0, ALU.add, ALU.min).then_inc(S("tok_m"), 1)
                dve.tensor_scalar(mish[:, 2, :], bank[0], V("b1n"), None, ALU.add).then_inc(S("tok_gb"), 1)
                dve.wait_ge(S("tok_e"), c + 1)
                dve.scalar_tensor_tensor(mish[:, 3, :], mish[:, 1, :], 2.0, mish[:, 1, :], ALU.add, ALU.mult).then_inc(S("tok_n"), 1)
                dve.wait_ge(S("tok_n"), c + 1)
                dve.tensor_scalar(mish[:, 4, :], mish[:, 3, :], 2.0, None, ALU.add).then_inc(S("tok_d"), 1)
                dve.wait_ge(S("tok_d"), c + 1)
                dve.reciprocal(mish[:, 5, :], mish[:, 4, :]).then_inc(S("tok_r"), 1)
                dve.wait_ge(S("tok_gb"), c + 1)
                dve.tensor_tensor(mish[:, 2, :], mish[:, 2, :], mish[:, 3, :], ALU.mult).then_inc(S("tok_p"), 1)
                dve.wait_ge(S("tok_p"), c + 1)
                dve.wait_ge(S("tok_r"), c + 1)
                dve.tensor_tensor(mish[:, 3, :], mish[:, 2, :], mish[:, 5, :], ALU.mult).then_inc(S("tok_q"), 1)
                dve.wait_ge(S("tok_q"), c + 1)
                if c >= 2:
                    dve.wait_ge(S("tok_y"), c - 1)
                dve.scalar_tensor_tensor(tokx[:, c % 2, :], bank[1], V("b2n"), mish[:, 3, :], ALU.add, ALU.mult).then_inc(S("tok_x"), 1)
                dve.wait_ge(S("tok_y"), c + 1)
                dve.scalar_tensor_tensor(hT[:, 8 * c * N:(8 * c + 8) * N].rearrange("p (b n) -> p b n", n=N)[:, :, 0:NP_],
                                         bank[2 + c % 2].rearrange("p (b n) -> p b n", n=NP_), V("W3_b"),
                                         C("pos").unsqueeze(1).to_broadcast([P, 8, NP_]), ALU.add, ALU.add).then_inc(S("tok_h"), 1)
            meet(dve, "ln1")
            if stop > 1:
                ln_dve(dve, "ln1")
            meet(dve, "attn0")

            def attn0_step(t, r):
                if live(t, 2, B):
                    dve.wait_ge(S("a_e_ready"), t - 1)
                    dve.reciprocal(a_m[:, r, 4:5], a_m[:, r, 2:3]).then_inc(S("a_r"), 1)
                    dve.reciprocal(a_m[0:NTAIL, r, 5:6], a_m[0:NTAIL, r, 3:4]).then_inc(S("a_rt"), 1)
                    dve.wait_ge(S("a_r"), t - 1)
                    dve.tensor_scalar(a_e[:, r, 0, :], a_e[:, r, 0, :], a_m[:, r, 4:5], None, ALU.mult)
                    dve.wait_ge(S("a_rt"), t - 1)
                    dve.tensor_scalar(a_e[0:NTAIL, r, 1, :], a_e[0:NTAIL, r, 1, :], a_m[0:NTAIL, r, 5:6], None, ALU.mult).then_inc(S("a_a_ready"), 1)
                if live(t, 1, B):
                    q = (r - 1) % 2
                    dve.wait_ge(S("a_s_done"), t)
                    reuse(dve, S("a_e_ready"), t - 1, 2)
                    dve.tensor_reduce(a_m[:, q, 0:2], bank[1 + q][:, 0:2 * N].rearrange("p (a n) -> p a n", a=2), AX, ALU.max, negate=True).then_inc(S("a_mx"), 1)
                    dve.wait_ge(S("a_mx"), t)
                    dve.tensor_scalar(a_m[:, q, 0:2], a_m[:, q, 0:2], D ** -0.5, None, ALU.mult).then_inc(S("a_m_ready"), 1)
                if live(t, 2, B):
                    dve.wait_ge(S("a_t_done"), t - 1)
                    reuse(dve, S("a_o_done"), t - 2, 2)
                    dve.tensor_copy(a_t[:, r].rearrange("p m n -> p (m n)"), bank[5 + r][:, 0:2 * N]).then_inc(S("a_t_ready"), 1)
                if live(t, 3, B):
                    q = (r - 3) % 2
                    dve.wait_ge(S("a_o_done"), t - 2)
                    dve.scalar_tensor_tensor(sample(hT, t - 3), bank[3 + q][:, 0:N], V("b_proj"), sample(hT, t - 3), ALU.add, ALU.add).then_inc(S("a_h"), 1)
            if stop > 2:
                run_steps(dve, B, 3, attn0_step, 6)
            meet(dve, "ln2")
            if stop > 3:
                ln_dve(dve, "ln2")
            meet(dve, "ffn")
            if stop > 4:
                def gate_step(t, r):
                    dve.wait_ge(S("gh_done"), t + 1)
                    dve.tensor_reduce(ghm[:, bass.ds(t * 2, 2)], hbuf[:, r, 0:2, :], AX, ALU.add).then_inc(S("gh_sum"), 1)
                run_steps(dve, B // 2, 0, gate_step, 2)
                dve.wait_ge(S("g9_in"), 16)
                dve.wait_ge(S("g_mm"), 1)
                dve.memset(g9[:, 0:B], 1.0).then_inc(S("g9_ready"), 1)
                dve.wait_ge(S("g9_ready"), 1)
                dve.tensor_scalar(g9[0:E, 0:B], bank[2][0:E, 0:B], 1.0 / N, g9[0:E, B:B + 1], ALU.mult, ALU.add).then_inc(S("g9_ready"), 1)
                dve.wait_ge(S("grep_mm"), 1)
                dve.tensor_copy(gcol[:, :], bank[3][0:72, 0:B]).then_inc(S("gcol_ready"), 1)
                dve.wait_ge(S("gcol_ready"), 1)
                dve.tensor_tensor(gblk[:, :, :], gcol[:, :].unsqueeze(1).to_broadcast([72, 8, B]),
                                  C("jmask", 72).unsqueeze(2).to_broadcast([72, 8, B]), ALU.mult).then_inc(S("gblk_ready"), 1)
                dve.wait_ge(S("bm_mm"), 1)
                dve.tensor_copy(w1m[:, :, F:F + 5].rearrange("p b k -> p k b"), bank[4][:, 0:5 * B].rearrange("p (k b) -> p k b", k=5)).then_inc(S("bm_copied"), 1)
                for w in range(2):
                    with dve.Fori(4 * w, 4 * w + 4) as n:
                        for r in range(2):
                            for s in (1, 3):
                                dve.wait_ge(S("mg_mm"), n * 8 + (4 * r + s + 1))
                                dve.tensor_copy(merged_dst(w, n * 2 + (r - 8 * w), s),
                                                bank[4 * r + s].rearrange("p (g j b) -> p g j b", g=2, j=8)).then_inc(S("mg_dve"), 1)
                dve.wait_ge(S("mg_dve"), 32)
                dve.wait_ge(S("mg_act"), 32)

                def ffn_step(t, r):
                    if live(t, 0, B):
                        dve.wait_ge(S("f_mm"), t + 1)
                        reuse(dve, S("f_y"), t, 2)
                        for k in (2, 3):
                            ins = dve.tensor_scalar(hbuf[:, r, k, :], bank[2 * r + 1][:, (k - 2) * N:(k - 1) * N], wst[:, r, F + k:F + k + 1], 0.0, ALU.add, ALU.max)
                        ins.then_inc(S("f_h_dve"), 1)
                    if live(t, 1, B):
                        q = (r - 1) % 2
                        dve.wait_ge(S("f_y"), t)
                        dve.scalar_tensor_tensor(sample(xn, t - 1), bank[4 + q][:, 0:N], wst[:, q, F + 4:F + 5], sample(xn, t - 1), ALU.add, ALU.add).then_inc(S("f_res"), 1)
                run_steps(dve, B, 1, ffn_step, 4)
            meet(dve, "lnf")
            if stop > 5:
                ln_dve(dve, "lnf")
            meet(dve, "lna")
            if stop > 6:
                ln_dve(dve, "lna")
            meet(dve, "attn1")

            def attn1_step(t, r):
                if live(t, 2, B):
                    dve.wait_ge(S("b_t_done"), t - 1)
                    reuse(dve, S("b_o_done"), t - 2, 2)
                    dve.tensor_copy(b_et[:, r, 4:8, 0:P], bank[6].rearrange("p (h n) -> p h n", h=4))
                    dve.tensor_copy(b_et[:, r, :, P:N], bank[7][:, 0:HT].rearrange("p (h n) -> p h n", h=H))
                    dve.tensor_copy(b_ett[0:HT, r, :], bank[7][0:HT, HT:HT + N]).then_inc(S("b_et_dve"), 1)
                if live(t, 0, B):
                    dve.wait_ge(S("b_q_ready"), t + 1)
                    reuse3(dve, S("b_s_done"), t)
                    dve.tensor_tensor(b_qm[:, r], b_q[:, r, P:N].unsqueeze(1).to_broadcast([P, H, NTAIL]),
                                      C("hmask").unsqueeze(2).to_broadcast([P, H, NTAIL]), ALU.mult).then_inc(S("b_qm_ready"), 1)
                if live(t, 1, B):
                    q = (r - 1) % 2
                    for g in range(3):
                        dve.wait_ge(S("b_s_done"), (t - 1) * 3 + (g + 1))
                        if g == 0:
                            reuse(dve, S("b_en_ready"), t - 1, 2)
                        dve.tensor_reduce(b_nm[:, q, 3 * g:3 * g + 3], ps3a[:, g, 0:3 * N].rearrange("p (h n) -> p h n", h=3), AX, ALU.max, negate=True).then_inc(S("b_nm_ready"), 1)
                if live(t, 2, B):
                    dve.wait_ge(S("b_o_done"), t - 1)
                    reuse(dve, S("b_y_done"), t - 2, 2)
                    dve.tensor_copy(b_o[:, r, :], bank[1][:, 0:N]).then_inc(S("b_o_ready"), 1)
                if live(t, 0, B):
                    dve.wait_ge(S("b_v_done"), t + 1)
                    reuse(dve, S("b_o_done"), t, 2)
                    dve.tensor_copy(diagonal(b_v, r), bank[0][:, 0:P].rearrange("p (h d) -> p h d", h=H))
                    dve.tensor_tensor(b_vt[0:HT, r, :], bank[0][0:HT, P:2 * P], C("vmask", HT), ALU.mult).then_inc(S("b_vm_ready"), 1)
                if live(t, 2, B):
                    dve.wait_ge(S("b_y_done"), t - 1)
                    dve.scalar_tensor_tensor(sample(hT, t - 2), bank[1][:, 256:256 + N], V("bpn"), sample(hT, t - 2), ALU.add, ALU.add).then_inc(S("b_h"), 1)
                if live(t, 1, B):
                    q = (r - 1) % 2
                    dve.wait_ge(S("b_e_ready"), (t - 1) * 3 + 3)
                    dve.reciprocal(b_r[:, q, 0:8], b_s[:, q, 0:8]).then_inc(S("b_r1"), 1)
                    dve.reciprocal(b_r[0:HT, q, 8:9], b_s[0:HT, q, 8:9]).then_inc(S("b_r2"), 1)
                    dve.wait_ge(S("b_r1"), t)
                    dve.tensor_tensor(b_ek[:, q, :].rearrange("p (h n) -> p h n", h=H), b_e[:, q, 0:8, P:N], b_r[:, q, 0:8].unsqueeze(2).to_broadcast([P, H, NTAIL]), ALU.mult)
                    dve.tensor_tensor(b_e[:, q, 0:8, 0:P], b_e[:, q, 0:8, 0:P], b_r[:, q, 0:8].unsqueeze(2).to_broadcast([P, H, P]), ALU.mult)
                    dve.wait_ge(S("b_r2"), t)
                    dve.tensor_scalar(b_e[0:HT, q, 8, :], b_e[0:HT, q, 8, :], b_r[0:HT, q, 8:9], None, ALU.mult).then_inc(S("b_en_ready"), 1)
                    dve.wait_ge(S("b_en_ready"), t)
                    dve.tensor_tensor(b_tt[0:HT, q, :].rearrange("p (h n) -> p h n", h=H), b_e[0:HT, q, 8, P:N].unsqueeze(1).to_broadcast([HT, H, NTAIL]),
                                      C("tmask", HT).rearrange("p (h n) -> p h n", h=H), ALU.mult).then_inc(S("b_tt_ready"), 1)
            if stop > 6:
                dve.wait_ge(S("b_v_zero"), 1)
                run_steps(dve, B, 2, attn1_step, 4)
            meet(dve, "lnm")
            if stop > 7:
                ln_dve(dve, "lnm")
            meet(dve, "gate")
            if stop > 8:
                dve.wait_ge(S("moe_in"), 16 * 7)

                def route_step(t, r):
                    dve.wait_ge(S("r_tr"), t + 1)
                    dve.tensor_copy(m_s[0:SUB, bass.ds(t * NSUB, NSUB), :], bank[2 + r][0:SUB, 0:NSUB * E].rearrange("p (s e) -> p s e", e=E)).then_inc(S("r_s"), 1)
                run_steps(dve, NCH, 0, route_step, 2)
                dve.wait_ge(S("r_s"), NCH)
                count = [0]

                def chain(ins):
                    count[0] += 1
                    ins.then_inc(S("router"), 1)
                    dve.wait_ge(S("router"), count[0])
                SB = NCH * NSUB
                s_, b_, one1, one2, tmp = m_s[0:SUB], m_t[0][0:SUB], m_t[1][0:SUB], m_t[2][0:SUB], m_t[3][0:SUB]
                mx = m_1[4][0:SUB, :]

                def wide(v):
                    return v.unsqueeze(2).to_broadcast([SUB, SB, E])

                def narrow(v):
                    return v.unsqueeze(1).to_broadcast([SUB, SB, E])

                def first_best(onehot, val):
                    chain(dve.tensor_reduce(mx, val, AX, ALU.max))
                    chain(dve.tensor_tensor(onehot, val, wide(mx), ALU.is_equal))
                    chain(dve.tensor_tensor(onehot, onehot, narrow(C("rank", SUB)), ALU.mult))
                    chain(dve.tensor_reduce(m_1[3][0:SUB, :], onehot, AX, ALU.max))
                    chain(dve.tensor_tensor(onehot, narrow(C("rank", SUB)), wide(m_1[3][0:SUB, :]), ALU.is_equal))

                def without(dst, val, onehot):
                    chain(dve.scalar_tensor_tensor(dst, onehot, -BIG, val, ALU.mult, ALU.add))
                first_best(one1, s_)
                chain(dve.tensor_copy(m_1[0][0:SUB, :], mx))
                without(tmp, s_, one1)
                chain(dve.tensor_reduce(m_1[1][0:SUB, :], tmp, AX, ALU.max))
                dve.sem_inc(S("top_ready"), 2)
                chain(dve.tensor_tensor(b_, s_, narrow(m_bias[0:SUB, :]), ALU.add))
                first_best(one1, b_)
                without(tmp, b_, one1)
                first_best(one2, tmp)
                dve.wait_ge(S("top_exp"), 2)
                for k in range(2):
                    chain(dve.tensor_scalar(m_1[k][0:SUB, :], m_1[k][0:SUB, :], 1.0, None, ALU.add))
                    chain(dve.reciprocal(m_1[k][0:SUB, :], m_1[k][0:SUB, :]))
                chain(dve.tensor_tensor(m_1[2][0:SUB, :], m_1[0][0:SUB, :], m_1[1][0:SUB, :], ALU.add))
                chain(dve.reciprocal(m_1[2][0:SUB, :], m_1[2][0:SUB, :]))
                for k, onehot in enumerate((one1, one2)):
                    chain(dve.tensor_tensor(m_1[k][0:SUB, :], m_1[k][0:SUB, :], m_1[2][0:SUB, :], ALU.mult))
                    chain(dve.tensor_tensor(onehot, onehot, wide(m_1[k][0:SUB, :]), ALU.mult))
                chain(dve.tensor_tensor(tmp, one1, one2, ALU.add))
                dve.sem_inc(S("comb"), 1)
            meet(dve, "moe")
            if stop > 8:
                dve.sem_inc(S("m_h"), 3)
                dve.sem_inc(S("m_f"), 1)

                def chunk_dve(c):
                    for v in range(UN):
                        e, k, s = v // 2, v % 2, v % 3
                        dve.wait_ge(S("m_silu"), c * UN + (v + 1))
                        src = m_a[:, s, :]
                        if e < E:
                            if k == 0:
                                dve.wait_ge(S("cb_taken"), c * E + (e + 2))
                            ins = dve.tensor_tensor(m_g[:, s, :], src, m_cb[:, e % 2, :], ALU.mult)
                            ins.then_inc(S("cb_used" if k == 1 else "cb_half"), 1)
                            dve.wait_ge(S("cb_used" if k == 1 else "cb_half"), c * E + (e + 1 + (2 if k == 1 else 0)))
                            src = m_g[:, s, :]
                        dve.wait_ge(S("m_y"), c * UN + (v + 1))
                        dve.tensor_tensor(m_h[:, s, :], bank[2 * s + 1][:, 0:CH], src, ALU.mult).then_inc(S("m_h"), 1)
                    dve.wait_ge(S("m_y"), c * UN + (UN + 3))
                    if not is_known(c):
                        dve.wait_ge(S("m_tr"), c)
                    dve.tensor_tensor(m_f[:, 0, :], bank[6][:, 0:CH], chunk(hT, c), ALU.add).then_inc(S("m_f"), 1)
                dve.sem_inc(S("cb_used"), 2)
                chunk_dve(0)
                with dve.Fori(1, NCH) as c:
                    chunk_dve(c)
            else:
                pass


UN = 2 * (E + 1)


def diagonal(values, r):
    v = values[:, r].rearrange("p h n -> p (h n)")
    return bass.AP(v.tensor, v.offset, [v.ap[0], [P + HD, H], [1, HD]])


_INS = ['x', 'txt', 'L0_tok_W1_w', 'L0_tok_W1_b', 'L0_tok_W1_sw', 'L0_tok_W1_sb', 'L0_tok_W2_w', 'L0_tok_W2_b', 'L0_tok_W2_sw', 'L0_tok_W2_sb', 'L0_tok_W3_w', 'L0_tok_W3_b', 'L0_tok_eps_in1', 'L0_tok_eps_out1', 'L0_tok_eps_in2', 'L0_tok_eps_out2', 'L0_attn_w_qkv', 'L0_attn_w_proj', 'L0_attn_b_proj', 'L0_ffn_gfc1_w', 'L0_ffn_gfc1_b', 'L0_ffn_gfc2_w', 'L0_ffn_gfc2_b', 'L0_ffn_W1', 'L0_ffn_b1', 'L0_ffn_W2', 'L0_ffn_b2', 'L0_ffn_ln_g', 'L0_ffn_ln_b', 'L0_ffn_tv_W1', 'L0_ffn_tv_b1', 'L0_ffn_tv_W2', 'L0_ffn_tv_b2', 'L0_ffn_tv_ln_g', 'L0_ffn_tv_ln_b', 'L1_attn_Wq', 'L1_attn_bq', 'L1_attn_Wk', 'L1_attn_bk', 'L1_attn_Wv', 'L1_attn_bv', 'L1_attn_Wp', 'L1_attn_bp', 'L1_ffn_gate_w', 'L1_ffn_biases', 'L1_ffn_w1', 'L1_ffn_w3', 'L1_ffn_w2', 'L1_ffn_sw1', 'L1_ffn_sw3', 'L1_ffn_sw2']


def shape_constants(np):
    c = np.zeros((P, NCONST), np.float32)

    def put(name, a):
        at, n = CONST[name]
        c[0:a.shape[0], at:at + n] = a
    p = np.arange(P)
    put("ident", np.eye(P))
    put("centre", np.eye(P) - 1.0 / P)
    put("average", np.full((P, P), 1.0 / P))
    pos = np.arange(NP_, dtype=np.float32)[:, None]
    div = np.exp(np.arange(0, D, 2, dtype=np.float32) * np.float32(-np.log(10000.0) / D))
    ang = pos * div
    put("pos", np.stack([np.sin(ang), np.cos(ang)], axis=-1).reshape(NP_, D).T)
    put("jmask", (np.arange(72)[:, None] % 8 == np.arange(8)[None]))
    put("hmask", p[:, None] // HD == np.arange(H)[None])
    ht = np.arange(HT)
    put("vmask", ht[:, None] // NTAIL == p[None] // HD)
    put("tmask", ht[:, None] // NTAIL == ht[None] // NTAIL)
    put("dsel", ht[:, None] % NTAIL == np.arange(NTAIL)[None])
    put("rep", np.arange(E + 1)[:, None] == np.arange(72)[None] // 8)
    put("select", np.arange(E)[:, None] == np.arange(E * P)[None] // P)
    put("rank", np.broadcast_to(E - np.arange(E), (P, E)))
    return c


def build(nc, args, const, out, stop=99):
    def group(prefix):
        return {n[len(prefix):]: a for n, a in args.items() if n.startswith(prefix)}
    early_fusion(nc, args["x"], args["txt"], group("L0_tok_"), group("L0_attn_"), group("L0_ffn_"),
                 group("L1_attn_"), group("L1_ffn_"), const, out, stop)


def kernel(**inputs):
    import numpy as _np
    import concourse.bacc as _bacc
    from concourse import mybir as _mybir
    from concourse.bass_utils import run_bass_kernel_spmd as _run

    nc = _bacc.Bacc("TRN2", target_bir_lowering=False, num_devices=1)
    arrays, args = {}, {}
    for name in _INS:
        a = _np.ascontiguousarray(inputs[name])
        arrays[f"in_{name}_dram"] = a
        args[name] = nc.dram_tensor(f"in_{name}_dram", a.shape, _mybir.dt.from_np(a.dtype), kind="ExternalInput").ap()
    arrays["shape_constants"] = shape_constants(_np)
    const = nc.dram_tensor("shape_constants", (P, NCONST), F32, kind="ExternalInput").ap()
    out = nc.dram_tensor("out_0_dram", (B, N, D), F32, kind="ExternalOutput").ap()
    build(nc, args, const, out)
    r = _run(nc, [arrays], core_ids=[0])
    return r.results[0]["out_0_dram"]
```

```python
from contextlib import ExitStack

import concourse.bass as bass
from concourse import mybir

P = 128
B, NP_, NT, D = 32, 64, 77, 128
N = NP_ + NT
T = B * N
NTAIL = N - P
CH = 376
NCH = T // CH
SUB = 94
NSUB = CH // SUB
H, HD = 8, 16
KC = 40
HT = H * NTAIL
E = 8
F = 512
HID = 256
FW = F + 5
GB = 2 * N
LN_EPS = 1e-5
LN_MERGE = 0.03
BIG = 3.0e38

ALU = mybir.AluOpType
ACT = mybir.ActivationFunctionType
AX = mybir.AxisListType.X
F32 = mybir.dt.float32
F32R = mybir.dt.float32r

CONST = {}
_at = 0
for _name, _n in (("ident", 128), ("centre", 128), ("average", 128), ("pos", NP_), ("jmask", 8),
                  ("hmask", H), ("vmask", 128), ("tmask", HT), ("dsel", NTAIL), ("rep", 72),
                  ("select", E * 128), ("rank", E)):
    CONST[_name] = (_at, _n)
    _at += _n
NCONST = _at

VECS = ["W1_b", "W1_sb", "W2_b", "W2_sb", "eps_out1", "eps_out2", "W3_b", "b_proj", "gfc1_b", "b2",
        "ln_g", "ln_b", "bq", "bk", "bv", "bp", "b1n", "b2n", "eo1", "eo2", "lng", "lnb", "bpn",
        "eps", "tmp0", "tmp1", "b3", "spare"]
VEC = {n: i for i, n in enumerate(VECS)}

SLOT = {n: i for i, n in enumerate(["W3", "gfc1", "proj", "v0", "Wq", "Wk", "Wv", "Wp",
                                    "n1a", "n1b", "n2a", "n2b", "gfc2", "gate", "tvg", "tvs"])}


UN = 2 * (E + 1)
ORDER = [E] + list(range(E))
PHASES = ["ln1", "attn0", "ln2", "ffn", "lnf", "lna", "attn1", "lnm", "gate", "moe"]
NORMS = ["ln1", "ln2", "lnf", "lna", "lnm"]


def is_known(u):
    return isinstance(u, int)


def reuse(eng, sem, u, depth):
    if is_known(u):
        if u >= depth:
            eng.wait_ge(sem, u - depth + 1)
    else:
        eng.wait_ge(sem, u - depth + 1)


def reuse3(eng, sem, u):
    if not is_known(u) or u >= 2:
        eng.wait_ge(sem, u * 3 - 3)


def run_steps(eng, units, lag, body, head):
    total = units + lag
    rounds = (units - head) // 2
    for t in range(head):
        body(t, t % 2)
    with eng.Fori(0, rounds) as i:
        for r in range(2):
            body(i * 2 + (head + r), r)
    for t in range(head + 2 * rounds, total):
        body(t, t % 2)


def live(t, k, units):
    return not is_known(t) or 0 <= t - k < units


def early_fusion(nc, x, txt, tok, attn0, ffn, attn1, moe, const, out, stop=99):
    with ExitStack() as ctx:
        def sb(name, shape, dt=F32, scope=None):
            return (scope or ctx).enter_context(nc.sbuf_tensor(name, shape, dt))

        sems = {}

        def S(name):
            if name not in sems:
                sems[name] = ctx.enter_context(nc.semaphore(name))
            return sems[name]

        ps = [ctx.enter_context(nc.psum_tensor(f"ps{i}", [P, 512], F32)) for i in range(2)]
        ps3a = ctx.enter_context(nc.psum_tensor("ps3a", [P, 3, 512], F32))
        ps3b = ctx.enter_context(nc.psum_tensor("ps3b", [P, 3, 512], F32))
        bank = [ps[0][:, :], ps[1][:, :]] + [ps3a[:, i, :] for i in range(3)] + [ps3b[:, i, :] for i in range(3)]

        hT = sb("hT", [P, T])
        xn = sb("xn", [P, T])
        cst = sb("cst", [P, NCONST])
        vec = sb("vec", [P, len(VECS)])
        wT = sb("wT", [P, len(SLOT), P])
        pq = sb("pq", [P, 2, P])
        small = sb("small", [P, 64])
        early = ctx.enter_context(ExitStack())
        arena = sb("arena", [P, B * FW + B * F], scope=early)

        def C(name, rows=P):
            a, n = CONST[name]
            return cst[0:rows, a:a + n]

        def V(name, rows=P):
            return vec[0:rows, VEC[name]:VEC[name] + 1]

        def W(name):
            return wT[:, SLOT[name], :]

        used = [0]

        def take(n):
            a = used[0]
            used[0] += n
            assert used[0] <= arena.shape[1], used[0]
            return arena[:, a:a + n]

        ident = C("ident")

        xp = take(2 * 2048).rearrange("p (t r w c) -> p t r w c", t=2, r=16, w=8)
        xq = take(2 * 2048).rearrange("p (t w n) -> p t w n", t=2, w=8)
        xT = take(2 * 2048).rearrange("p (k n) -> p k n", k=2)
        wN = take(len(SLOT) * P).rearrange("p (s c) -> p s c", s=len(SLOT))
        wqk = take(2 * P).rearrange("p (s c) -> p s c", s=2)
        txn = take(B * D).rearrange("p (b d) -> p b d", b=B)
        sw = take(2 * 256).rearrange("p (k n) -> p k n", k=2)
        wraw = take(2 * 256).rearrange("p (k n) -> p k n", k=2)
        ei = take(2 * 256).rearrange("p (k n) -> p k n", k=2)
        ea = take(2 * 256).rearrange("p (k n) -> p k n", k=2)
        mish = take(6 * 512).rearrange("p (k n) -> p k n", k=6)
        tokx = take(2 * 512).rearrange("p (k n) -> p k n", k=2)
        tvln = sb("tvln", [P, 2, E], scope=early)
        used[0] = 0
        a_u = take(2 * N).rearrange("p (k n) -> p k n", k=2)
        a_x = take(2 * N).rearrange("p (k n) -> p k n", k=2)
        a_v = take(2 * 2 * P).rearrange("p (k m n) -> p k m n", k=2, m=2)
        a_e = take(2 * 2 * N).rearrange("p (k m n) -> p k m n", k=2, m=2)
        a_t = take(2 * 2 * N).rearrange("p (k m n) -> p k m n", k=2, m=2)
        a_m = take(2 * 6).rearrange("p (k m) -> p k m", k=2)
        used[0] = 0
        w1m = take(B * FW).rearrange("p (b f) -> p b f", b=B)
        w2m = take(B * F).rearrange("p (b f) -> p b f", b=B)
        tvc = sb("tvc", [P, 2, 1024], scope=early)
        tvb = sb("tvb", [E + 1, F + D], scope=early)
        g9 = sb("g9", [E + 1, B + 1], scope=early)
        gblk = sb("gblk", [P, 8, B], scope=early)
        gcol = sb("gcol", [72, B], scope=early)
        ghm = sb("ghm", [P, B], scope=early)
        wst = sb("wst", [P, 2, 2 * F], scope=early)
        hbuf = sb("hbuf", [P, 2, 4, N], scope=early)
        ln_early = wst[:, :, :].rearrange("p k n -> p (k n)")[:, 0:4 * CH].rearrange("p (k n) -> p k n", k=4)
        early.close()

        wparts = sb("wparts", [P, 2, 3 * (E + 1) * HID], F32R)
        ln_late = sb("ln_late", [P, 4, CH])
        middle = ctx.enter_context(ExitStack())
        wraw_e = sb("wraw_e", [P, 3 * (E + 1) * HID], scope=middle)
        m_w1, m_w3, m_w2 = (wraw_e[:, i * (E + 1) * HID:(i + 1) * (E + 1) * HID] for i in range(3))
        m_w1 = m_w1.rearrange("p (e h) -> p e h", e=E + 1)
        m_w3 = m_w3.rearrange("p (e h) -> p e h", e=E + 1)
        m_w2 = m_w2.rearrange("p (e k d) -> p e k d", e=E + 1, k=2)
        arena = sb("arena1", [P, 13000], scope=middle)
        used[0] = 0
        b_x = take(2 * N).rearrange("p (k n) -> p k n", k=2)
        b_xt = take(2 * HT).rearrange("p (k n) -> p k n", k=2)
        b_ek = take(2 * HT).rearrange("p (k n) -> p k n", k=2)
        b_q = take(2 * N).rearrange("p (k n) -> p k n", k=2)
        b_k = take(2 * N).rearrange("p (k n) -> p k n", k=2)
        b_km = take(2 * H * N).rearrange("p (k h n) -> p k h n", k=2, h=H)
        b_qm = take(2 * HT).rearrange("p (k h n) -> p k h n", k=2, h=H)
        b_v = take(2 * H * P).rearrange("p (k h n) -> p k h n", k=2, h=H)
        b_vt = take(2 * P).rearrange("p (k n) -> p k n", k=2)
        b_nm = take(2 * 9).rearrange("p (k h) -> p k h", k=2)
        b_s = take(2 * 9).rearrange("p (k h) -> p k h", k=2)
        b_r = take(2 * 9).rearrange("p (k h) -> p k h", k=2)
        b_e = take(2 * 9 * N).rearrange("p (k h n) -> p k h n", k=2, h=9)
        b_tt = take(2 * HT).rearrange("p (k n) -> p k n", k=2)
        b_et = take(2 * H * N).rearrange("p (k h n) -> p k h n", k=2, h=H)
        b_ett = take(2 * N).rearrange("p (k n) -> p k n", k=2)
        b_o = take(2 * N).rearrange("p (k n) -> p k n", k=2)
        middle.close()

        xh = sb("xh", [P, T], F32R)
        xl = sb("xl", [P, T], F32R)
        m_ct = sb("m_ct", [P, T], F32R)
        selr = sb("selr", [P, E * P], F32R)
        m_bias = sb("m_bias", [P, E])
        router = ctx.enter_context(ExitStack())
        m_sc = sb("m_sc", [P, 2, CH], scope=router)
        m_s = sb("m_s", [P, NCH * NSUB, E], scope=router)
        m_t = [sb(f"m_t{i}", [P, NCH * NSUB, E], scope=router) for i in range(4)]
        m_1 = [sb(f"m_1{i}", [P, NCH * NSUB], scope=router) for i in range(5)]
        m_chi = sb("m_chi", [P, NCH * NSUB, E], F32R, scope=router)
        m_c40 = sb("m_c40", [P, NCH * NSUB, KC], scope=router)
        router.close()
        m_cb = sb("m_cb", [P, 2, CH])
        m_a = sb("m_a", [P, 3, CH])
        m_g = sb("m_g", [P, 3, CH])
        m_hf = sb("m_hf", [P, 3, CH])
        m_hh = sb("m_hh", [P, 3, CH], F32R)
        m_hl = sb("m_hl", [P, 3, CH], F32R)
        m_f = sb("m_f", [P, CH])
        m_o = sb("m_o", [P, NSUB, D])

        def expert(part, kind, e, k):
            at = (kind * (E + 1) + e) * HID + k * P
            return wparts[:, part, at:at + P]

        def chunk(buf, c, n=CH):
            return buf[:, bass.ds(c * n, n)]

        def sample(buf, b):
            return buf[:, bass.ds(b * N, N)]

        def meet(eng, phase):
            eng.drain().then_inc(S("phases_met"), 1)
            eng.wait_ge(S("phases_met"), 5 * (PHASES.index(phase) + 1))

        def merged_dst(w, c, s):
            if w == 0:
                return w1m[:, :, 0:F].rearrange("p b (j g) -> p g j b", j=8)[:, bass.ds(c * 8 + 2 * s, 2)]
            v = w2m[:, :, :].rearrange("p b (k j g) -> p g k j b", k=4, j=8)
            return v[:, bass.ds(c * 2 + s // 2, 1), 2 * (s % 2):2 * (s % 2) + 2].rearrange("p a k j b -> p (a k) j b")

        def merged_bias(b, k):
            return w1m[:, bass.ds(b, 1), F + k]

        turns = []
        for t in range(2):
            for k in range(2):
                for half in range(2):
                    turns.append(("x", [(xq[:, t, 4 * half + i, k * P:(k + 1) * P], P) for i in range(4)],
                                  xT[:, k, t * 1024:(t + 1) * 1024].rearrange("p (q w) -> p w q", w=8)[:, 4 * half:4 * half + 4, :], P))
        for g in range(4):
            n = min(4, len(SLOT) - 4 * g)
            rows = P if g < 3 else E
            turns.append(("w" if g == 2 else "n",
                          [(wN[0:rows, 4 * g + i, :], rows) for i in range(n)],
                          wT[:, 4 * g:4 * g + n, 0:rows], rows))
        for g in range(8):
            turns.append(("t", [(txn[0:NT, 4 * g + i, :], NT) for i in range(4)],
                          hT[:, 4 * g * N:(4 * g + 4) * N].rearrange("p (b n) -> p b n", n=N)[:, :, NP_:N], NT))

        block = ctx.enter_context(nc.Block())

        @block.sync
        def _(sp):
            sp.dma_start(cst[:, :], const).then_inc(S("const_in"), 16)
            for t in range(2):
                sp.dma_start(xp[:, t].rearrange("p r w c -> p (r w c)"),
                             x[16 * t:16 * t + 16].rearrange("b o (q r) w -> (b o q) (r w)", q=8)).then_inc(S(f"x_in{t}"), 16)
            for k, n in enumerate(("1", "2")):
                sp.dma_start(wraw[:, k, :], tok[f"W{n}_w"]).then_inc(S("noise_in"), 16)
                sp.dma_start(sw[:, k, :], tok[f"W{n}_sw"]).then_inc(S("noise_in"), 16)
                sp.dma_start(ei[:, k, :], tok[f"eps_in{n}"].unsqueeze(0).to_broadcast([P, 256])).then_inc(S("noise_in"), 16)
            vsrc = {"W1_b": tok["W1_b"], "W1_sb": tok["W1_sb"], "W2_b": tok["W2_b"], "W2_sb": tok["W2_sb"],
                    "eps_out1": tok["eps_out1"], "eps_out2": tok["eps_out2"], "W3_b": tok["W3_b"],
                    "b_proj": attn0["b_proj"], "gfc1_b": ffn["gfc1_b"], "b2": ffn["b2"], "ln_g": ffn["ln_g"],
                    "ln_b": ffn["ln_b"], "bq": attn1["bq"], "bk": attn1["bk"], "bv": attn1["bv"], "bp": attn1["bp"]}
            for n, a in vsrc.items():
                sp.dma_start(V(n), a.unsqueeze(1)).then_inc(S("vec_in"), 16)
            nat = {"W3": tok["W3_w"], "gfc1": ffn["gfc1_w"], "proj": attn0["w_proj"], "v0": attn0["w_qkv"][256:384],
                   "Wq": attn1["Wq"], "Wk": attn1["Wk"], "Wv": attn1["Wv"], "Wp": attn1["Wp"]}
            for n, a in nat.items():
                sp.dma_start(wN[:, SLOT[n], :], a).then_inc(S("nat_in"), 16)
            sp.dma_start(wN[0:E, SLOT["gfc2"], :], ffn["gfc2_w"]).then_inc(S("nat_in"), 16)
            sp.dma_start(wN[0:E, SLOT["gate"], :], moe["gate_w"]).then_inc(S("nat_in"), 16)
            sp.dma_start(wN[0:E, SLOT["tvg"], :], ffn["tv_ln_g"]).then_inc(S("nat_in"), 16)
            sp.dma_start(wN[0:E, SLOT["tvs"], :], ffn["tv_ln_b"]).then_inc(S("nat_in"), 16)
            for k in range(2):
                sp.dma_start(wqk[:, k, :], attn0["w_qkv"][128 * k:128 * k + 128]).then_inc(S("nat_in"), 16)
            sp.dma_start(txn[0:NT, :, :], txt.rearrange("b n d -> n b d")).then_inc(S("txt_in"), 16)
            sp.dma_start(tvb[0:E, 0:F], ffn["tv_b1"]).then_inc(S("tvb_in"), 16)
            sp.dma_start(tvb[0:E, F:F + D], ffn["tv_b2"]).then_inc(S("tvb_in"), 16)
            sp.dma_start(tvb[E:E + 1, 0:F], ffn["b1"].unsqueeze(0)).then_inc(S("tvb_in"), 16)
            sp.dma_start(tvb[E:E + 1, F:F + D], ffn["b2"].unsqueeze(0)).then_inc(S("tvb_in"), 16)
            sp.wait_ge(S("g9_ones"), 1)
            sp.dma_start(g9[0:E, B:B + 1], ffn["gfc2_b"].unsqueeze(1)).then_inc(S("g9_in"), 16)
            for ph in ("ln1", "attn0", "ln2", "ffn"):
                meet(sp, ph)
            for w, (tv, base) in enumerate((("tv_W1", "W1"), ("tv_W2", "W2")) if stop > 4 else ()):
                tvr = ffn[tv].rearrange("e (j g) c -> (e j) (g c)", j=8)
                bsr = ffn[base].rearrange("(j g) c -> j (g c)", j=8)

                def load(n, r):
                    if not (is_known(n) and n == 0):
                        sp.wait_ge(S("mg_mm"), n * 8 + (4 * r - 4))
                    at = (n * 2 + (r - 8 * w)) * 1024
                    sp.dma_start(tvc[0:64, r, :], tvr[:, bass.ds(at, 1024)]).then_inc(S(f"tv_in{r}"), 16)
                    sp.dma_start(tvc[64:72, r, :], bsr[:, bass.ds(at, 1024)]).then_inc(S(f"tv_in{r}"), 16)
                if w == 0:
                    load(0, 0)
                    load(0, 1)
                with sp.Fori(1 if w == 0 else 4, 4 if w == 0 else 8) as n:
                    for r in range(2):
                        load(n, r)
            meet(sp, "lnf")
            for dst, src in ((m_w1, "w1"), (m_w3, "w3")):
                sp.dma_start(dst[:, 0:E, :], moe[src].rearrange("e d h -> d e h")).then_inc(S("moe_in"), 16)
                sp.dma_start(dst[:, E, :], moe["s" + src]).then_inc(S("moe_in"), 16)
            for k in range(2):
                sp.dma_start(m_w2[:, 0:E, k, :], moe["w2"].rearrange("e (k h) d -> k h e d", k=2)[k]).then_inc(S("moe_in"), 16)
                sp.dma_start(m_w2[:, E, k, :], moe["sw2"].rearrange("(k h) d -> k h d", k=2)[k]).then_inc(S("moe_in"), 16)
            meet(sp, "lna")
            for ph in ("attn1", "lnm"):
                meet(sp, ph)
            sp.dma_start(m_bias[0:SUB, :], moe["biases"].unsqueeze(0).to_broadcast([SUB, E])).then_inc(S("bias_in"), 16)
            for ph in ("gate", "moe"):
                meet(sp, ph)
            o = out.rearrange("b n d -> (b n) d").rearrange("(c s p) d -> c p s d", s=NSUB, p=SUB)

            if stop > 8:
                sp.sem_inc(S("stored"), 16)
                with sp.Fori(0, NCH) as c:
                    sp.wait_ge(S("out_copied"), c + 1)
                    sp.dma_start(o[bass.ds(c, 1)].rearrange("a p s d -> (a p) s d"), m_o[0:SUB]).then_inc(S("stored"), 16)
                sp.wait_ge(S("stored"), 16 * (NCH + 1))
            else:
                for n, v in (("tvb_in", 64), ("g9_in", 16), ("moe_in", 128), ("bias_in", 16)):
                    sp.wait_ge(S(n), v)
                sp.dma_start(out.rearrange("b n d -> (b n d)").rearrange("(p t) -> p t", p=P), hT[:, :]).then_inc(S("stored"), 16)
                sp.wait_ge(S("stored"), 16)

        def ln_pe(pe, name):
            done = NCH * NORMS.index(name)
            ln_a = ln_early if name in ("ln1", "ln2") else ln_late
            src = xn if name == "lnf" else hT

            def body(t, r):
                if live(t, 0, NCH):
                    if not is_known(t) or t >= 4:
                        pe.wait_ge(S("ln_out"), t + (done - 3))
                    pe.matmul(bank[r][:, 0:CH], C("centre"), chunk(src, t), start=True, stop=True).then_inc(S("ln_cen"), 1)
                if live(t, 2, NCH):
                    q = (r - 2) % 4
                    pe.wait_ge(S("ln_sq"), t + (done - 1))
                    if not is_known(t) or t >= 6:
                        pe.wait_ge(S("ln_var_read"), t + (done - 5))
                    pe.matmul(bank[4 + q][:, 0:CH], C("average"), ln_a[:, q, :], start=True, stop=True).then_inc(S("ln_var"), 1)
            for t in range(NCH + 2):
                body(t, t % 4)

        def ln_act(act, name):
            done = NCH * NORMS.index(name)
            ln_a = ln_early if name in ("ln1", "ln2") else ln_late

            def body(t, r):
                if live(t, 0, NCH):
                    act.wait_ge(S("ln_cen"), t + (done + 1))
                    if not is_known(t) or t >= 4:
                        act.wait_ge(S("ln_out"), t + (done - 3))
                    act.activation(ln_a[:, r, :], bank[r][:, 0:CH], ACT.Square).then_inc(S("ln_sq"), 1)
                if live(t, 2, NCH):
                    q = (r - 2) % 4
                    act.wait_ge(S("ln_var"), t + (done - 1))
                    act.activation(ln_a[:, q, :], bank[4 + q][:, 0:CH], ACT.Ln, bias=V("eps")).then_inc(S("ln_var_read"), 1)
                    act.wait_ge(S("ln_var_read"), t + (done - 1))
                    act.activation(ln_a[:, q, :], ln_a[:, q, :], ACT.Exp, scale=-0.5).then_inc(S("ln_rs"), 1)
            for t in range(NCH + 2):
                body(t, t % 4)

        def ln_dve(dve, name):
            done = NCH * NORMS.index(name)
            ln_a = ln_early if name in ("ln1", "ln2") else ln_late

            def body(t, r):
                dve.wait_ge(S("ln_rs"), t + (done + 1))
                dve.tensor_tensor(chunk(xn, t), bank[r][:, 0:CH], ln_a[:, r, :], ALU.mult).then_inc(S("ln_out"), 1)
                if name == "lnf":
                    dve.wait_ge(S("ln_out"), t + (done + 1))
                    dve.tensor_scalar(chunk(xn, t), chunk(xn, t), V("lng"), V("lnb"), ALU.mult, ALU.add).then_inc(S("lnf_aff"), 1)
                    dve.wait_ge(S("lnf_aff"), t + 1)
                    dve.tensor_tensor(chunk(hT, t), chunk(hT, t), chunk(xn, t), ALU.add)
                if name == "lnm":
                    dve.wait_ge(S("ln_out"), t + (done + 1))
                    dve.tensor_copy(chunk(xh, t), chunk(xn, t)).then_inc(S("xh_ready"), 1)
            for t in range(NCH):
                body(t, t % 4)

        @block.gpsimd
        def _(pool):
            pool.memset(V("eps"), LN_EPS).then_inc(S("eps_set"), 1)
            pool.memset(g9[:, B:B + 1], 1.0).then_inc(S("g9_ones"), 1)
            meet(pool, "ln1")
            pool.memset(tvc[64:P, :, :], 0.0).then_inc(S("tvc_zero"), 1)
            pool.memset(gblk[64:P, :, :], 0.0).then_inc(S("tvc_zero"), 1)
            meet(pool, "attn0")

            def stage0(t, r):
                reuse(pool, S("a_v_done"), t, 2)
                pool.tensor_copy(a_x[:, r, :], sample(xn, t)).then_inc(S("a_x_ready"), 1)
            if stop > 2:
                run_steps(pool, B, 0, stage0, 2)
            for ph in ("ln2", "ffn"):
                meet(pool, ph)
            if stop > 4:
                pool.wait_ge(S("mg_act"), 32)
                pool.wait_ge(S("mg_dve"), 32)

                def stage_w(t, r):
                    reuse(pool, S("f_y"), t, 2)
                    pool.tensor_copy(wst[:, r, F:2 * F], w2m[:, bass.ds(t, 1), :].rearrange("p a f -> p (a f)")).then_inc(S("f_w2"), 1)
                run_steps(pool, B, 0, stage_w, 2)
            meet(pool, "lnf")
            meet(pool, "lna")
            step = (E + 1) * HID
            for k in range(3):
                pool.wait_ge(S("w_high"), k + 1)
                pool.tensor_tensor(wparts[:, 1, k * step:(k + 1) * step], wraw_e[:, k * step:(k + 1) * step],
                                   wparts[:, 0, k * step:(k + 1) * step].bitcast(F32), ALU.subtract)
            if stop > 6:
                pool.memset(b_v[:, :, :, :], 0.0).then_inc(S("b_v_zero"), 1)
            meet(pool, "attn1")

            def masked_keys(t, r):
                if live(t, 0, B):
                    pool.wait_ge(S("b_k_ready"), t + 1)
                    reuse3(pool, S("b_s_done"), t)
                    pool.tensor_tensor(b_km[:, r], b_k[:, r, :].unsqueeze(1).to_broadcast([P, H, N]),
                                       C("hmask").unsqueeze(2).to_broadcast([P, H, N]), ALU.mult).then_inc(S("b_km_ready"), 1)
                if live(t, 1, B):
                    q = (r - 1) % 2
                    reuse(pool, S("b_v_done"), t - 1, 2)
                    pool.tensor_copy(b_x[:, q, :], sample(xn, t - 1))
                    pool.tensor_copy(b_xt[:, q, :].rearrange("p (h n) -> p h n", h=H),
                                     xn[:, bass.ds((t - 1) * N + P, NTAIL)].unsqueeze(1).to_broadcast([P, H, NTAIL])).then_inc(S("b_x_ready"), 1)
            if stop > 6:
                run_steps(pool, B, 1, masked_keys, 4)
            meet(pool, "lnm")
            for c in range(NCH if stop > 7 else 0):
                pool.wait_ge(S("xh_ready"), c + 1)
                pool.tensor_tensor(chunk(xl, c), chunk(xn, c), chunk(xh, c).bitcast(F32), ALU.subtract)
            meet(pool, "gate")
            if stop > 8:
                pool.memset(m_c40[:, :, :], 0.0).then_inc(S("c40_zero"), 1)
            meet(pool, "moe")
            if stop > 8:
                pool.sem_inc(S("m_lo"), 3)

                def low_parts(c):
                    for v in range(UN):
                        s = v % 3
                        pool.wait_ge(S("m_hi"), c * UN + (v + 1))
                        pool.tensor_tensor(m_hl[:, s, :], m_hf[:, s, :], m_hh[:, s, :].bitcast(F32), ALU.subtract).then_inc(S("m_lo"), 1)
                with pool.Fori(0, NCH) as c:
                    low_parts(c)

        @block.tensor
        def _(pe):
            pe.wait_ge(S("const_in"), 16)
            pe.wait_ge(S("psum_zero"), 8)
            for u, (kind, srcs, _, rows) in enumerate(turns):
                if kind == "x":
                    pe.wait_ge(S("xq_ready"), u // 4 + 1)
                if kind == "n":
                    pe.wait_ge(S("nat_in"), 16 * 14)
                if kind == "w":
                    pe.wait_ge(S("noisy"), 2)
                if kind == "t":
                    pe.wait_ge(S("txt_in"), 16)
                if u >= 4:
                    pe.wait_ge(S("turned_act" if u % 2 == 0 else "turned_dve"), (u - 4) // 2 + 1)
                for i, (src, rows) in enumerate(srcs):
                    mm = pe.transpose(bank[u % 4][:, i * rows:(i + 1) * rows], src, ident[0:rows, 0:rows])
                mm.then_inc(S("turned"), 1)
            pe.wait_ge(S("turned_act"), len(turns) // 2)
            pe.wait_ge(S("turned_dve"), len(turns) // 2)
            pe.matmul(bank[4][:, 0:P], wqk[:, 0, :], wqk[:, 1, :], start=True, stop=True)
            pe.matmul(bank[4][:, P:2 * P], wN[:, SLOT["v0"], :], W("proj"), start=True, stop=True)
            pe.wait_ge(S("wp_scaled"), 1)
            pe.matmul(bank[4][:, 2 * P:2 * P + 1], W("Wp"), V("bv"), start=True, stop=True).then_inc(S("wprod"), 1)
            for c in range(4):
                cols = slice(512 * c, 512 * c + 512)
                if c:
                    pe.wait_ge(S("tok_x"), c)
                for k in range(2):
                    pe.matmul(bank[0], W("n1a" if k == 0 else "n1b"), xT[:, k, cols], start=k == 0, stop=k == 1)
                for k in range(2):
                    mm = pe.matmul(bank[1], W("n2a" if k == 0 else "n2b"), xT[:, k, cols], start=k == 0, stop=k == 1)
                mm.then_inc(S("tok_g"), 1)
                pe.wait_ge(S("tok_x"), c + 1)
                if c >= 2:
                    pe.wait_ge(S("tok_h"), c - 1)
                pe.matmul(bank[2 + c % 2], W("W3"), tokx[:, c % 2, :], start=True, stop=True).then_inc(S("tok_y"), 1)
            meet(pe, "ln1")
            if stop > 1:
                ln_pe(pe, "ln1")
            meet(pe, "attn0")

            def attn0_step(t, r):
                q = (r - 1) % 2
                if live(t, 0, B):
                    reuse(pe, S("a_u_ready"), t, 1)
                    pe.matmul(bank[0][:, 0:N], pq[:, 0, :], sample(xn, t), start=True, stop=True).then_inc(S("a_u_done"), 1)
                if live(t, 3, B):
                    pe.wait_ge(S("a_a_ready"), t - 2)
                    reuse(pe, S("a_t_ready"), t - 3, 2)
                    tp = bank[5 + q]
                    pe.transpose(tp[:, 0:P], a_e[:, q, 0, 0:P], ident)
                    pe.transpose(tp[:, P:N], a_e[0:NTAIL, q, 1, 0:P], ident[0:NTAIL, 0:NTAIL])
                    pe.transpose(tp[0:NTAIL, N:N + P], a_e[:, q, 0, P:N], ident)
                    pe.transpose(tp[0:NTAIL, N + P:2 * N], a_e[0:NTAIL, q, 1, P:N], ident[0:NTAIL, 0:NTAIL]).then_inc(S("a_t_done"), 1)
                if live(t, 1, B):
                    pe.wait_ge(S("a_u_ready"), t)
                    reuse(pe, S("a_e_ready"), t - 1, 2)
                    sc = bank[1 + q]
                    pe.matmul(sc[:, 0:N], a_u[:, q, 0:P], sample(xn, t - 1), start=True, stop=True)
                    pe.matmul(sc[0:NTAIL, N:2 * N], a_u[:, q, P:N], sample(xn, t - 1), start=True, stop=True, skip_group_check=True).then_inc(S("a_s_done"), 1)
                if live(t, 3, B):
                    pe.wait_ge(S("a_x_ready"), t - 2)
                    reuse(pe, S("a_v_ready"), t - 3, 1)
                    pe.matmul(bank[7][:, 0:P], a_x[:, q, 0:P], pq[:, 1, :], start=True, stop=True)
                    pe.matmul(bank[7][0:NTAIL, P:2 * P], a_x[:, q, P:N], pq[:, 1, :], start=True, stop=True, skip_group_check=True).then_inc(S("a_v_done"), 1)
                if live(t, 4, B):
                    pe.wait_ge(S("a_v_ready"), t - 3)
                    pe.wait_ge(S("a_t_ready"), t - 3)
                    reuse(pe, S("a_h"), t - 4, 2)
                    o = bank[3 + r][:, 0:N]
                    pe.matmul(o, W("v0"), sample(xn, t - 4), start=True, stop=False)
                    pe.matmul(o, a_v[:, r, 0, :], a_t[:, r, 0, :], start=False, stop=False)
                    pe.matmul(o, a_v[0:NTAIL, r, 1, :], a_t[0:NTAIL, r, 1, :], start=False, stop=True).then_inc(S("a_o_done"), 1)
            if stop > 2:
                run_steps(pe, B, 4, attn0_step, 6)
            meet(pe, "ln2")
            if stop > 3:
                ln_pe(pe, "ln2")
            meet(pe, "ffn")
            if stop > 4:
                def gate_step(t, r):
                    reuse(pe, S("gh_done"), t, 2)
                    pe.matmul(bank[r][:, 0:GB], W("gfc1"), chunk(xn, t, GB), start=True, stop=True).then_inc(S("gh_mm"), 1)
                run_steps(pe, B // 2, 0, gate_step, 2)
                pe.wait_ge(S("gh_sum"), B // 2)
                pe.matmul(bank[2][0:E, 0:B], W("gfc2")[:, 0:E], ghm[:, :], start=True, stop=True).then_inc(S("g_mm"), 1)
                pe.wait_ge(S("g9_ready"), 2)
                pe.matmul(bank[3][0:72, 0:B], C("rep", E + 1), g9[:, 0:B], start=True, stop=True).then_inc(S("grep_mm"), 1)
                pe.wait_ge(S("tvb_in"), 64)
                for k in range(5):
                    mm = pe.matmul(bank[4][:, k * B:(k + 1) * B], tvb[:, k * P:(k + 1) * P], g9[:, 0:B], start=True, stop=True, skip_group_check=True)
                mm.then_inc(S("bm_mm"), 1)
                pe.wait_ge(S("gblk_ready"), 1)
                def merge(n, r):
                    pe.wait_ge(S(f"tv_in{r}"), n * 32 + 32)
                    for s in range(4):
                        if not (is_known(n) and n == 0):
                            pe.wait_ge(S("mg_act" if s % 2 == 0 else "mg_dve"), n * 4 + (2 * r + s // 2 - 3))
                        for k in range(2):
                            mm = pe.matmul(bank[4 * r + s][:, k * 256:(k + 1) * 256], tvc[:, r, (2 * s + k) * P:(2 * s + k + 1) * P],
                                           gblk[:, :, :].rearrange("p j b -> p (j b)"), start=True, stop=True, skip_group_check=True)
                        mm.then_inc(S("mg_mm"), 1)
                pe.wait_ge(S("bm_copied"), 1)
                for r in range(2):
                    merge(0, r)
                with pe.Fori(1, 8) as n:
                    for r in range(2):
                        merge(n, r)
                pe.wait_ge(S("mg_act"), 32)
                pe.wait_ge(S("mg_dve"), 32)

                def ffn_step(t, r):
                    if live(t, 0, B):
                        pe.wait_ge(S("f_w1"), t + 1)
                        reuse(pe, S("f_h_act"), t, 2)
                        reuse(pe, S("f_h_dve"), t, 2)
                        for k in range(4):
                            mm = pe.matmul(bank[2 * r + k // 2][:, (k % 2) * N:(k % 2) * N + N], wst[:, r, k * P:(k + 1) * P],
                                           sample(xn, t), start=True, stop=True, skip_group_check=True)
                        mm.then_inc(S("f_mm"), 1)
                    if live(t, 1, B):
                        q = (r - 1) % 2
                        pe.wait_ge(S("f_w2"), t)
                        pe.wait_ge(S("f_h_act"), t)
                        pe.wait_ge(S("f_h_dve"), t)
                        reuse(pe, S("f_res"), t - 1, 2)
                        for k in range(4):
                            mm = pe.matmul(bank[4 + q][:, 0:N], wst[:, q, F + k * P:F + (k + 1) * P], hbuf[:, q, k, :],
                                           start=k == 0, stop=k == 3)
                        mm.then_inc(S("f_y"), 1)
                run_steps(pe, B, 1, ffn_step, 4)
            meet(pe, "lnf")
            if stop > 5:
                ln_pe(pe, "lnf")
            meet(pe, "lna")
            if stop > 6:
                ln_pe(pe, "lna")
            meet(pe, "attn1")

            def attn1_step(t, r):
                q = (r - 1) % 2
                if live(t, 0, B):
                    reuse(pe, S("b_vm_ready"), t - 2, 1)
                    if is_known(t) and 0 < t < 3:
                        pe.wait_ge(S("b_k_ready"), t)
                    xs = sample(xn, t)
                    pe.matmul(bank[0][:, 0:N], W("Wq"), xs, start=True, stop=True)
                    pe.matmul(bank[0][:, N:2 * N], W("Wk"), xs, start=True, stop=True, skip_group_check=True).then_inc(S("b_qk_done"), 1)
                if live(t, 4, B):
                    pe.wait_ge(S("b_o_ready"), t - 3)
                    pe.matmul(bank[1][:, 256:256 + N], W("Wp"), b_o[:, r, :], start=True, stop=True).then_inc(S("b_y_done"), 1)
                if live(t, 3, B):
                    pe.wait_ge(S("b_en_ready"), t - 2)
                    pe.wait_ge(S("b_tt_ready"), t - 2)
                    reuse(pe, S("b_et_act"), t - 3, 1)
                    reuse(pe, S("b_et_dve"), t - 3, 1)
                    ee = b_e[:, q]
                    for h in range(H):
                        pe.transpose(bank[5 + h // 4][:, (h % 4) * P:(h % 4) * P + P], ee[:, h, 0:P], ident)
                    pe.transpose(bank[7][:, 0:HT], ee[0:HT, 8, 0:P], ident[0:HT, 0:HT])
                    pe.transpose(bank[7][0:HT, HT:HT + P], b_ek[:, q, :], ident)
                    pe.matmul(bank[7][0:HT, HT + P:HT + N], b_tt[0:HT, q, :], C("dsel", HT), start=True, stop=True, skip_group_check=True).then_inc(S("b_t_done"), 1)
                if live(t, 2, B):
                    pe.wait_ge(S("b_x_ready"), t - 1)
                    pe.wait_ge(S("b_k_ready"), min(t + 1, B) if is_known(t) else t + 1)
                    pe.matmul(bank[0][:, 0:P], b_x[:, r, 0:P], W("Wv"), start=True, stop=True)
                    pe.matmul(bank[0][0:HT, P:2 * P], b_xt[:, r, :], W("Wv"),
                              start=True, stop=True, skip_group_check=True).then_inc(S("b_v_done"), 1)
                if live(t, 1, B):
                    pe.wait_ge(S("b_km_ready"), t)
                    pe.wait_ge(S("b_qm_ready"), t)
                    for g in range(3):
                        if not (is_known(t) and t == 1):
                            pe.wait_ge(S("b_e_ready"), (t - 2) * 3 + (g + 1))
                        n = 3 if g < 2 else 2
                        mm = pe.matmul(ps3a[:, g, 0:n * N], b_q[:, q, 0:P], b_km[:, q, 3 * g:3 * g + n, :].rearrange("p h n -> p (h n)"), start=True, stop=True)
                        if g == 2:
                            mm = pe.matmul(ps3a[0:HT, 2, 2 * N:3 * N], b_qm[:, q].rearrange("p h n -> p (h n)"), b_k[:, q, :], start=True, stop=True, skip_group_check=True)
                        mm.then_inc(S("b_s_done"), 1)
                if live(t, 3, B):
                    pe.wait_ge(S("b_et_act"), t - 2)
                    pe.wait_ge(S("b_et_dve"), t - 2)
                    pe.wait_ge(S("b_vm_ready"), t - 2)
                    reuse(pe, S("b_h"), t - 3, 1)
                    o = bank[1][:, 0:N]
                    for h in range(H):
                        pe.matmul(o, b_v[:, q, h, :], b_et[:, q, h, :], start=h == 0, stop=False)
                    pe.matmul(o, b_vt[0:HT, q, :], b_ett[0:HT, q, :], start=False, stop=True).then_inc(S("b_o_done"), 1)
            if stop > 6:
                run_steps(pe, B, 4, attn1_step, 6)
            meet(pe, "lnm")
            if stop > 7:
                ln_pe(pe, "lnm")
            meet(pe, "gate")
            if stop > 8:
                def route_step(t, r):
                    if live(t, 1, NCH):
                        pe.wait_ge(S("r_sc"), t)
                        reuse(pe, S("r_s"), t - 1, 2)
                    if live(t, 0, NCH):
                        reuse(pe, S("r_sc"), t, 2)
                        pe.matmul(bank[r][0:E, 0:CH], W("gate")[:, 0:E], chunk(xn, t), start=True, stop=True).then_inc(S("r_mm"), 1)
                    if live(t, 1, NCH):
                        q = (r - 1) % 2
                        for s in range(NSUB):
                            mm = pe.transpose(bank[2 + q][0:SUB, s * E:(s + 1) * E], m_sc[0:E, q, s * SUB:(s + 1) * SUB], ident[0:E, 0:E])
                        mm.then_inc(S("r_tr"), 1)
                run_steps(pe, NCH, 1, route_step, 4)
                pe.wait_ge(S("comb"), 1)
                for c in range(NCH):
                    if c >= 4:
                        pe.wait_ge(S("ct"), c - 3)
                    for s in range(NSUB):
                        mm = pe.transpose(bank[4 + c % 4][0:KC, s * SUB:(s + 1) * SUB], m_c40[0:SUB, c * NSUB + s, :], ident[0:SUB, 0:SUB])
                    mm.then_inc(S("ct_tr"), 1)
            meet(pe, "moe")
            if stop > 8:
                pe.sem_inc(S("m_tr"), 1)
                pe.sem_inc(S("m_y"), 3)

                def turn_out(cb):
                    pe.wait_ge(S("cb_taken"), cb + 1)
                    for s in range(NSUB):
                        mm = pe.transpose(bank[7][0:SUB, s * P:(s + 1) * P], m_f[:, s * SUB:(s + 1) * SUB], ident)
                    mm.then_inc(S("m_tr"), 1)

                def three(dst, e, kind, k, high, low, start, stop_):
                    pe.matmul(dst, expert(0, kind, e, k), high, start=start, stop=False)
                    pe.matmul(dst, expert(0, kind, e, k), low, start=False, stop=False)
                    return pe.matmul(dst, expert(1, kind, e, k), high, start=False, stop=stop_)

                def down(c, v):
                    if v == 0:
                        pe.wait_ge(S("m_f"), c + 1)
                    pe.wait_ge(S("m_lo"), c * UN + (v + 4))
                    three(bank[6][:, 0:CH], ORDER[v // 2], 2, v % 2, m_hh[:, v % 3, :], m_hl[:, v % 3, :], v == 0, v == UN - 1).then_inc(S("m_y"), 1)

                def chunk_pe(c):
                    later = not is_known(c)
                    for v in range(UN):
                        s = v % 3
                        cb = v // 2
                        if v == 6 and later:
                            pe.wait_ge(S("m_f"), c + 1)
                            turn_out(c * E + 3)
                        if v % 2 == 1 and cb < E:
                            pe.wait_ge(S("cb_taken"), c * E + (cb + 1))
                            if v == 7 and later:
                                pe.wait_ge(S("out_copied"), c)
                        pe.wait_ge(S("m_prod"), c * UN + (v + 1))
                        three(bank[2 * s][:, 0:CH], ORDER[v // 2], 0, v % 2, chunk(xh, c), chunk(xl, c), True, True)
                        three(bank[2 * s + 1][:, 0:CH], ORDER[v // 2], 1, v % 2, chunk(xh, c), chunk(xl, c), True, True).then_inc(S("m_ab"), 1)
                        if v % 2 == 1 and cb < E:
                            pe.matmul(bank[7][:, 0:CH], selr[0:KC, cb * P:(cb + 1) * P], m_ct[0:KC, bass.ds(c * CH, CH)],
                                      start=True, stop=True).then_inc(S("cb_mm"), 1)
                        if v >= 3:
                            down(c, v - 3)
                        elif later:
                            down(c - 1, UN + v - 3)
                chunk_pe(0)
                with pe.Fori(1, NCH) as c:
                    chunk_pe(c)
                for v in range(UN - 3, UN):
                    down(NCH - 1, v)
                pe.wait_ge(S("m_f"), NCH + 1)
                turn_out(NCH * E)

        @block.scalar
        def _(act):
            act.wait_ge(S("noise_in"), 96)
            act.wait_ge(S("vec_in"), 16 * 16)
            act.activation(ea[:, :, :], ei[:, :, :], ACT.Abs).then_inc(S("f_abs"), 1)
            act.activation(V("tmp0"), V("eps_out1"), ACT.Abs).then_inc(S("f_abs"), 1)
            act.activation(V("tmp1"), V("eps_out2"), ACT.Abs).then_inc(S("f_abs"), 1)
            act.activation(ei[:, :, :], ei[:, :, :], ACT.Sign).then_inc(S("f_sign"), 1)
            act.activation(V("eps_out1"), V("eps_out1"), ACT.Sign).then_inc(S("f_sign"), 1)
            act.activation(V("eps_out2"), V("eps_out2"), ACT.Sign).then_inc(S("f_sign"), 1)
            act.wait_ge(S("f_abs"), 3)
            act.wait_ge(S("f_sign"), 3)
            act.activation(ea[:, :, :], ea[:, :, :], ACT.Sqrt).then_inc(S("f_sqrt"), 1)
            act.activation(V("eo1"), V("tmp0"), ACT.Sqrt).then_inc(S("f_sqrt"), 1)
            act.activation(V("eo2"), V("tmp1"), ACT.Sqrt).then_inc(S("f_sqrt"), 1)
            for u, (kind, srcs, dst, rows) in enumerate(turns):
                if u % 2 == 0:
                    act.wait_ge(S("turned"), u + 1)
                    act.copy(dst, bank[u % 4][:, 0:len(srcs) * rows].rearrange("p (a b) -> p a b", a=len(srcs))).then_inc(S("turned_act"), 1)
            act.wait_ge(S("wprod"), 1)
            act.copy(pq[:, :, :], bank[4][:, 0:2 * P].rearrange("p (a b) -> p a b", a=2)).then_inc(S("pq_ready"), 1)
            act.activation(V("bpn"), bank[4][:, 2 * P:2 * P + 1], ACT.Identity, bias=V("bp")).then_inc(S("pq_ready"), 1)
            for c in range(4):
                act.wait_ge(S("tok_m"), c + 1)
                act.activation(mish[:, 1, :], mish[:, 0, :], ACT.Exp).then_inc(S("tok_e"), 1)
            meet(act, "ln1")
            act.preload_act_table_set("natural_log_exp_and_others")
            if stop > 1:
                ln_act(act, "ln1")
            meet(act, "attn0")

            def attn0_step(t, r):
                if live(t, 0, B):
                    act.wait_ge(S("a_u_done"), t + 1)
                    reuse(act, S("a_s_done"), t, 2)
                    act.copy(a_u[:, r, :], bank[0][:, 0:N]).then_inc(S("a_u_ready"), 1)
                if live(t, 1, B):
                    q = (r - 1) % 2
                    act.wait_ge(S("a_m_ready"), t)
                    reuse(act, S("a_t_done"), t - 1, 2)
                    act.activation(a_e[:, q, 0, :], bank[1 + q][:, 0:N], ACT.Exp, bias=a_m[:, q, 0:1], scale=D ** -0.5, accum_out=a_m[:, q, 2:3])
                    act.activation(a_e[0:NTAIL, q, 1, :], bank[1 + q][0:NTAIL, N:2 * N], ACT.Exp, bias=a_m[0:NTAIL, q, 1:2], scale=D ** -0.5,
                                   accum_out=a_m[0:NTAIL, q, 3:4]).then_inc(S("a_e_ready"), 1)
                if live(t, 3, B):
                    act.wait_ge(S("a_v_done"), t - 2)
                    reuse(act, S("a_o_done"), t - 3, 2)
                    act.copy(a_v[:, (r - 3) % 2].rearrange("p m n -> p (m n)"), bank[7][:, 0:2 * P]).then_inc(S("a_v_ready"), 1)
            if stop > 2:
                run_steps(act, B, 3, attn0_step, 4)
            meet(act, "ln2")
            if stop > 3:
                ln_act(act, "ln2")
            meet(act, "ffn")
            if stop > 4:
                def gate_step(t, r):
                    act.wait_ge(S("gh_mm"), t + 1)
                    reuse(act, S("gh_sum"), t, 2)
                    act.activation(hbuf[:, r, 0:2, :].rearrange("p a n -> p (a n)"), bank[r][:, 0:GB], ACT.Relu, bias=V("gfc1_b")).then_inc(S("gh_done"), 1)
                run_steps(act, B // 2, 0, gate_step, 2)

                for w in range(2):
                    with act.Fori(4 * w, 4 * w + 4) as n:
                        for r in range(2):
                            for s in (0, 2):
                                act.wait_ge(S("mg_mm"), n * 8 + (4 * r + s + 1))
                                act.copy(merged_dst(w, n * 2 + (r - 8 * w), s),
                                         bank[4 * r + s].rearrange("p (g j b) -> p g j b", g=2, j=8)).then_inc(S("mg_act"), 1)
                act.wait_ge(S("bm_copied"), 1)
                act.wait_ge(S("mg_act"), 32)
                act.wait_ge(S("mg_dve"), 32)

                def ffn_step(t, r):
                    if live(t, 0, B):
                        reuse(act, S("f_mm"), t, 2)
                        act.copy(wst[:, r, 0:F], w1m[:, bass.ds(t, 1), 0:F].rearrange("p a f -> p (a f)")).then_inc(S("f_w1"), 1)
                    if live(t, 1, B):
                        q = (r - 1) % 2
                        act.wait_ge(S("f_mm"), t)
                        reuse(act, S("f_y"), t - 1, 2)
                        act.activation(hbuf[:, q, 0, :], bank[2 * q][:, 0:N], ACT.Relu, bias=merged_bias(t - 1, 0))
                        act.activation(hbuf[:, q, 1, :], bank[2 * q][:, N:2 * N], ACT.Relu, bias=merged_bias(t - 1, 1)).then_inc(S("f_h_act"), 1)
                run_steps(act, B, 1, ffn_step, 4)
            meet(act, "lnf")
            if stop > 5:
                ln_act(act, "lnf")
            meet(act, "lna")
            if stop > 6:
                ln_act(act, "lna")
            meet(act, "attn1")

            def attn1_step(t, r):
                if live(t, 0, B):
                    act.wait_ge(S("b_qk_done"), t + 1)
                    reuse3(act, S("b_s_done"), t)
                    act.activation(b_q[:, r, :], bank[0][:, 0:N], ACT.Identity, bias=V("bq")).then_inc(S("b_q_ready"), 1)
                    reuse(act, S("b_km_ready"), t, 2)
                    act.activation(b_k[:, r, :], bank[0][:, N:2 * N], ACT.Identity, bias=V("bk")).then_inc(S("b_k_ready"), 1)
                if live(t, 3, B):
                    act.wait_ge(S("b_t_done"), t - 2)
                    reuse(act, S("b_o_done"), t - 3, 2)
                    act.copy(b_et[:, (r - 3) % 2, 0:4, 0:P], bank[5].rearrange("p (h n) -> p h n", h=4)).then_inc(S("b_et_act"), 1)
                if live(t, 1, B):
                    q = (r - 1) % 2
                    reuse(act, S("b_t_done"), t - 1, 2)
                    for h in range(9):
                        if h % 3 == 0:
                            act.wait_ge(S("b_nm_ready"), (t - 1) * 3 + (h // 3 + 1))
                        rows = P if h < 8 else HT
                        ins = act.activation(b_e[0:rows, q, h, :], ps3a[0:rows, h // 3, (h % 3) * N:(h % 3) * N + N], ACT.Exp,
                                             bias=b_nm[0:rows, q, h:h + 1], accum_out=b_s[0:rows, q, h:h + 1])
                        if h % 3 == 2:
                            ins.then_inc(S("b_e_ready"), 1)
            if stop > 6:
                run_steps(act, B, 3, attn1_step, 4)
            meet(act, "lnm")
            if stop > 7:
                ln_act(act, "lnm")
            meet(act, "gate")
            if stop > 8:
                def route_step(t, r):
                    act.wait_ge(S("r_mm"), t + 1)
                    reuse(act, S("r_tr"), t, 2)
                    act.copy(m_sc[0:E, r, :], bank[r][0:E, 0:CH]).then_inc(S("r_sc"), 1)
                run_steps(act, NCH, 0, route_step, 2)
                act.wait_ge(S("top_ready"), 2)
                for k in range(2):
                    act.activation(m_1[k][0:SUB, :], m_1[k][0:SUB, :], ACT.Exp, scale=-1.0).then_inc(S("top_exp"), 1)
                for c in range(NCH):
                    act.wait_ge(S("ct_tr"), c + 1)
                    act.copy(m_ct[0:KC, c * CH:(c + 1) * CH], bank[4 + c % 4][0:KC, 0:CH]).then_inc(S("ct"), 1)
            meet(act, "moe")
            if stop > 8:
                act.sem_inc(S("cb_taken"), 1)

                def out_act(n):
                    act.wait_ge(S("m_tr"), n + 1)
                    act.wait_ge(S("stored"), n * 16)
                    act.copy(m_o[0:SUB], bank[7][0:SUB].rearrange("p (s d) -> p s d", s=NSUB)).then_inc(S("out_copied"), 1)

                def high_part(c, v):
                    act.wait_ge(S("m_prod"), c * UN + (v + 4))
                    act.wait_ge(S("m_y"), c * UN + (v + 1))
                    act.copy(m_hh[:, v % 3, :], m_hf[:, v % 3, :]).then_inc(S("m_hi"), 1)

                def chunk_act(c):
                    later = not is_known(c)
                    for v in range(UN):
                        s, cb = v % 3, v // 2
                        act.wait_ge(S("m_ab"), c * UN + (v + 1))
                        act.wait_ge(S("m_prod"), c * UN + (v + 1))
                        act.activation(m_a[:, s, :], bank[2 * s][:, 0:CH], ACT.Silu).then_inc(S("m_silu"), 1)
                        if v == 6 and later:
                            out_act(c)
                        if v % 2 == 1 and cb < E:
                            act.wait_ge(S("cb_mm"), c * E + (cb + 1))
                            act.wait_ge(S("cb_used"), c * E + (cb + 1))
                            act.copy(m_cb[:, cb % 2, :], bank[7][:, 0:CH]).then_inc(S("cb_taken"), 1)
                        if v >= 1:
                            high_part(c, v - 1)
                        elif later:
                            high_part(c - 1, UN - 1)
                chunk_act(0)
                with act.Fori(1, NCH) as c:
                    chunk_act(c)
                high_part(NCH - 1, UN - 1)
                out_act(NCH)

        @block.vector
        def _(dve):
            for i in range(8):
                dve.memset(bank[i], 0.0).then_inc(S("psum_zero"), 1)
            for t in range(2):
                dve.wait_ge(S(f"x_in{t}"), 16)
                dve.tensor_copy(xq[:, t].rearrange("p w (r c) -> p w r c", c=16), xp[:, t].rearrange("p r w c -> p w r c")).then_inc(S("xq_ready"), 1)
            dve.wait_ge(S("f_sqrt"), 3)
            dve.tensor_tensor(ei[:, :, :], ei[:, :, :], ea[:, :, :], ALU.mult).then_inc(S("n_f"), 1)
            dve.tensor_tensor(V("eo1"), V("eo1"), V("eps_out1"), ALU.mult).then_inc(S("n_f"), 1)
            dve.tensor_tensor(V("eo2"), V("eo2"), V("eps_out2"), ALU.mult).then_inc(S("n_f"), 1)
            dve.wait_ge(S("n_f"), 3)
            for k in range(2):
                dve.scalar_tensor_tensor(ea[:, k, :], ei[:, k, :], V(f"eo{k + 1}"), sw[:, k, :], ALU.mult, ALU.mult).then_inc(S("n_sw"), 1)
                dve.tensor_scalar(V(f"b{k + 1}n"), V(f"W{k + 1}_sb"), V(f"eo{k + 1}"), V(f"W{k + 1}_b"), ALU.mult, ALU.add).then_inc(S("n_b"), 1)
            dve.wait_ge(S("n_sw"), 2)
            for k in range(2):
                s0 = SLOT["n1a"] + 2 * k
                dve.tensor_tensor(wN[:, s0:s0 + 2, :], ea[:, k, :].rearrange("p (a c) -> p a c", a=2),
                                  wraw[:, k, :].rearrange("p (a c) -> p a c", a=2), ALU.add).then_inc(S("noisy"), 1)
            for u, (kind, srcs, dst, rows) in enumerate(turns):
                if u % 2 == 1:
                    dve.wait_ge(S("turned"), u + 1)
                    dve.tensor_copy(dst, bank[u % 4][0:dst.shape[0], 0:len(srcs) * rows].rearrange("p (a b) -> p a b", a=len(srcs))).then_inc(S("turned_dve"), 1)
            dve.wait_ge(S("turned_dve"), len(turns) // 2)
            dve.tensor_scalar(W("Wp"), W("Wp"), D ** -0.5, None, ALU.mult).then_inc(S("wp_scaled"), 1)
            dve.wait_ge(S("turned_act"), len(turns) // 2)
            for k, (v, n) in enumerate((("ln_g", "lng"), ("ln_b", "lnb"))):
                dve.tensor_scalar(tvln[:, k, :], W("tvg" if k == 0 else "tvs")[:, 0:E], V(v), None, ALU.subtract).then_inc(S("ln_d"), 1)
                dve.wait_ge(S("ln_d"), 3 * k + 1)
                dve.tensor_reduce(V(n), tvln[:, k, :], AX, ALU.add).then_inc(S("ln_d"), 1)
                dve.wait_ge(S("ln_d"), 3 * k + 2)
                dve.tensor_scalar(V(n), V(n), LN_MERGE, V(v), ALU.mult, ALU.add).then_inc(S("ln_d"), 1)
            dve.wait_ge(S("n_b"), 2)
            for c in range(4):
                dve.wait_ge(S("tok_g"), c + 1)
                dve.tensor_scalar(mish[:, 0, :], bank[0], V("b1n"), 30.0, ALU.add, ALU.min).then_inc(S("tok_m"), 1)
                dve.tensor_scalar(mish[:, 2, :], bank[0], V("b1n"), None, ALU.add).then_inc(S("tok_gb"), 1)
                dve.wait_ge(S("tok_e"), c + 1)
                dve.scalar_tensor_tensor(mish[:, 3, :], mish[:, 1, :], 2.0, mish[:, 1, :], ALU.add, ALU.mult).then_inc(S("tok_n"), 1)
                dve.wait_ge(S("tok_n"), c + 1)
                dve.tensor_scalar(mish[:, 4, :], mish[:, 3, :], 2.0, None, ALU.add).then_inc(S("tok_d"), 1)
                dve.wait_ge(S("tok_d"), c + 1)
                dve.reciprocal(mish[:, 5, :], mish[:, 4, :]).then_inc(S("tok_r"), 1)
                dve.wait_ge(S("tok_gb"), c + 1)
                dve.tensor_tensor(mish[:, 2, :], mish[:, 2, :], mish[:, 3, :], ALU.mult).then_inc(S("tok_p"), 1)
                dve.wait_ge(S("tok_p"), c + 1)
                dve.wait_ge(S("tok_r"), c + 1)
                dve.tensor_tensor(mish[:, 3, :], mish[:, 2, :], mish[:, 5, :], ALU.mult).then_inc(S("tok_q"), 1)
                dve.wait_ge(S("tok_q"), c + 1)
                if c >= 2:
                    dve.wait_ge(S("tok_y"), c - 1)
                dve.scalar_tensor_tensor(tokx[:, c % 2, :], bank[1], V("b2n"), mish[:, 3, :], ALU.add, ALU.mult).then_inc(S("tok_x"), 1)
                dve.wait_ge(S("tok_y"), c + 1)
                dve.scalar_tensor_tensor(hT[:, 8 * c * N:(8 * c + 8) * N].rearrange("p (b n) -> p b n", n=N)[:, :, 0:NP_],
                                         bank[2 + c % 2].rearrange("p (b n) -> p b n", n=NP_), V("W3_b"),
                                         C("pos").unsqueeze(1).to_broadcast([P, 8, NP_]), ALU.add, ALU.add).then_inc(S("tok_h"), 1)
            meet(dve, "ln1")
            if stop > 1:
                ln_dve(dve, "ln1")
            meet(dve, "attn0")

            def attn0_step(t, r):
                if live(t, 2, B):
                    dve.wait_ge(S("a_e_ready"), t - 1)
                    dve.reciprocal(a_m[:, r, 4:5], a_m[:, r, 2:3]).then_inc(S("a_r"), 1)
                    dve.reciprocal(a_m[0:NTAIL, r, 5:6], a_m[0:NTAIL, r, 3:4]).then_inc(S("a_rt"), 1)
                    dve.wait_ge(S("a_r"), t - 1)
                    dve.tensor_scalar(a_e[:, r, 0, :], a_e[:, r, 0, :], a_m[:, r, 4:5], None, ALU.mult)
                    dve.wait_ge(S("a_rt"), t - 1)
                    dve.tensor_scalar(a_e[0:NTAIL, r, 1, :], a_e[0:NTAIL, r, 1, :], a_m[0:NTAIL, r, 5:6], None, ALU.mult).then_inc(S("a_a_ready"), 1)
                if live(t, 1, B):
                    q = (r - 1) % 2
                    dve.wait_ge(S("a_s_done"), t)
                    reuse(dve, S("a_e_ready"), t - 1, 2)
                    dve.tensor_reduce(a_m[:, q, 0:2], bank[1 + q][:, 0:2 * N].rearrange("p (a n) -> p a n", a=2), AX, ALU.max, negate=True).then_inc(S("a_mx"), 1)
                    dve.wait_ge(S("a_mx"), t)
                    dve.tensor_scalar(a_m[:, q, 0:2], a_m[:, q, 0:2], D ** -0.5, None, ALU.mult).then_inc(S("a_m_ready"), 1)
                if live(t, 3, B):
                    q = (r - 3) % 2
                    dve.wait_ge(S("a_t_done"), t - 2)
                    reuse(dve, S("a_o_done"), t - 3, 2)
                    dve.tensor_copy(a_t[:, q].rearrange("p m n -> p (m n)"), bank[5 + q][:, 0:2 * N]).then_inc(S("a_t_ready"), 1)
                if live(t, 4, B):
                    dve.wait_ge(S("a_o_done"), t - 3)
                    dve.scalar_tensor_tensor(sample(hT, t - 4), bank[3 + r][:, 0:N], V("b_proj"), sample(hT, t - 4), ALU.add, ALU.add).then_inc(S("a_h"), 1)
            if stop > 2:
                run_steps(dve, B, 4, attn0_step, 6)
            meet(dve, "ln2")
            if stop > 3:
                ln_dve(dve, "ln2")
            meet(dve, "ffn")
            if stop > 4:
                def gate_step(t, r):
                    dve.wait_ge(S("gh_done"), t + 1)
                    dve.tensor_reduce(ghm[:, bass.ds(t * 2, 2)], hbuf[:, r, 0:2, :], AX, ALU.add).then_inc(S("gh_sum"), 1)
                run_steps(dve, B // 2, 0, gate_step, 2)
                dve.wait_ge(S("g9_in"), 16)
                dve.wait_ge(S("g_mm"), 1)
                dve.memset(g9[:, 0:B], 1.0).then_inc(S("g9_ready"), 1)
                dve.wait_ge(S("g9_ready"), 1)
                dve.tensor_scalar(g9[0:E, 0:B], bank[2][0:E, 0:B], 1.0 / N, g9[0:E, B:B + 1], ALU.mult, ALU.add).then_inc(S("g9_ready"), 1)
                dve.wait_ge(S("grep_mm"), 1)
                dve.tensor_copy(gcol[:, :], bank[3][0:72, 0:B]).then_inc(S("gcol_ready"), 1)
                dve.wait_ge(S("gcol_ready"), 1)
                dve.tensor_tensor(gblk[0:72, :, :], gcol[:, :].unsqueeze(1).to_broadcast([72, 8, B]),
                                  C("jmask", 72).unsqueeze(2).to_broadcast([72, 8, B]), ALU.mult).then_inc(S("gblk_ready"), 1)
                dve.wait_ge(S("bm_mm"), 1)
                dve.tensor_copy(w1m[:, :, F:F + 5].rearrange("p b k -> p k b"), bank[4][:, 0:5 * B].rearrange("p (k b) -> p k b", k=5)).then_inc(S("bm_copied"), 1)
                for w in range(2):
                    with dve.Fori(4 * w, 4 * w + 4) as n:
                        for r in range(2):
                            for s in (1, 3):
                                dve.wait_ge(S("mg_mm"), n * 8 + (4 * r + s + 1))
                                dve.tensor_copy(merged_dst(w, n * 2 + (r - 8 * w), s),
                                                bank[4 * r + s].rearrange("p (g j b) -> p g j b", g=2, j=8)).then_inc(S("mg_dve"), 1)
                dve.wait_ge(S("mg_dve"), 32)
                dve.wait_ge(S("mg_act"), 32)

                def ffn_step(t, r):
                    if live(t, 0, B):
                        dve.wait_ge(S("f_mm"), t + 1)
                        reuse(dve, S("f_y"), t, 2)
                        for k in (2, 3):
                            ins = dve.tensor_scalar(hbuf[:, r, k, :], bank[2 * r + 1][:, (k - 2) * N:(k - 1) * N], merged_bias(t, k), 0.0, ALU.add, ALU.max)
                        ins.then_inc(S("f_h_dve"), 1)
                    if live(t, 1, B):
                        q = (r - 1) % 2
                        dve.wait_ge(S("f_y"), t)
                        dve.scalar_tensor_tensor(sample(xn, t - 1), bank[4 + q][:, 0:N], merged_bias(t - 1, 4), sample(xn, t - 1), ALU.add, ALU.add).then_inc(S("f_res"), 1)
                run_steps(dve, B, 1, ffn_step, 4)
            meet(dve, "lnf")
            if stop > 5:
                ln_dve(dve, "lnf")
            meet(dve, "lna")
            dve.wait_ge(S("moe_in"), 16 * 8)
            for k in range(3):
                step = (E + 1) * HID
                dve.tensor_copy(wparts[:, 0, k * step:(k + 1) * step], wraw_e[:, k * step:(k + 1) * step]).then_inc(S("w_high"), 1)
            if stop > 6:
                ln_dve(dve, "lna")
            meet(dve, "attn1")

            def attn1_step(t, r):
                q = (r - 1) % 2
                if live(t, 2, B):
                    dve.wait_ge(S("b_e_ready"), t * 3 - 3)
                    dve.reciprocal(b_r[:, r, 0:8], b_s[:, r, 0:8]).then_inc(S("b_r1"), 1)
                    dve.reciprocal(b_r[0:HT, r, 8:9], b_s[0:HT, r, 8:9]).then_inc(S("b_r2"), 1)
                    dve.wait_ge(S("b_r1"), t - 1)
                    dve.tensor_tensor(b_ek[:, r, :].rearrange("p (h n) -> p h n", h=H), b_e[:, r, 0:8, P:N], b_r[:, r, 0:8].unsqueeze(2).to_broadcast([P, H, NTAIL]), ALU.mult)
                    dve.tensor_tensor(b_e[:, r, 0:8, 0:P], b_e[:, r, 0:8, 0:P], b_r[:, r, 0:8].unsqueeze(2).to_broadcast([P, H, P]), ALU.mult)
                    dve.wait_ge(S("b_r2"), t - 1)
                    dve.tensor_scalar(b_e[0:HT, r, 8, :], b_e[0:HT, r, 8, :], b_r[0:HT, r, 8:9], None, ALU.mult).then_inc(S("b_en_ready"), 1)
                    dve.wait_ge(S("b_en_ready"), t - 1)
                    dve.tensor_tensor(b_tt[0:HT, r, :].rearrange("p (h n) -> p h n", h=H), b_e[0:HT, r, 8, P:N].unsqueeze(1).to_broadcast([HT, H, NTAIL]),
                                      C("tmask", HT).rearrange("p (h n) -> p h n", h=H), ALU.mult).then_inc(S("b_tt_ready"), 1)
                if live(t, 4, B):
                    dve.wait_ge(S("b_y_done"), t - 3)
                    dve.scalar_tensor_tensor(sample(hT, t - 4), bank[1][:, 256:256 + N], V("bpn"), sample(hT, t - 4), ALU.add, ALU.add).then_inc(S("b_h"), 1)
                if live(t, 3, B):
                    dve.wait_ge(S("b_t_done"), t - 2)
                    reuse(dve, S("b_o_done"), t - 3, 2)
                    dve.tensor_copy(b_et[:, q, 4:8, 0:P], bank[6].rearrange("p (h n) -> p h n", h=4))
                    dve.tensor_copy(b_et[:, q, :, P:N], bank[7][:, 0:HT].rearrange("p (h n) -> p h n", h=H))
                    dve.tensor_copy(b_ett[0:HT, q, :], bank[7][0:HT, HT:HT + N]).then_inc(S("b_et_dve"), 1)
                if live(t, 2, B):
                    dve.wait_ge(S("b_v_done"), t - 1)
                    reuse(dve, S("b_o_done"), t - 2, 2)
                    dve.tensor_copy(diagonal(b_v, r), bank[0][:, 0:P].rearrange("p (h d) -> p h d", h=H))
                    dve.tensor_tensor(b_vt[0:HT, r, :], bank[0][0:HT, P:2 * P], C("vmask", HT), ALU.mult).then_inc(S("b_vm_ready"), 1)
                if live(t, 1, B):
                    for g in range(3):
                        dve.wait_ge(S("b_s_done"), (t - 1) * 3 + (g + 1))
                        dve.tensor_reduce(b_nm[:, q, 3 * g:3 * g + 3], ps3a[:, g, 0:3 * N].rearrange("p (h n) -> p h n", h=3), AX, ALU.max, negate=True).then_inc(S("b_nm_ready"), 1)
                if live(t, 0, B):
                    dve.wait_ge(S("b_q_ready"), t + 1)
                    reuse3(dve, S("b_s_done"), t)
                    dve.tensor_tensor(b_qm[:, r], b_q[:, r, P:N].unsqueeze(1).to_broadcast([P, H, NTAIL]),
                                      C("hmask").unsqueeze(2).to_broadcast([P, H, NTAIL]), ALU.mult).then_inc(S("b_qm_ready"), 1)
                if live(t, 3, B):
                    dve.wait_ge(S("b_o_done"), t - 2)
                    reuse(dve, S("b_y_done"), t - 3, 2)
                    dve.tensor_copy(b_o[:, q, :], bank[1][:, 0:N]).then_inc(S("b_o_ready"), 1)
            if stop > 6:
                dve.wait_ge(S("b_v_zero"), 1)
                run_steps(dve, B, 4, attn1_step, 6)
            meet(dve, "lnm")
            if stop > 7:
                ln_dve(dve, "lnm")
            meet(dve, "gate")
            if stop > 8:
                dve.wait_ge(S("bias_in"), 16)

                def route_step(t, r):
                    dve.wait_ge(S("r_tr"), t + 1)
                    dve.tensor_copy(m_s[0:SUB, bass.ds(t * NSUB, NSUB), :], bank[2 + r][0:SUB, 0:NSUB * E].rearrange("p (s e) -> p s e", e=E)).then_inc(S("r_s"), 1)
                run_steps(dve, NCH, 0, route_step, 2)
                dve.wait_ge(S("r_s"), NCH)
                dve.tensor_copy(selr[0:KC, :], C("select", KC))
                count = [0]

                def chain(ins):
                    count[0] += 1
                    ins.then_inc(S("router"), 1)
                    dve.wait_ge(S("router"), count[0])
                SB = NCH * NSUB
                s_, b_, one1, one2, tmp = m_s[0:SUB], m_t[0][0:SUB], m_t[1][0:SUB], m_t[2][0:SUB], m_t[3][0:SUB]
                mx = m_1[4][0:SUB, :]

                def wide(v):
                    return v.unsqueeze(2).to_broadcast([SUB, SB, E])

                def narrow(v):
                    return v.unsqueeze(1).to_broadcast([SUB, SB, E])

                def first_best(onehot, val):
                    chain(dve.tensor_reduce(mx, val, AX, ALU.max))
                    chain(dve.tensor_tensor(onehot, val, wide(mx), ALU.is_equal))
                    chain(dve.tensor_tensor(onehot, onehot, narrow(C("rank", SUB)), ALU.mult))
                    chain(dve.tensor_reduce(m_1[3][0:SUB, :], onehot, AX, ALU.max))
                    chain(dve.tensor_tensor(onehot, narrow(C("rank", SUB)), wide(m_1[3][0:SUB, :]), ALU.is_equal))

                def without(dst, val, onehot):
                    chain(dve.scalar_tensor_tensor(dst, onehot, -BIG, val, ALU.mult, ALU.add))
                first_best(one1, s_)
                chain(dve.tensor_copy(m_1[0][0:SUB, :], mx))
                without(tmp, s_, one1)
                chain(dve.tensor_reduce(m_1[1][0:SUB, :], tmp, AX, ALU.max))
                dve.sem_inc(S("top_ready"), 2)
                chain(dve.tensor_tensor(b_, s_, narrow(m_bias[0:SUB, :]), ALU.add))
                first_best(one1, b_)
                without(tmp, b_, one1)
                first_best(one2, tmp)
                dve.wait_ge(S("top_exp"), 2)
                for k in range(2):
                    chain(dve.tensor_scalar(m_1[k][0:SUB, :], m_1[k][0:SUB, :], 1.0, None, ALU.add))
                    chain(dve.reciprocal(m_1[k][0:SUB, :], m_1[k][0:SUB, :]))
                chain(dve.tensor_tensor(m_1[2][0:SUB, :], m_1[0][0:SUB, :], m_1[1][0:SUB, :], ALU.add))
                chain(dve.reciprocal(m_1[2][0:SUB, :], m_1[2][0:SUB, :]))
                for k, onehot in enumerate((one1, one2)):
                    chain(dve.tensor_tensor(m_1[k][0:SUB, :], m_1[k][0:SUB, :], m_1[2][0:SUB, :], ALU.mult))
                    chain(dve.tensor_tensor(onehot, onehot, wide(m_1[k][0:SUB, :]), ALU.mult))
                chain(dve.tensor_tensor(tmp, one1, one2, ALU.add))
                dve.wait_ge(S("c40_zero"), 1)
                chi = m_chi[0:SUB]
                chain(dve.tensor_copy(chi, tmp))
                chain(dve.tensor_copy(m_c40[0:SUB, :, 0:E], chi.bitcast(F32)))
                chain(dve.tensor_tensor(m_c40[0:SUB, :, 32:32 + E], tmp, chi.bitcast(F32), ALU.subtract))
                dve.sem_inc(S("comb"), 1)
            meet(dve, "moe")
            if stop > 8:
                dve.sem_inc(S("m_prod"), 3)
                dve.sem_inc(S("m_f"), 1)
                dve.sem_inc(S("cb_used"), 2)

                def finish(n):
                    dve.wait_ge(S("m_y"), n * UN + 3)
                    dve.wait_ge(S("m_tr"), n)
                    dve.tensor_tensor(m_f[:, :], bank[6][:, 0:CH], hT[:, bass.ds((n - 1) * CH, CH)], ALU.add).then_inc(S("m_f"), 1)

                def chunk_dve(c):
                    for v in range(UN):
                        s, e = v % 3, ORDER[v // 2]
                        if v == 3 and not is_known(c):
                            finish(c)
                        dve.wait_ge(S("m_silu"), c * UN + (v + 1))
                        src = m_a[:, s, :]
                        if e < E:
                            if v % 2 == 0:
                                dve.wait_ge(S("cb_taken"), c * E + (e + 2))
                            used_up = "cb_used" if v % 2 == 1 else "cb_half"
                            dve.tensor_tensor(m_g[:, s, :], src, m_cb[:, e % 2, :], ALU.mult).then_inc(S(used_up), 1)
                            dve.wait_ge(S(used_up), c * E + (e + 1 + (2 if v % 2 == 1 else 0)))
                            src = m_g[:, s, :]
                        dve.wait_ge(S("m_lo"), c * UN + (v + 1))
                        dve.tensor_tensor(m_hf[:, s, :], bank[2 * s + 1][:, 0:CH], src, ALU.mult).then_inc(S("m_prod"), 1)
                chunk_dve(0)
                with dve.Fori(1, NCH) as c:
                    chunk_dve(c)
                finish(NCH)


def diagonal(values, r):
    v = values[:, r].rearrange("p h n -> p (h n)")
    return bass.AP(v.tensor, v.offset, [v.ap[0], [P + HD, H], [1, HD]])


_INS = ['x', 'txt', 'L0_tok_W1_w', 'L0_tok_W1_b', 'L0_tok_W1_sw', 'L0_tok_W1_sb', 'L0_tok_W2_w', 'L0_tok_W2_b', 'L0_tok_W2_sw', 'L0_tok_W2_sb', 'L0_tok_W3_w', 'L0_tok_W3_b', 'L0_tok_eps_in1', 'L0_tok_eps_out1', 'L0_tok_eps_in2', 'L0_tok_eps_out2', 'L0_attn_w_qkv', 'L0_attn_w_proj', 'L0_attn_b_proj', 'L0_ffn_gfc1_w', 'L0_ffn_gfc1_b', 'L0_ffn_gfc2_w', 'L0_ffn_gfc2_b', 'L0_ffn_W1', 'L0_ffn_b1', 'L0_ffn_W2', 'L0_ffn_b2', 'L0_ffn_ln_g', 'L0_ffn_ln_b', 'L0_ffn_tv_W1', 'L0_ffn_tv_b1', 'L0_ffn_tv_W2', 'L0_ffn_tv_b2', 'L0_ffn_tv_ln_g', 'L0_ffn_tv_ln_b', 'L1_attn_Wq', 'L1_attn_bq', 'L1_attn_Wk', 'L1_attn_bk', 'L1_attn_Wv', 'L1_attn_bv', 'L1_attn_Wp', 'L1_attn_bp', 'L1_ffn_gate_w', 'L1_ffn_biases', 'L1_ffn_w1', 'L1_ffn_w3', 'L1_ffn_w2', 'L1_ffn_sw1', 'L1_ffn_sw3', 'L1_ffn_sw2']


def shape_constants(np):
    c = np.zeros((P, NCONST), np.float32)

    def put(name, a):
        at, n = CONST[name]
        c[0:a.shape[0], at:at + n] = a
    p = np.arange(P)
    put("ident", np.eye(P))
    put("centre", np.eye(P) - 1.0 / P)
    put("average", np.full((P, P), 1.0 / P))
    pos = np.arange(NP_, dtype=np.float32)[:, None]
    div = np.exp(np.arange(0, D, 2, dtype=np.float32) * np.float32(-np.log(10000.0) / D))
    ang = pos * div
    put("pos", np.stack([np.sin(ang), np.cos(ang)], axis=-1).reshape(NP_, D).T)
    put("jmask", (np.arange(72)[:, None] % 8 == np.arange(8)[None]))
    put("hmask", p[:, None] // HD == np.arange(H)[None])
    ht = np.arange(HT)
    put("vmask", ht[:, None] // NTAIL == p[None] // HD)
    put("tmask", ht[:, None] // NTAIL == ht[None] // NTAIL)
    put("dsel", ht[:, None] % NTAIL == np.arange(NTAIL)[None])
    put("rep", np.arange(E + 1)[:, None] == np.arange(72)[None] // 8)
    row = np.arange(KC)[:, None]
    put("select", ((row < E) | (row >= 32)) & (row % 32 == np.arange(E * P)[None] // P))
    put("rank", np.broadcast_to(E - np.arange(E), (P, E)))
    return c


def build(nc, args, const, out, stop=99):
    def group(prefix):
        return {n[len(prefix):]: a for n, a in args.items() if n.startswith(prefix)}
    early_fusion(nc, args["x"], args["txt"], group("L0_tok_"), group("L0_attn_"), group("L0_ffn_"),
                 group("L1_attn_"), group("L1_ffn_"), const, out, stop)


def kernel(**inputs):
    import numpy as _np
    import concourse.bacc as _bacc
    from concourse import mybir as _mybir
    from concourse.bass_utils import run_bass_kernel_spmd as _run

    nc = _bacc.Bacc("TRN2", target_bir_lowering=False, num_devices=1)
    arrays, args = {}, {}
    for name in _INS:
        a = _np.ascontiguousarray(inputs[name])
        arrays[f"in_{name}_dram"] = a
        args[name] = nc.dram_tensor(f"in_{name}_dram", a.shape, _mybir.dt.from_np(a.dtype), kind="ExternalInput").ap()
    arrays["shape_constants"] = shape_constants(_np)
    const = nc.dram_tensor("shape_constants", (P, NCONST), F32, kind="ExternalInput").ap()
    out = nc.dram_tensor("out_0_dram", (B, N, D), F32, kind="ExternalOutput").ap()
    build(nc, args, const, out)
    r = _run(nc, [arrays], core_ids=[0])
    return r.results[0]["out_0_dram"]
```

```python
from contextlib import ExitStack

import concourse.bass as bass
from concourse import mybir

P = 128
B, NP_, NT, D = 32, 64, 77, 128
N = NP_ + NT
T = B * N
NTAIL = N - P
CH = 376
NCH = T // CH
SUB = 94
NSUB = CH // SUB
H, HD = 8, 16
KC = 40
HT = H * NTAIL
E = 8
F = 512
HID = 256
FW = F + 5
GB = 2 * N
LN_EPS = 1e-5
LN_MERGE = 0.03
BIG = 3.0e38

ALU = mybir.AluOpType
ACT = mybir.ActivationFunctionType
AX = mybir.AxisListType.X
F32 = mybir.dt.float32
F32R = mybir.dt.float32r

CONST = {}
_at = 0
for _name, _n in (("ident", 128), ("centre", 128), ("average", 128), ("pos", NP_), ("jmask", 8),
                  ("hmask", H), ("vmask", 128), ("tmask", HT), ("dsel", NTAIL), ("rep", 72),
                  ("rank", E), ("select", E * 128)):
    CONST[_name] = (_at, _n)
    _at += _n
NCONST = _at

VECS = ["W1_b", "W1_sb", "W2_b", "W2_sb", "eps_out1", "eps_out2", "W3_b", "b_proj", "gfc1_b",
        "ln_g", "ln_b", "bq", "bk", "bv", "bp", "b1n", "b2n", "eo1", "eo2", "lng", "lnb", "bpn",
        "eps", "tmp0", "tmp1"]
VEC = {n: i for i, n in enumerate(VECS)}

SLOT = {n: i for i, n in enumerate(["W3", "gfc1", "proj", "v0", "Wq", "Wk", "Wv", "Wp",
                                    "n1a", "n1b", "n2a", "n2b", "gfc2", "gate", "tvg", "tvs"])}

UN = 2 * (E + 1)
ORDER = [E] + list(range(E))
MEETINGS = ["ln1", "lnf"]
NORMS = ["ln1", "ln2", "lnf", "lna", "lnm"]


def is_known(u):
    return isinstance(u, int)


def reuse(eng, sem, u, depth):
    if is_known(u):
        if u >= depth:
            eng.wait_ge(sem, u - depth + 1)
    else:
        eng.wait_ge(sem, u - depth + 1)


def reuse3(eng, sem, u):
    if not is_known(u) or u >= 2:
        eng.wait_ge(sem, u * 3 - 3)


def run_steps(eng, units, lag, body, head):
    total = units + lag
    rounds = (units - head) // 2
    for t in range(head):
        body(t, t % 2)
    with eng.Fori(0, rounds) as i:
        for r in range(2):
            body(i * 2 + (head + r), r)
    for t in range(head + 2 * rounds, total):
        body(t, t % 2)


def live(t, k, units):
    return not is_known(t) or 0 <= t - k < units


def early_fusion(nc, x, txt, tok, attn0, ffn, attn1, moe, const, out):
    with ExitStack() as ctx:
        def sb(name, shape, dt=F32, scope=None):
            return (scope or ctx).enter_context(nc.sbuf_tensor(name, shape, dt))

        sems = {}

        def S(name):
            if name not in sems:
                sems[name] = ctx.enter_context(nc.semaphore(name))
            return sems[name]

        ps = [ctx.enter_context(nc.psum_tensor(f"ps{i}", [P, 512], F32)) for i in range(2)]
        ps3a = ctx.enter_context(nc.psum_tensor("ps3a", [P, 3, 512], F32))
        ps3b = ctx.enter_context(nc.psum_tensor("ps3b", [P, 3, 512], F32))
        bank = [ps[0][:, :], ps[1][:, :]] + [ps3a[:, i, :] for i in range(3)] + [ps3b[:, i, :] for i in range(3)]

        hT = sb("hT", [P, T])
        xn = sb("xn", [P, T])
        cst = sb("cst", [P, NCONST])
        vec = sb("vec", [P, len(VECS)])
        wT = sb("wT", [P, len(SLOT), P])
        pq = sb("pq", [P, 2, P])
        early = ctx.enter_context(ExitStack())
        arena = sb("arena", [P, B * FW + B * F], scope=early)

        def C(name, rows=P):
            a, n = CONST[name]
            return cst[0:rows, a:a + n]

        def V(name, rows=P):
            return vec[0:rows, VEC[name]:VEC[name] + 1]

        def W(name):
            return wT[:, SLOT[name], :]

        used = [0]

        def take(n):
            a = used[0]
            used[0] += n
            assert used[0] <= arena.shape[1], used[0]
            return arena[:, a:a + n]

        ident = C("ident")

        xp = take(2 * 2048).rearrange("p (t r w c) -> p t r w c", t=2, r=16, w=8)
        xq = take(2 * 2048).rearrange("p (t w n) -> p t w n", t=2, w=8)
        xT = take(2 * 2048).rearrange("p (k n) -> p k n", k=2)
        wN = take(len(SLOT) * P).rearrange("p (s c) -> p s c", s=len(SLOT))
        wqk = take(2 * P).rearrange("p (s c) -> p s c", s=2)
        txn = take(B * D).rearrange("p (b d) -> p b d", b=B)
        sw = take(2 * 256).rearrange("p (k n) -> p k n", k=2)
        wraw = take(2 * 256).rearrange("p (k n) -> p k n", k=2)
        ei = take(2 * 256).rearrange("p (k n) -> p k n", k=2)
        ea = take(2 * 256).rearrange("p (k n) -> p k n", k=2)
        mish = take(2 * 5 * 512).rearrange("p (a k n) -> p a k n", a=2, k=5)
        tokx = take(2 * 512).rearrange("p (k n) -> p k n", k=2)
        tvln = sb("tvln", [P, 2, E], scope=early)
        used[0] = 0
        a_u = take(2 * N).rearrange("p (k n) -> p k n", k=2)
        a_x = take(2 * N).rearrange("p (k n) -> p k n", k=2)
        a_v = take(2 * 2 * P).rearrange("p (k m n) -> p k m n", k=2, m=2)
        a_e = take(2 * 2 * N).rearrange("p (k m n) -> p k m n", k=2, m=2)
        a_t = take(2 * 2 * N).rearrange("p (k m n) -> p k m n", k=2, m=2)
        a_m = take(2 * 6).rearrange("p (k m) -> p k m", k=2)
        used[0] = 0
        w1m = take(B * FW).rearrange("p (b f) -> p b f", b=B)
        w2m = take(B * F).rearrange("p (b f) -> p b f", b=B)
        tvc = sb("tvc", [P, 2, 1024], scope=early)
        tvb = sb("tvb", [E + 1, F + D], scope=early)
        g9 = sb("g9", [E + 1, B + 1], scope=early)
        gblk = sb("gblk", [P, 8, B], scope=early)
        gcol = sb("gcol", [72, B], scope=early)
        ghm = sb("ghm", [P, B], scope=early)
        merging = ctx.enter_context(ExitStack())
        mg_high = sb("mg_high", [P, 4, 256], F32R, scope=merging)
        mg_low = sb("mg_low", [P, 4, 256], F32R, scope=merging)
        gb_high = sb("gb_high", [P, 8 * B], F32R, scope=merging)
        gb_low = sb("gb_low", [P, 8 * B], F32R, scope=merging)
        merging.close()
        wst = sb("wst", [P, 2, 2 * F], scope=early)
        hbuf = sb("hbuf", [P, 2, 4, N], scope=early)
        ln_early = wst[:, :, :].rearrange("p k n -> p (k n)")[:, 0:4 * CH].rearrange("p (k n) -> p k n", k=4)
        early.close()

        wparts = sb("wparts", [P, 2, 3 * (E + 1) * HID], F32R)
        ln_late = sb("ln_late", [P, 4, CH])
        middle = ctx.enter_context(ExitStack())
        wraw_e = sb("wraw_e", [P, 3 * (E + 1) * HID], scope=middle)
        m_w1, m_w3, m_w2 = (wraw_e[:, i * (E + 1) * HID:(i + 1) * (E + 1) * HID] for i in range(3))
        m_w1 = m_w1.rearrange("p (e h) -> p e h", e=E + 1)
        m_w3 = m_w3.rearrange("p (e h) -> p e h", e=E + 1)
        m_w2 = m_w2.rearrange("p (e k d) -> p e k d", e=E + 1, k=2)
        arena = sb("arena1", [P, 13000], scope=middle)
        used[0] = 0
        b_x = take(2 * N).rearrange("p (k n) -> p k n", k=2)
        b_xt = take(2 * HT).rearrange("p (k n) -> p k n", k=2)
        b_ek = take(2 * HT).rearrange("p (k n) -> p k n", k=2)
        b_q = take(2 * N).rearrange("p (k n) -> p k n", k=2)
        b_k = take(2 * N).rearrange("p (k n) -> p k n", k=2)
        b_km = take(2 * H * N).rearrange("p (k h n) -> p k h n", k=2, h=H)
        b_qm = take(2 * HT).rearrange("p (k h n) -> p k h n", k=2, h=H)
        b_v = take(2 * H * P).rearrange("p (k h n) -> p k h n", k=2, h=H)
        b_vt = take(2 * P).rearrange("p (k n) -> p k n", k=2)
        b_nm = take(2 * 9).rearrange("p (k h) -> p k h", k=2)
        b_s = take(2 * 9).rearrange("p (k h) -> p k h", k=2)
        b_r = take(2 * 9).rearrange("p (k h) -> p k h", k=2)
        b_e = take(2 * 9 * N).rearrange("p (k h n) -> p k h n", k=2, h=9)
        b_tt = take(2 * HT).rearrange("p (k n) -> p k n", k=2)
        b_et = take(2 * H * N).rearrange("p (k h n) -> p k h n", k=2, h=H)
        b_ett = take(2 * N).rearrange("p (k n) -> p k n", k=2)
        b_o = take(2 * N).rearrange("p (k n) -> p k n", k=2)
        middle.close()

        xh = sb("xh", [P, T], F32R)
        xl = sb("xl", [P, T], F32R)
        m_ct = sb("m_ct", [P, T], F32R)
        selr = sb("selr", [P, E * P], F32R)
        m_bias = sb("m_bias", [P, E])
        router = ctx.enter_context(ExitStack())
        m_sc = sb("m_sc", [P, 2, CH], scope=router)
        m_s = sb("m_s", [P, NCH * NSUB, E], scope=router)
        m_t = [sb(f"m_t{i}", [P, NCH * NSUB, E], scope=router) for i in range(4)]
        m_1 = [sb(f"m_1{i}", [P, NCH * NSUB], scope=router) for i in range(5)]
        m_p = [sb(f"m_p{i}", [P, NCH * NSUB, E], scope=router) for i in range(3)]
        m_chi = sb("m_chi", [P, NCH * NSUB, E], F32R, scope=router)
        m_c40 = sb("m_c40", [P, NCH * NSUB, KC], scope=router)
        router.close()
        m_cb = sb("m_cb", [P, 2, CH])
        m_a = sb("m_a", [P, 3, CH])
        m_g = sb("m_g", [P, 3, CH])
        m_hf = sb("m_hf", [P, 3, CH])
        m_hh = sb("m_hh", [P, 3, CH], F32R)
        m_hl = sb("m_hl", [P, 3, CH], F32R)
        m_f = sb("m_f", [P, CH])
        m_o = sb("m_o", [P, NSUB, D])

        def expert(part, kind, e, k):
            at = (kind * (E + 1) + e) * HID + k * P
            return wparts[:, part, at:at + P]

        def chunk(buf, c, n=CH):
            return buf[:, bass.ds(c * n, n)]

        def sample(buf, b):
            return buf[:, bass.ds(b * N, N)]

        def meet(eng, phase):
            eng.drain().then_inc(S("engines_met"), 1)
            eng.wait_ge(S("engines_met"), 5 * (MEETINGS.index(phase) + 1))

        def normed(eng, name, chunks):
            eng.wait_ge(S("ln_out"), NCH * NORMS.index(name) + chunks)

        def merged_dst(w, c, s):
            if w == 0:
                return w1m[:, :, 0:F].rearrange("p b (j g) -> p g j b", j=8)[:, bass.ds(c * 8 + 2 * s, 2)]
            v = w2m[:, :, :].rearrange("p b (k j g) -> p g k j b", k=4, j=8)
            return v[:, bass.ds(c * 2 + s // 2, 1), 2 * (s % 2):2 * (s % 2) + 2].rearrange("p a k j b -> p (a k) j b")

        def gate_hidden(t):
            return hbuf[:, t % 4 // 2, 2 * (t % 2):2 * (t % 2) + 2, :]

        def merged_bias(b, k):
            return w1m[:, bass.ds(b, 1), F + k]

        turns = []
        for t in range(2):
            for k in range(2):
                for half in range(2):
                    turns.append((f"x{t}", [(xq[:, t, 4 * half + i, k * P:(k + 1) * P], P) for i in range(4)],
                                  xT[:, k, t * 1024:(t + 1) * 1024].rearrange("p (q w) -> p w q", w=8)[:, 4 * half:4 * half + 4, :], P))
            for g in ((2, 0), (1, 3))[t]:
                rows = P if g < 3 else E
                turns.append(("noisy" if g == 2 else "natural", [(wN[0:rows, 4 * g + i, :], rows) for i in range(4)],
                              wT[:, 4 * g:4 * g + 4, 0:rows], rows))
        for g in range(8):
            turns.append(("text", [(txn[0:NT, 4 * g + i, :], NT) for i in range(4)],
                          hT[:, 4 * g * N:(4 * g + 4) * N].rearrange("p (b n) -> p b n", n=N)[:, :, NP_:N], NT))
        X0, X1, TEXT = range(0, 6), range(6, 12), range(12, 20)

        block = ctx.enter_context(nc.Block())

        @block.sync
        def _(sp):
            first = CONST["select"][0]
            sp.dma_start(cst[:, 0:first], const[:, 0:first]).then_inc(S("const_in"), 16)
            for k, n in enumerate(("1", "2")):
                sp.dma_start(ei[:, k, :], tok[f"eps_in{n}"].unsqueeze(0).to_broadcast([P, 256])).then_inc(S("noise_in"), 16)
                sp.dma_start(V(f"eps_out{n}"), tok[f"eps_out{n}"].unsqueeze(1)).then_inc(S("noise_in"), 16)

            def load_images(t):
                sp.dma_start(xp[:, t].rearrange("p r w c -> p (r w c)"),
                             x[16 * t:16 * t + 16].rearrange("b o (q r) w -> (b o q) (r w)", q=8)).then_inc(S(f"x_in{t}"), 16)
            load_images(0)
            for k, n in enumerate(("1", "2")):
                sp.dma_start(sw[:, k, :], tok[f"W{n}_sw"]).then_inc(S("noisew_in"), 16)
                sp.dma_start(wraw[:, k, :], tok[f"W{n}_w"]).then_inc(S("noisew_in"), 16)
                sp.dma_start(V(f"W{n}_sb"), tok[f"W{n}_sb"].unsqueeze(1)).then_inc(S("noisew_in"), 16)
                sp.dma_start(V(f"W{n}_b"), tok[f"W{n}_b"].unsqueeze(1)).then_inc(S("noisew_in"), 16)
            load_images(1)
            nat = {"W3": tok["W3_w"], "gfc1": ffn["gfc1_w"], "proj": attn0["w_proj"], "v0": attn0["w_qkv"][256:384],
                   "Wq": attn1["Wq"], "Wk": attn1["Wk"], "Wv": attn1["Wv"], "Wp": attn1["Wp"]}
            for n, a in nat.items():
                sp.dma_start(wN[:, SLOT[n], :], a).then_inc(S("nat_in"), 16)
            for n, a in {"gfc2": ffn["gfc2_w"], "gate": moe["gate_w"], "tvg": ffn["tv_ln_g"], "tvs": ffn["tv_ln_b"]}.items():
                sp.dma_start(wN[0:E, SLOT[n], :], a).then_inc(S("nat_in"), 16)
            sp.dma_start(V("W3_b"), tok["W3_b"].unsqueeze(1)).then_inc(S("w3b_in"), 16)
            sp.dma_start(txn[0:NT, :, :], txt.rearrange("b n d -> n b d")).then_inc(S("txt_in"), 16)
            for k in range(2):
                sp.dma_start(wqk[:, k, :], attn0["w_qkv"][128 * k:128 * k + 128]).then_inc(S("vec_in"), 16)
            for n, a in {"b_proj": attn0["b_proj"], "gfc1_b": ffn["gfc1_b"], "ln_g": ffn["ln_g"],
                         "ln_b": ffn["ln_b"], "bq": attn1["bq"], "bk": attn1["bk"], "bv": attn1["bv"], "bp": attn1["bp"]}.items():
                sp.dma_start(V(n), a.unsqueeze(1)).then_inc(S("vec_in"), 16)
            sp.dma_start(cst[0:KC, first:], const[0:KC, first:]).then_inc(S("select_in"), 16)
            sp.dma_start(tvb[0:E, 0:F], ffn["tv_b1"]).then_inc(S("tvb_in"), 16)
            sp.dma_start(tvb[0:E, F:F + D], ffn["tv_b2"]).then_inc(S("tvb_in"), 16)
            sp.dma_start(tvb[E:E + 1, 0:F], ffn["b1"].unsqueeze(0)).then_inc(S("tvb_in"), 16)
            sp.dma_start(tvb[E:E + 1, F:F + D], ffn["b2"].unsqueeze(0)).then_inc(S("tvb_in"), 16)
            sp.wait_ge(S("g9_ones"), 1)
            sp.dma_start(g9[0:E, B:B + 1], ffn["gfc2_b"].unsqueeze(1)).then_inc(S("g9_in"), 16)
            meet(sp, "ln1")
            sp.wait_ge(S("tvc_zero"), 2)
            for w, (tv, base) in enumerate((("tv_W1", "W1"), ("tv_W2", "W2"))):
                tvr = ffn[tv].rearrange("e (j g) c -> (e j) (g c)", j=8)
                bsr = ffn[base].rearrange("(j g) c -> j (g c)", j=8)

                def load(n, r):
                    for half in range(2):
                        if not (is_known(n) and n == 0):
                            sp.wait_ge(S("mg_low"), n * 8 + (4 * r + 2 * half - 6))
                        at, cols = (n * 2 + (r - 8 * w)) * 1024 + 512 * half, slice(512 * half, 512 * half + 512)
                        sp.dma_start(tvc[0:64, r, cols], tvr[:, bass.ds(at, 512)]).then_inc(S(f"tv_in{r}{half}"), 16)
                        sp.dma_start(tvc[64:72, r, cols], bsr[:, bass.ds(at, 512)]).then_inc(S(f"tv_in{r}{half}"), 16)
                if w == 0:
                    load(0, 0)
                    load(0, 1)
                with sp.Fori(1 if w == 0 else 4, 4 if w == 0 else 8) as n:
                    for r in range(2):
                        load(n, r)
            meet(sp, "lnf")
            for i, (dst, src) in enumerate(((m_w1, "w1"), (m_w3, "w3"))):
                sp.dma_start(dst[:, 0:E, :], moe[src].rearrange("e d h -> d e h")).then_inc(S(f"moe_in{i}"), 16)
                sp.dma_start(dst[:, E, :], moe["s" + src]).then_inc(S(f"moe_in{i}"), 16)
            for k in range(2):
                sp.dma_start(m_w2[:, 0:E, k, :], moe["w2"].rearrange("e (k h) d -> k h e d", k=2)[k]).then_inc(S("moe_in2"), 16)
                sp.dma_start(m_w2[:, E, k, :], moe["sw2"].rearrange("(k h) d -> k h d", k=2)[k]).then_inc(S("moe_in2"), 16)
            sp.wait_ge(S("b_h"), B)
            sp.dma_start(m_bias[0:SUB, :], moe["biases"].unsqueeze(0).to_broadcast([SUB, E])).then_inc(S("bias_in"), 16)
            o = out.rearrange("b n d -> (b n) d").rearrange("(c s p) d -> c p s d", s=NSUB, p=SUB)

            sp.sem_inc(S("stored"), 16)
            with sp.Fori(0, NCH) as c:
                sp.wait_ge(S("out_copied"), c + 1)
                sp.dma_start(o[bass.ds(c, 1)].rearrange("a p s d -> (a p) s d"), m_o[0:SUB]).then_inc(S("stored"), 16)
            sp.wait_ge(S("stored"), 16 * (NCH + 1))

        def route_pe(pe, t, done):
            if 0 <= t - 1 < NCH:
                pe.wait_ge(S("r_sc"), t)
                if t >= 2:
                    pe.wait_ge(S("r_s"), t - 1)
                for s in range(NSUB):
                    mm = pe.transpose(bank[7][0:SUB, s * E:(s + 1) * E], m_sc[0:E, (t - 1) % 2, s * SUB:(s + 1) * SUB], ident[0:E, 0:E])
                mm.then_inc(S("r_tr"), 1)
            if 0 <= t < NCH:
                pe.wait_ge(S("ln_out"), done + t + 1)
                pe.matmul(bank[6][0:E, 0:CH], W("gate")[:, 0:E], chunk(xn, t), start=True, stop=True).then_inc(S("r_mm"), 1)

        def route_act(act, t):
            if 0 <= t < NCH:
                act.wait_ge(S("r_mm"), t + 1)
                if t >= 2:
                    act.wait_ge(S("r_tr"), t - 1)
                act.copy(m_sc[0:E, t % 2, :], bank[6][0:E, 0:CH]).then_inc(S("r_sc"), 1)

        def route_dve(dve, t):
            if 0 <= t < NCH:
                dve.wait_ge(S("r_tr"), t + 1)
                dve.tensor_copy(m_s[0:SUB, t * NSUB:(t + 1) * NSUB, :], bank[7][0:SUB, 0:NSUB * E].rearrange("p (s e) -> p s e", e=E)).then_inc(S("r_s"), 1)

        def ln_pe(pe, name):
            done = NCH * NORMS.index(name)
            ln_a = ln_early if name in ("ln1", "ln2") else ln_late
            src = xn if name == "lnf" else hT
            follows = name == "lna"

            def body(t, r):
                if live(t, 0, NCH):
                    if t >= 4 or follows:
                        pe.wait_ge(S("ln_out"), t + (done - 3))
                    if name == "ln2" and t == 0:
                        pe.wait_ge(S("a_u_ready"), B)
                        pe.wait_ge(S("a_h"), -(-CH // N))
                    if name == "ln2" and t == 1:
                        pe.wait_ge(S("a_e_ready"), B)
                        pe.wait_ge(S("a_t_ready"), B)
                        pe.wait_ge(S("a_h"), B)
                    if name == "lnm" and t == 0:
                        pe.wait_ge(S("b_vm_ready"), B)
                        pe.wait_ge(S("b_h"), -(-CH // N))
                    if name == "lnm" and t == 1:
                        pe.wait_ge(S("b_e_ready"), 3 * B)
                        pe.wait_ge(S("b_et_act"), B)
                        pe.wait_ge(S("b_h"), B)
                    if follows:
                        pe.wait_ge(S("lnf_added"), t + 1)
                    pe.matmul(bank[r][:, 0:CH], C("centre"), chunk(src, t), start=True, stop=True).then_inc(S("ln_cen"), 1)
                if live(t, 1, NCH):
                    q = (r - 1) % 4
                    pe.wait_ge(S("ln_sq"), t + done)
                    if t >= 3 or follows:
                        pe.wait_ge(S("ln_var_read"), t + (done - 2))
                    pe.matmul(bank[4 + q % 2][:, 0:CH], C("average"), ln_a[:, q, :], start=True, stop=True).then_inc(S("ln_var"), 1)
            for t in range(NCH + 1):
                body(t, t % 4)
                if name == "lnm":
                    route_pe(pe, t - 3, done)
            if name == "lnm":
                for t in range(NCH - 2, NCH + 1):
                    route_pe(pe, t, done)

        def ln_act(act, name):
            done = NCH * NORMS.index(name)
            ln_a = ln_early if name in ("ln1", "ln2") else ln_late
            follows = name == "lna"

            for t in range(NCH + 2):
                if live(t, 0, NCH):
                    act.wait_ge(S("ln_cen"), t + (done + 1))
                    if t >= 4 or follows:
                        act.wait_ge(S("ln_out"), t + (done - 3))
                    act.activation(ln_a[:, t % 4, :], bank[t % 4][:, 0:CH], ACT.Square).then_inc(S("ln_sq"), 1)
                if live(t, 2, NCH):
                    q = (t - 2) % 4
                    act.wait_ge(S("ln_var_read"), t + (done - 1))
                    act.activation(ln_a[:, q, :], ln_a[:, q, :], ACT.Exp, scale=-0.5).then_inc(S("ln_rs"), 1)
                if live(t, 1, NCH):
                    q = (t - 1) % 4
                    act.wait_ge(S("ln_var"), t + done)
                    act.activation(ln_a[:, q, :], bank[4 + q % 2][:, 0:CH], ACT.Ln, bias=V("eps")).then_inc(S("ln_var_read"), 1)
                if name == "lnm":
                    route_act(act, t - 3)
            if name == "lnm":
                route_act(act, NCH - 1)

        def ln_dve(dve, name):
            done = NCH * NORMS.index(name)
            ln_a = ln_early if name in ("ln1", "ln2") else ln_late

            def high_part(k):
                kind = slice(k * (E + 1) * HID, (k + 1) * (E + 1) * HID)
                dve.wait_ge(S(f"moe_in{k}"), 16 * (2 if k < 2 else 4))
                dve.tensor_copy(wparts[:, 0, kind], wraw_e[:, kind]).then_inc(S("w_high"), 1)

            def body(t, r):
                if name == "lnf" and t in (5, 8):
                    high_part(t // 8)
                if name == "lna" and t == 0:
                    high_part(2)
                dve.wait_ge(S("ln_rs"), t + (done + 1))
                if name != "lnf":
                    dve.tensor_tensor(chunk(xn, t), bank[r][:, 0:CH], ln_a[:, r, :], ALU.mult).then_inc(S("ln_out"), 1)
                else:
                    dve.scalar_tensor_tensor(chunk(xn, t), bank[r][:, 0:CH], V("lng"), ln_a[:, r, :], ALU.mult, ALU.mult).then_inc(S("ln_out"), 1)
                    dve.wait_ge(S("ln_out"), t + (done + 1))
                    dve.scalar_tensor_tensor(chunk(hT, t), chunk(xn, t), V("lnb"), chunk(hT, t), ALU.add, ALU.add).then_inc(S("lnf_added"), 1)
                if name == "lnm":
                    dve.wait_ge(S("ln_out"), t + (done + 1))
                    dve.tensor_copy(chunk(xh, t), chunk(xn, t)).then_inc(S("xh_ready"), 1)
            for t in range(NCH):
                if name == "lnm":
                    route_dve(dve, t - 3)
                body(t, t % 4)
            if name == "lnm":
                for t in range(NCH - 3, NCH):
                    route_dve(dve, t)

        @block.gpsimd
        def _(pool):
            pool.memset(V("eps"), LN_EPS).then_inc(S("eps_set"), 1)
            pool.memset(g9[:, B:B + 1], 1.0).then_inc(S("g9_ones"), 1)
            for c in range(4):
                pool.wait_ge(S("tok_n"), c + 1)
                pool.tensor_tensor(mish[:, c % 2, 4, :], mish[:, c % 2, 0, :], mish[:, c % 2, 2, :], ALU.mult).then_inc(S("tok_p"), 1)
            meet(pool, "ln1")
            pool.memset(tvc[64:P, :, :], 0.0).then_inc(S("tvc_zero"), 1)
            pool.memset(gblk[64:P, :, :], 0.0).then_inc(S("tvc_zero"), 1)
            pool.wait_ge(S("tvc_zero"), 2)
            normed(pool, "ln1", NCH)

            def stage0(t, r):
                reuse(pool, S("a_v_done"), t, 2)
                pool.tensor_copy(a_x[:, r, :], sample(xn, t)).then_inc(S("a_x_ready"), 1)
            run_steps(pool, B, 0, stage0, 2)
            with pool.Fori(0, 8) as n:
                for r in range(2):
                    for s in range(4):
                        pool.wait_ge(S("mg_high"), n * 8 + (4 * r + s + 1))
                        pool.tensor_tensor(mg_low[:, s, :], tvc[:, r, s * 256:(s + 1) * 256],
                                           mg_high[:, s, :].bitcast(F32), ALU.subtract).then_inc(S("mg_low"), 1)
            pool.wait_ge(S("mg_act"), 32)
            pool.wait_ge(S("mg_dve"), 32)

            def stage_w(t, r):
                reuse(pool, S("f_y"), t, 2)
                pool.tensor_copy(wst[:, r, F:2 * F], w2m[:, bass.ds(t, 1), :].rearrange("p a f -> p (a f)")).then_inc(S("f_w2"), 1)
            run_steps(pool, B, 0, stage_w, 2)
            meet(pool, "lnf")
            pool.memset(b_v[:, :, :, :], 0.0).then_inc(S("b_v_zero"), 1)
            step = (E + 1) * HID
            for k in range(3):
                kind = slice(k * step, (k + 1) * step)
                pool.wait_ge(S("w_high"), k + 1)
                pool.tensor_tensor(wparts[:, 1, kind], wraw_e[:, kind], wparts[:, 0, kind].bitcast(F32), ALU.subtract).then_inc(S("w_low"), 1)
            pool.wait_ge(S("w_low"), 3)
            normed(pool, "lna", NCH)

            def masked_keys(t, r):
                if live(t, 0, B):
                    pool.wait_ge(S("b_k_ready"), t + 1)
                    reuse3(pool, S("b_s_done"), t)
                    pool.tensor_tensor(b_km[:, r], b_k[:, r, :].unsqueeze(1).to_broadcast([P, H, N]),
                                       C("hmask").unsqueeze(2).to_broadcast([P, H, N]), ALU.mult).then_inc(S("b_km_ready"), 1)
                if live(t, 1, B):
                    q = (r - 1) % 2
                    reuse(pool, S("b_v_done"), t - 1, 2)
                    pool.tensor_copy(b_x[:, q, :], sample(xn, t - 1))
                    pool.tensor_copy(b_xt[:, q, :].rearrange("p (h n) -> p h n", h=H),
                                     xn[:, bass.ds((t - 1) * N + P, NTAIL)].unsqueeze(1).to_broadcast([P, H, NTAIL])).then_inc(S("b_x_ready"), 1)
            run_steps(pool, B, 1, masked_keys, 4)
            pool.wait_ge(S("b_h"), B)
            pool.memset(m_c40[:, :, :], 0.0).then_inc(S("c40_zero"), 1)
            pool.wait_ge(S("c40_zero"), 1)
            for c in range(NCH):
                pool.wait_ge(S("xh_ready"), c + 1)
                pool.tensor_tensor(chunk(xl, c), chunk(xn, c), chunk(xh, c).bitcast(F32), ALU.subtract).then_inc(S("xl_ready"), 1)
            pool.wait_ge(S("xl_ready"), NCH)
            pool.sem_inc(S("m_lo"), 3)

            def low_parts(c):
                for v in range(UN):
                    s = v % 3
                    pool.wait_ge(S("m_hi"), c * UN + (v + 1))
                    pool.tensor_tensor(m_hl[:, s, :], m_hf[:, s, :], m_hh[:, s, :].bitcast(F32), ALU.subtract).then_inc(S("m_lo"), 1)
            with pool.Fori(0, NCH // 2) as n:
                for r in range(2):
                    low_parts(n * 2 + r)

        @block.tensor
        def _(pe):
            pe.wait_ge(S("const_in"), 16)
            pe.wait_ge(S("psum_zero"), 8)

            def turn(units):
                for u in units:
                    kind, srcs, _, rows = turns[u]
                    if kind == "x0":
                        pe.wait_ge(S("xq_ready"), 1)
                    if kind == "x1":
                        pe.wait_ge(S("xq_ready"), 2)
                    if kind == "noisy":
                        pe.wait_ge(S("noisy"), 2)
                    if kind == "natural":
                        pe.wait_ge(S("nat_in"), 16 * 12)
                    if kind == "text":
                        pe.wait_ge(S("txt_in"), 16)
                    if u >= 3:
                        pe.wait_ge(S("turned_out"), u - 2)
                    for i, (src, rows) in enumerate(srcs):
                        mm = pe.transpose(bank[5 + u % 3][:, i * rows:(i + 1) * rows], src, ident[0:rows, 0:rows])
                    mm.then_inc(S("turned"), 1)

            def product(c, j):
                for k in range(2):
                    mm = pe.matmul(bank[2 * (c % 2) + j], W(("n1", "n2")[j] + "ab"[k]), xT[:, k, 512 * c:512 * c + 512], start=k == 0, stop=k == 1)
                return mm

            def gate(c):
                if c >= 2:
                    pe.wait_ge(S("tok_gb"), c - 1)
                product(c, 0).then_inc(S("tok_g"), 1)

            def value(c):
                if c >= 2:
                    pe.wait_ge(S("tok_x"), c - 1)
                product(c, 1).then_inc(S("tok_v"), 1)

            def project(c):
                pe.wait_ge(S("tok_x"), c + 1)
                if c:
                    pe.wait_ge(S("tok_h"), c)
                pe.matmul(bank[4], W("W3"), tokx[:, c % 2, :], start=True, stop=True).then_inc(S("tok_y"), 1)
            turn(X0[0:5])
            pe.wait_ge(S("turned_out"), 5)
            gate(0)
            turn(X0[5:6])
            value(0)
            gate(1)
            turn(X1)
            value(1)
            pe.wait_ge(S("turned_out"), len(X0) + len(X1))
            gate(2)
            project(0)
            value(2)
            gate(3)
            turn(TEXT[0:4])
            project(1)
            value(3)
            turn(TEXT[4:8])
            project(2)
            pe.wait_ge(S("turned_out"), len(turns))
            pe.wait_ge(S("vec_in"), 16 * 10)
            pe.matmul(bank[5][:, 0:P], wqk[:, 0, :], wqk[:, 1, :], start=True, stop=True)
            pe.matmul(bank[5][:, P:2 * P], wN[:, SLOT["v0"], :], W("proj"), start=True, stop=True)
            pe.wait_ge(S("wp_scaled"), 1)
            pe.matmul(bank[5][:, 2 * P:2 * P + 1], W("Wp"), V("bv"), start=True, stop=True).then_inc(S("wprod"), 1)
            project(3)
            meet(pe, "ln1")
            ln_pe(pe, "ln1")
            normed(pe, "ln1", 9)

            def attn0_step(t, r):
                q = (r - 1) % 2
                if live(t, 0, B):
                    reuse(pe, S("a_u_ready"), t, 1)
                    pe.matmul(bank[0][:, 0:N], pq[:, 0, :], sample(xn, t), start=True, stop=True).then_inc(S("a_u_done"), 1)
                if live(t, 3, B):
                    pe.wait_ge(S("a_a_ready"), t - 2)
                    reuse(pe, S("a_t_ready"), t - 3, 2)
                    tp = bank[5 + q]
                    pe.transpose(tp[:, 0:P], a_e[:, q, 0, 0:P], ident)
                    pe.transpose(tp[:, P:N], a_e[0:NTAIL, q, 1, 0:P], ident[0:NTAIL, 0:NTAIL])
                    pe.transpose(tp[0:NTAIL, N:N + P], a_e[:, q, 0, P:N], ident)
                    pe.transpose(tp[0:NTAIL, N + P:2 * N], a_e[0:NTAIL, q, 1, P:N], ident[0:NTAIL, 0:NTAIL]).then_inc(S("a_t_done"), 1)
                if live(t, 1, B):
                    if is_known(t) and t == 1:
                        normed(pe, "ln1", NCH)
                    pe.wait_ge(S("a_u_ready"), t)
                    reuse(pe, S("a_e_ready"), t - 1, 2)
                    sc = bank[1 + q]
                    pe.matmul(sc[:, 0:N], a_u[:, q, 0:P], sample(xn, t - 1), start=True, stop=True)
                    pe.matmul(sc[0:NTAIL, N:2 * N], a_u[:, q, P:N], sample(xn, t - 1), start=True, stop=True, skip_group_check=True).then_inc(S("a_s_done"), 1)
                if live(t, 3, B):
                    pe.wait_ge(S("a_x_ready"), t - 2)
                    reuse(pe, S("a_v_ready"), t - 3, 1)
                    pe.matmul(bank[7][:, 0:P], a_x[:, q, 0:P], pq[:, 1, :], start=True, stop=True)
                    pe.matmul(bank[7][0:NTAIL, P:2 * P], a_x[:, q, P:N], pq[:, 1, :], start=True, stop=True, skip_group_check=True).then_inc(S("a_v_done"), 1)
                if live(t, 4, B):
                    pe.wait_ge(S("a_v_ready"), t - 3)
                    pe.wait_ge(S("a_t_ready"), t - 3)
                    reuse(pe, S("a_h"), t - 4, 2)
                    o = bank[3 + r][:, 0:N]
                    pe.matmul(o, W("v0"), sample(xn, t - 4), start=True, stop=False)
                    pe.matmul(o, a_v[:, r, 0, :], a_t[:, r, 0, :], start=False, stop=False)
                    pe.matmul(o, a_v[0:NTAIL, r, 1, :], a_t[0:NTAIL, r, 1, :], start=False, stop=True).then_inc(S("a_o_done"), 1)
            run_steps(pe, B, 4, attn0_step, 6)
            ln_pe(pe, "ln2")
            for t in range(B // 2):
                if t < 4:
                    normed(pe, "ln2", 9 + t)
                reuse(pe, S("gh_done"), t, 4)
                pe.matmul(bank[t % 4][:, 0:GB], W("gfc1"), chunk(xn, t, GB), start=True, stop=True).then_inc(S("gh_mm"), 1)
            pe.wait_ge(S("gh_sum"), B // 2)
            pe.matmul(bank[4][0:E, 0:B], W("gfc2")[:, 0:E], ghm[:, :], start=True, stop=True).then_inc(S("g_mm"), 1)
            pe.wait_ge(S("g9_ready"), 2)
            pe.matmul(bank[5][0:72, 0:B], C("rep", E + 1), g9[:, 0:B], start=True, stop=True).then_inc(S("grep_mm"), 1)
            pe.wait_ge(S("tvb_in"), 64)
            for k in range(5):
                mm = pe.matmul(bank[6][:, k * B:(k + 1) * B], tvb[:, k * P:(k + 1) * P], g9[:, 0:B], start=True, stop=True, skip_group_check=True)
            mm.then_inc(S("bm_mm"), 1)
            pe.wait_ge(S("gblk_ready"), 1)
            def merge(n, r):
                for s in range(4):
                    pe.wait_ge(S("mg_low"), n * 8 + (4 * r + s + 1))
                    if not (is_known(n) and n == 0):
                        pe.wait_ge(S("mg_act" if s % 2 == 0 else "mg_dve"), n * 4 + (2 * r + s // 2 - 3))
                    for k in range(2):
                        dst, at = bank[4 * r + s][:, k * 256:(k + 1) * 256], slice(k * P, (k + 1) * P)
                        pe.matmul(dst, mg_high[:, s, at], gb_high[:, :], start=True, stop=False, skip_group_check=True)
                        pe.matmul(dst, mg_high[:, s, at], gb_low[:, :], start=False, stop=False, skip_group_check=True)
                        mm = pe.matmul(dst, mg_low[:, s, at], gb_high[:, :], start=False, stop=True, skip_group_check=True)
                    mm.then_inc(S("mg_mm"), 1)
            pe.wait_ge(S("bm_copied"), 1)
            for r in range(2):
                merge(0, r)
            with pe.Fori(1, 8) as n:
                for r in range(2):
                    merge(n, r)
            pe.wait_ge(S("mg_act"), 32)
            pe.wait_ge(S("mg_dve"), 32)

            def ffn_step(t, r):
                if live(t, 0, B):
                    pe.wait_ge(S("f_w1"), t + 1)
                    reuse(pe, S("f_h_act"), t, 2)
                    reuse(pe, S("f_h_dve"), t, 2)
                    for k in range(4):
                        mm = pe.matmul(bank[2 * r + k // 2][:, (k % 2) * N:(k % 2) * N + N], wst[:, r, k * P:(k + 1) * P],
                                       sample(xn, t), start=True, stop=True, skip_group_check=True)
                    mm.then_inc(S("f_mm"), 1)
                if live(t, 1, B):
                    q = (r - 1) % 2
                    pe.wait_ge(S("f_w2"), t)
                    pe.wait_ge(S("f_h_act"), t)
                    pe.wait_ge(S("f_h_dve"), t)
                    reuse(pe, S("f_res"), t - 1, 2)
                    for k in range(4):
                        mm = pe.matmul(bank[4 + q][:, 0:N], wst[:, q, F + k * P:F + (k + 1) * P], hbuf[:, q, k, :],
                                       start=k == 0, stop=k == 3)
                    mm.then_inc(S("f_y"), 1)
            run_steps(pe, B, 1, ffn_step, 4)
            meet(pe, "lnf")
            ln_pe(pe, "lnf")
            ln_pe(pe, "lna")
            normed(pe, "lna", 9)

            def attn1_step(t, r):
                q = (r - 1) % 2
                if live(t, 0, B):
                    reuse(pe, S("b_vm_ready"), t - 2, 1)
                    if is_known(t) and 0 < t < 3:
                        pe.wait_ge(S("b_k_ready"), t)
                    xs = sample(xn, t)
                    pe.matmul(bank[0][:, 0:N], W("Wq"), xs, start=True, stop=True)
                    pe.matmul(bank[0][:, N:2 * N], W("Wk"), xs, start=True, stop=True, skip_group_check=True).then_inc(S("b_qk_done"), 1)
                if live(t, 3, B):
                    pe.wait_ge(S("b_en_ready"), t - 2)
                    pe.wait_ge(S("b_tt_ready"), t - 2)
                    reuse(pe, S("b_et_act"), t - 3, 1)
                    reuse(pe, S("b_et_dve"), t - 3, 1)
                    ee = b_e[:, q]
                    for h in range(H):
                        pe.transpose(bank[5 + h // 4][:, (h % 4) * P:(h % 4) * P + P], ee[:, h, 0:P], ident)
                    pe.transpose(bank[7][:, 0:HT], ee[0:HT, 8, 0:P], ident[0:HT, 0:HT])
                    pe.transpose(bank[7][0:HT, HT:HT + P], b_ek[:, q, :], ident)
                    pe.matmul(bank[7][0:HT, HT + P:HT + N], b_tt[0:HT, q, :], C("dsel", HT), start=True, stop=True, skip_group_check=True).then_inc(S("b_t_done"), 1)
                if live(t, 4, B):
                    pe.wait_ge(S("b_o_ready"), t - 3)
                    pe.matmul(bank[1][:, 256:256 + N], W("Wp"), b_o[:, r, :], start=True, stop=True).then_inc(S("b_y_done"), 1)
                if live(t, 1, B):
                    if is_known(t) and t == 1:
                        normed(pe, "lna", NCH)
                    pe.wait_ge(S("b_km_ready"), t)
                    pe.wait_ge(S("b_qm_ready"), t)
                    for g in range(3):
                        if not (is_known(t) and t == 1):
                            pe.wait_ge(S("b_e_ready"), (t - 2) * 3 + (g + 1))
                        n = 3 if g < 2 else 2
                        mm = pe.matmul(ps3a[:, g, 0:n * N], b_q[:, q, 0:P], b_km[:, q, 3 * g:3 * g + n, :].rearrange("p h n -> p (h n)"), start=True, stop=True)
                        if g == 2:
                            mm = pe.matmul(ps3a[0:HT, 2, 2 * N:3 * N], b_qm[:, q].rearrange("p h n -> p (h n)"), b_k[:, q, :], start=True, stop=True, skip_group_check=True)
                        mm.then_inc(S("b_s_done"), 1)
                if live(t, 2, B):
                    pe.wait_ge(S("b_x_ready"), t - 1)
                    pe.wait_ge(S("b_k_ready"), min(t + 1, B) if is_known(t) else t + 1)
                    pe.matmul(bank[0][:, 0:P], b_x[:, r, 0:P], W("Wv"), start=True, stop=True)
                    pe.matmul(bank[0][0:HT, P:2 * P], b_xt[:, r, :], W("Wv"),
                              start=True, stop=True, skip_group_check=True).then_inc(S("b_v_done"), 1)
                if live(t, 3, B):
                    pe.wait_ge(S("b_et_act"), t - 2)
                    pe.wait_ge(S("b_et_dve"), t - 2)
                    pe.wait_ge(S("b_vm_ready"), t - 2)
                    reuse(pe, S("b_h"), t - 3, 1)
                    o = bank[1][:, 0:N]
                    for h in range(H):
                        pe.matmul(o, b_v[:, q, h, :], b_et[:, q, h, :], start=h == 0, stop=False)
                    pe.matmul(o, b_vt[0:HT, q, :], b_ett[0:HT, q, :], start=False, stop=True).then_inc(S("b_o_done"), 1)
            run_steps(pe, B, 4, attn1_step, 6)
            ln_pe(pe, "lnm")
            pe.wait_ge(S("comb"), 2)
            for c in range(NCH):
                if c >= 8:
                    pe.wait_ge(S(f"ct{c % 2}"), c // 2 - 3)
                for s in range(NSUB):
                    mm = pe.transpose(bank[c % 8][0:KC, s * SUB:(s + 1) * SUB], m_c40[0:SUB, c * NSUB + s, :], ident[0:SUB, 0:SUB])
                mm.then_inc(S("ct_tr"), 1)
            pe.wait_ge(S("xl_ready"), NCH)
            pe.wait_ge(S("ct0"), NCH // 2 - 1)
            pe.wait_ge(S("ct1"), NCH // 2 - 1)
            pe.sem_inc(S("m_tr"), 1)
            pe.sem_inc(S("m_y"), 3)

            def turn_out(cb):
                pe.wait_ge(S("cb_taken"), cb + 1)
                for s in range(NSUB):
                    mm = pe.transpose(bank[7][0:SUB, s * P:(s + 1) * P], m_f[:, s * SUB:(s + 1) * SUB], ident)
                mm.then_inc(S("m_tr"), 1)

            def three(dst, e, kind, k, high, low, start, stop_):
                pe.matmul(dst, expert(0, kind, e, k), high, start=start, stop=False)
                pe.matmul(dst, expert(0, kind, e, k), low, start=False, stop=False)
                return pe.matmul(dst, expert(1, kind, e, k), high, start=False, stop=stop_)

            def down(c, v):
                if v == 0:
                    pe.wait_ge(S("m_f"), c + 1)
                pe.wait_ge(S("m_lo"), c * UN + (v + 4))
                three(bank[6][:, 0:CH], ORDER[v // 2], 2, v % 2, m_hh[:, v % 3, :], m_hl[:, v % 3, :], v == 0, v == UN - 1).then_inc(S("m_y"), 1)

            def chunk_pe(c, first=False):
                for v in range(UN):
                    s = v % 3
                    cb = v // 2
                    if v == 1 and first:
                        pe.wait_ge(S("ct0"), NCH // 2)
                        pe.wait_ge(S("ct1"), NCH // 2)
                    pe.wait_ge(S("m_prod"), c * UN + (v + 1))
                    three(bank[2 * s][:, 0:CH], ORDER[v // 2], 0, v % 2, chunk(xh, c), chunk(xl, c), True, True)
                    three(bank[2 * s + 1][:, 0:CH], ORDER[v // 2], 1, v % 2, chunk(xh, c), chunk(xl, c), True, True).then_inc(S("m_ab"), 1)
                    if v == 6 and not first:
                        pe.wait_ge(S("m_f"), c + 1)
                        turn_out(c * E + 3)
                    if v % 2 == 1 and cb < E:
                        pe.wait_ge(S("cb_taken"), c * E + (cb + 1))
                        if v == 7 and not first:
                            pe.wait_ge(S("out_copied"), c)
                    if v >= 3:
                        down(c, v - 3)
                    elif not first:
                        down(c - 1, UN + v - 3)
                    if v % 2 == 1 and cb < E:
                        pe.matmul(bank[7][:, 0:CH], selr[0:KC, cb * P:(cb + 1) * P], m_ct[0:KC, bass.ds(c * CH, CH)],
                                  start=True, stop=True).then_inc(S("cb_mm"), 1)
            chunk_pe(0, True)
            with pe.Fori(0, (NCH - 2) // 2) as n:
                for r in range(2):
                    chunk_pe(n * 2 + (r + 1))
            chunk_pe(NCH - 1)
            for v in range(UN - 3, UN):
                down(NCH - 1, v)
            pe.wait_ge(S("m_f"), NCH + 1)
            turn_out(NCH * E)

        @block.scalar
        def _(act):
            act.wait_ge(S("noise_in"), 64)
            act.activation(ea[:, :, :], ei[:, :, :], ACT.Abs).then_inc(S("f_abs"), 1)
            act.activation(V("tmp0"), V("eps_out1"), ACT.Abs).then_inc(S("f_abs"), 1)
            act.activation(V("tmp1"), V("eps_out2"), ACT.Abs).then_inc(S("f_abs"), 1)
            act.activation(ei[:, :, :], ei[:, :, :], ACT.Sign).then_inc(S("f_sign"), 1)
            act.activation(V("eps_out1"), V("eps_out1"), ACT.Sign).then_inc(S("f_sign"), 1)
            act.activation(V("eps_out2"), V("eps_out2"), ACT.Sign).then_inc(S("f_sign"), 1)
            act.wait_ge(S("f_abs"), 3)
            act.wait_ge(S("f_sign"), 3)
            act.activation(ea[:, :, :], ea[:, :, :], ACT.Sqrt).then_inc(S("f_sqrt"), 1)
            act.activation(V("eo1"), V("tmp0"), ACT.Sqrt).then_inc(S("f_sqrt"), 1)
            act.activation(V("eo2"), V("tmp1"), ACT.Sqrt).then_inc(S("f_sqrt"), 1)
            act.preload_act_table_set("natural_log_exp_and_others")

            def turned(units):
                for u in units:
                    kind, srcs, dst, rows = turns[u]
                    act.wait_ge(S("turned"), u + 1)
                    act.copy(dst, bank[5 + u % 3][:, 0:len(srcs) * rows].rearrange("p (a b) -> p a b", a=len(srcs))).then_inc(S("turned_out"), 1)

            def gate_bias(c):
                act.wait_ge(S("tok_g"), c + 1)
                if c >= 2:
                    act.wait_ge(S("tok_p"), c - 1)
                act.activation(mish[:, c % 2, 0, :], bank[2 * (c % 2)], ACT.Identity, bias=V("b1n")).then_inc(S("tok_gb"), 1)

            def gate_exp(c):
                act.wait_ge(S("tok_m"), c + 1)
                act.activation(mish[:, c % 2, 1, :], mish[:, c % 2, 1, :], ACT.Exp).then_inc(S("tok_e"), 1)
            turned(X0[0:5])
            act.wait_ge(S("n_b"), 2)
            gate_bias(0)
            turned(X0[5:6])
            gate_exp(0)
            gate_bias(1)
            turned(X1)
            gate_exp(1)
            gate_bias(2)
            gate_exp(2)
            gate_bias(3)
            turned(TEXT[0:4])
            turned(TEXT[4:8])
            gate_exp(3)
            act.wait_ge(S("wprod"), 1)
            act.copy(pq[:, :, :], bank[5][:, 0:2 * P].rearrange("p (a b) -> p a b", a=2))
            act.activation(V("bpn"), bank[5][:, 2 * P:2 * P + 1], ACT.Identity, bias=V("bp"))
            meet(act, "ln1")
            ln_act(act, "ln1")

            def attn0_step(t, r):
                if live(t, 0, B):
                    act.wait_ge(S("a_u_done"), t + 1)
                    reuse(act, S("a_s_done"), t, 2)
                    act.copy(a_u[:, r, :], bank[0][:, 0:N]).then_inc(S("a_u_ready"), 1)
                if live(t, 3, B):
                    act.wait_ge(S("a_v_done"), t - 2)
                    reuse(act, S("a_o_done"), t - 3, 2)
                    act.copy(a_v[:, (r - 3) % 2].rearrange("p m n -> p (m n)"), bank[7][:, 0:2 * P]).then_inc(S("a_v_ready"), 1)
                if live(t, 1, B):
                    q = (r - 1) % 2
                    act.wait_ge(S("a_m_ready"), t)
                    reuse(act, S("a_t_done"), t - 1, 2)
                    act.activation(a_e[:, q, 0, :], bank[1 + q][:, 0:N], ACT.Exp, bias=a_m[:, q, 0:1], scale=D ** -0.5, accum_out=a_m[:, q, 2:3])
                    act.activation(a_e[0:NTAIL, q, 1, :], bank[1 + q][0:NTAIL, N:2 * N], ACT.Exp, bias=a_m[0:NTAIL, q, 1:2], scale=D ** -0.5,
                                   accum_out=a_m[0:NTAIL, q, 3:4]).then_inc(S("a_e_ready"), 1)
            run_steps(act, B, 3, attn0_step, 4)
            ln_act(act, "ln2")
            for t in range(B // 2):
                act.wait_ge(S("gh_mm"), t + 1)
                reuse(act, S("gh_sum"), t, 4)
                act.activation(gate_hidden(t).rearrange("p a n -> p (a n)"), bank[t % 4][:, 0:GB], ACT.Relu, bias=V("gfc1_b")).then_inc(S("gh_done"), 1)

            for w in range(2):
                with act.Fori(4 * w, 4 * w + 4) as n:
                    for r in range(2):
                        for s in (0, 2):
                            act.wait_ge(S("mg_mm"), n * 8 + (4 * r + s + 1))
                            act.copy(merged_dst(w, n * 2 + (r - 8 * w), s),
                                     bank[4 * r + s].rearrange("p (g j b) -> p g j b", g=2, j=8)).then_inc(S("mg_act"), 1)
            act.wait_ge(S("bm_copied"), 1)
            act.wait_ge(S("mg_act"), 32)
            act.wait_ge(S("mg_dve"), 32)

            def ffn_step(t, r):
                if live(t, 0, B):
                    reuse(act, S("f_mm"), t, 2)
                    act.copy(wst[:, r, 0:F], w1m[:, bass.ds(t, 1), 0:F].rearrange("p a f -> p (a f)")).then_inc(S("f_w1"), 1)
                if live(t, 1, B):
                    q = (r - 1) % 2
                    act.wait_ge(S("f_mm"), t)
                    reuse(act, S("f_y"), t - 1, 2)
                    act.activation(hbuf[:, q, 0, :], bank[2 * q][:, 0:N], ACT.Relu, bias=merged_bias(t - 1, 0))
                    act.activation(hbuf[:, q, 1, :], bank[2 * q][:, N:2 * N], ACT.Relu, bias=merged_bias(t - 1, 1)).then_inc(S("f_h_act"), 1)
            run_steps(act, B, 1, ffn_step, 4)
            meet(act, "lnf")
            ln_act(act, "lnf")
            ln_act(act, "lna")

            def attn1_step(t, r):
                if live(t, 0, B):
                    act.wait_ge(S("b_qk_done"), t + 1)
                    reuse3(act, S("b_s_done"), t)
                    act.activation(b_q[:, r, :], bank[0][:, 0:N], ACT.Identity, bias=V("bq")).then_inc(S("b_q_ready"), 1)
                    reuse(act, S("b_km_ready"), t, 2)
                    act.activation(b_k[:, r, :], bank[0][:, N:2 * N], ACT.Identity, bias=V("bk")).then_inc(S("b_k_ready"), 1)
                if live(t, 3, B):
                    act.wait_ge(S("b_t_done"), t - 2)
                    reuse(act, S("b_o_done"), t - 3, 2)
                    act.copy(b_et[:, (r - 3) % 2, 0:4, 0:P], bank[5].rearrange("p (h n) -> p h n", h=4)).then_inc(S("b_et_act"), 1)
                if live(t, 1, B):
                    q = (r - 1) % 2
                    reuse(act, S("b_t_done"), t - 1, 2)
                    for h in range(9):
                        if h % 3 == 0:
                            act.wait_ge(S("b_nm_ready"), (t - 1) * 3 + (h // 3 + 1))
                        rows = P if h < 8 else HT
                        ins = act.activation(b_e[0:rows, q, h, :], ps3a[0:rows, h // 3, (h % 3) * N:(h % 3) * N + N], ACT.Exp,
                                             bias=b_nm[0:rows, q, h:h + 1], accum_out=b_s[0:rows, q, h:h + 1])
                        if h % 3 == 2:
                            ins.then_inc(S("b_e_ready"), 1)
            run_steps(act, B, 3, attn1_step, 4)
            ln_act(act, "lnm")
            act.wait_ge(S("top_ready"), 1)
            for k in range(2):
                act.activation(m_1[k][0:SUB, :], m_1[k][0:SUB, :], ACT.Exp, scale=-1.0).then_inc(S("top_exp"), 1)
            act.wait_ge(S("c_high"), 1)
            act.wait_ge(S("c40_zero"), 1)
            act.copy(m_c40[0:SUB, :, 0:E], m_chi[0:SUB].bitcast(F32)).then_inc(S("comb"), 1)
            for c in range(0, NCH, 2):
                act.wait_ge(S("ct_tr"), c + 1)
                act.copy(m_ct[0:KC, c * CH:(c + 1) * CH], bank[c % 8][0:KC, 0:CH]).then_inc(S("ct0"), 1)
            act.sem_inc(S("cb_taken"), 1)

            def out_act(n):
                act.wait_ge(S("m_tr"), n + 1)
                act.wait_ge(S("stored"), n * 16)
                act.copy(m_o[0:SUB], bank[7][0:SUB].rearrange("p (s d) -> p s d", s=NSUB)).then_inc(S("out_copied"), 1)

            def high_part(c, v):
                act.wait_ge(S("m_prod"), c * UN + (v + 4))
                act.wait_ge(S("m_y"), c * UN + (v + 1))
                act.copy(m_hh[:, v % 3, :], m_hf[:, v % 3, :]).then_inc(S("m_hi"), 1)

            def chunk_act(c, first=False):
                for v in range(UN):
                    s, cb = v % 3, v // 2
                    act.wait_ge(S("m_ab"), c * UN + (v + 1))
                    act.wait_ge(S("m_prod"), c * UN + (v + 1))
                    act.activation(m_a[:, s, :], bank[2 * s][:, 0:CH], ACT.Silu).then_inc(S("m_silu"), 1)
                    if v == 6 and not first:
                        out_act(c)
                    if v >= 1:
                        high_part(c, v - 1)
                    elif not first:
                        high_part(c - 1, UN - 1)
                    if v % 2 == 1 and cb < E:
                        act.wait_ge(S("cb_mm"), c * E + (cb + 1))
                        act.wait_ge(S("cb_used"), c * E + (cb + 1))
                        act.copy(m_cb[:, cb % 2, :], bank[7][:, 0:CH]).then_inc(S("cb_taken"), 1)
            chunk_act(0, True)
            with act.Fori(0, (NCH - 2) // 2) as n:
                for r in range(2):
                    chunk_act(n * 2 + (r + 1))
            chunk_act(NCH - 1)
            high_part(NCH - 1, UN - 1)
            out_act(NCH)

        @block.vector
        def _(dve):
            for i in range(8):
                dve.memset(bank[i], 0.0).then_inc(S("psum_zero"), 1)

            def gather_pixels(t):
                dve.wait_ge(S(f"x_in{t}"), 16)
                dve.tensor_copy(xq[:, t].rearrange("p w (r c) -> p w r c", c=16), xp[:, t].rearrange("p r w c -> p w r c")).then_inc(S("xq_ready"), 1)
            gather_pixels(0)
            dve.wait_ge(S("f_sqrt"), 3)
            dve.wait_ge(S("noisew_in"), 16 * 8)
            dve.tensor_tensor(ei[:, :, :], ei[:, :, :], ea[:, :, :], ALU.mult).then_inc(S("n_f"), 1)
            dve.tensor_tensor(V("eo1"), V("eo1"), V("eps_out1"), ALU.mult).then_inc(S("n_f"), 1)
            dve.tensor_tensor(V("eo2"), V("eo2"), V("eps_out2"), ALU.mult).then_inc(S("n_f"), 1)
            dve.wait_ge(S("n_f"), 3)
            for k in range(2):
                dve.scalar_tensor_tensor(ea[:, k, :], ei[:, k, :], V(f"eo{k + 1}"), sw[:, k, :], ALU.mult, ALU.mult).then_inc(S("n_sw"), 1)
                dve.tensor_scalar(V(f"b{k + 1}n"), V(f"W{k + 1}_sb"), V(f"eo{k + 1}"), V(f"W{k + 1}_b"), ALU.mult, ALU.add).then_inc(S("n_b"), 1)
            dve.wait_ge(S("n_sw"), 2)
            for k in range(2):
                s0 = SLOT["n1a"] + 2 * k
                dve.tensor_tensor(wN[:, s0:s0 + 2, :], ea[:, k, :].rearrange("p (a c) -> p a c", a=2),
                                  wraw[:, k, :].rearrange("p (a c) -> p a c", a=2), ALU.add).then_inc(S("noisy"), 1)
            gather_pixels(1)

            def clamp(c):
                dve.wait_ge(S("tok_gb"), c + 1)
                dve.tensor_scalar(mish[:, c % 2, 1, :], mish[:, c % 2, 0, :], 30.0, None, ALU.min).then_inc(S("tok_m"), 1)

            def to_stream(c):
                dve.wait_ge(S("tok_y"), c + 1)
                dve.scalar_tensor_tensor(hT[:, 8 * c * N:(8 * c + 8) * N].rearrange("p (b n) -> p b n", n=N)[:, :, 0:NP_],
                                         bank[4].rearrange("p (b n) -> p b n", n=NP_), V("W3_b"),
                                         C("pos").unsqueeze(1).to_broadcast([P, 8, NP_]), ALU.add, ALU.add).then_inc(S("tok_h"), 1)
            dve.wait_ge(S("w3b_in"), 16)
            clamp(0)
            for c in range(4):
                m = mish[:, c % 2]
                dve.wait_ge(S("tok_e"), c + 1)
                dve.scalar_tensor_tensor(m[:, 2, :], m[:, 1, :], 2.0, m[:, 1, :], ALU.add, ALU.mult).then_inc(S("tok_n"), 1)
                dve.wait_ge(S("tok_n"), c + 1)
                dve.tensor_scalar(m[:, 3, :], m[:, 2, :], 2.0, None, ALU.add).then_inc(S("tok_d"), 1)
                dve.wait_ge(S("tok_d"), c + 1)
                dve.reciprocal(m[:, 3, :], m[:, 3, :]).then_inc(S("tok_r"), 1)
                if c < 3:
                    clamp(c + 1)
                if c >= 1:
                    to_stream(c - 1)
                dve.wait_ge(S("tok_p"), c + 1)
                dve.wait_ge(S("tok_r"), c + 1)
                dve.tensor_tensor(m[:, 4, :], m[:, 4, :], m[:, 3, :], ALU.mult).then_inc(S("tok_q"), 1)
                dve.wait_ge(S("tok_q"), c + 1)
                dve.wait_ge(S("tok_v"), c + 1)
                dve.scalar_tensor_tensor(tokx[:, c % 2, :], bank[2 * (c % 2) + 1], V("b2n"), m[:, 4, :], ALU.add, ALU.mult).then_inc(S("tok_x"), 1)
                if c == 1:
                    dve.wait_ge(S("turned_out"), len(X0) + len(X1))
                    dve.tensor_scalar(W("Wp"), W("Wp"), D ** -0.5, None, ALU.mult).then_inc(S("wp_scaled"), 1)
            dve.wait_ge(S("vec_in"), 16 * 10)
            for k, (v, n) in enumerate((("ln_g", "lng"), ("ln_b", "lnb"))):
                dve.tensor_scalar(tvln[:, k, :], W("tvg" if k == 0 else "tvs")[:, 0:E], V(v), None, ALU.subtract).then_inc(S("ln_d"), 1)
                dve.wait_ge(S("ln_d"), 3 * k + 1)
                dve.tensor_reduce(V(n), tvln[:, k, :], AX, ALU.add).then_inc(S("ln_d"), 1)
                dve.wait_ge(S("ln_d"), 3 * k + 2)
                dve.tensor_scalar(V(n), V(n), LN_MERGE, V(v), ALU.mult, ALU.add).then_inc(S("ln_d"), 1)
            to_stream(3)
            meet(dve, "ln1")
            ln_dve(dve, "ln1")

            def attn0_step(t, r):
                if live(t, 2, B):
                    dve.wait_ge(S("a_e_ready"), t - 1)
                    dve.reciprocal(a_m[:, r, 4:5], a_m[:, r, 2:3]).then_inc(S("a_r"), 1)
                    dve.reciprocal(a_m[0:NTAIL, r, 5:6], a_m[0:NTAIL, r, 3:4]).then_inc(S("a_rt"), 1)
                    dve.wait_ge(S("a_r"), t - 1)
                    dve.tensor_scalar(a_e[:, r, 0, :], a_e[:, r, 0, :], a_m[:, r, 4:5], None, ALU.mult)
                    dve.wait_ge(S("a_rt"), t - 1)
                    dve.tensor_scalar(a_e[0:NTAIL, r, 1, :], a_e[0:NTAIL, r, 1, :], a_m[0:NTAIL, r, 5:6], None, ALU.mult).then_inc(S("a_a_ready"), 1)
                if live(t, 1, B):
                    q = (r - 1) % 2
                    dve.wait_ge(S("a_s_done"), t)
                    reuse(dve, S("a_e_ready"), t - 1, 2)
                    dve.tensor_reduce(a_m[:, q, 0:2], bank[1 + q][:, 0:2 * N].rearrange("p (a n) -> p a n", a=2), AX, ALU.max, negate=True).then_inc(S("a_mx"), 1)
                    dve.wait_ge(S("a_mx"), t)
                    dve.tensor_scalar(a_m[:, q, 0:2], a_m[:, q, 0:2], D ** -0.5, None, ALU.mult).then_inc(S("a_m_ready"), 1)
                if live(t, 3, B):
                    q = (r - 3) % 2
                    dve.wait_ge(S("a_t_done"), t - 2)
                    reuse(dve, S("a_o_done"), t - 3, 2)
                    dve.tensor_copy(a_t[:, q].rearrange("p m n -> p (m n)"), bank[5 + q][:, 0:2 * N]).then_inc(S("a_t_ready"), 1)
                if live(t, 4, B):
                    dve.wait_ge(S("a_o_done"), t - 3)
                    dve.scalar_tensor_tensor(sample(hT, t - 4), bank[3 + r][:, 0:N], V("b_proj"), sample(hT, t - 4), ALU.add, ALU.add).then_inc(S("a_h"), 1)
            run_steps(dve, B, 4, attn0_step, 6)
            ln_dve(dve, "ln2")
            for t in range(B // 2):
                dve.wait_ge(S("gh_done"), t + 1)
                dve.tensor_reduce(ghm[:, 2 * t:2 * t + 2], gate_hidden(t), AX, ALU.add).then_inc(S("gh_sum"), 1)
            dve.wait_ge(S("g9_in"), 16)
            dve.wait_ge(S("g_mm"), 1)
            dve.memset(g9[:, 0:B], 1.0).then_inc(S("g9_ready"), 1)
            dve.wait_ge(S("g9_ready"), 1)
            dve.tensor_scalar(g9[0:E, 0:B], bank[4][0:E, 0:B], 1.0 / N, g9[0:E, B:B + 1], ALU.mult, ALU.add).then_inc(S("g9_ready"), 1)
            dve.wait_ge(S("grep_mm"), 1)
            dve.tensor_copy(gcol[:, :], bank[5][0:72, 0:B]).then_inc(S("gcol_ready"), 1)
            dve.wait_ge(S("gcol_ready"), 1)
            dve.tensor_tensor(gblk[0:72, :, :], gcol[:, :].unsqueeze(1).to_broadcast([72, 8, B]),
                              C("jmask", 72).unsqueeze(2).to_broadcast([72, 8, B]), ALU.mult).then_inc(S("gblk_set"), 1)
            dve.wait_ge(S("gblk_set"), 1)
            dve.wait_ge(S("tvc_zero"), 2)
            dve.tensor_copy(gb_high[:, :], gblk[:, :, :].rearrange("p j b -> p (j b)")).then_inc(S("gb_split"), 1)
            dve.wait_ge(S("gb_split"), 1)
            dve.tensor_tensor(gb_low[:, :], gblk[:, :, :].rearrange("p j b -> p (j b)"), gb_high[:, :].bitcast(F32), ALU.subtract).then_inc(S("gblk_ready"), 1)
            dve.wait_ge(S("bm_mm"), 1)
            dve.tensor_copy(w1m[:, :, F:F + 5].rearrange("p b k -> p k b"), bank[6][:, 0:5 * B].rearrange("p (k b) -> p k b", k=5)).then_inc(S("bm_copied"), 1)
            def high(n, r, s):
                if s % 2 == 0:
                    dve.wait_ge(S(f"tv_in{r}{s // 2}"), n * 32 + 32)
                if not (is_known(n) and n == 0 and r == 0):
                    dve.wait_ge(S("mg_mm"), n * 8 + (4 * r + s - 3))
                dve.tensor_copy(mg_high[:, s, :], tvc[:, r, s * 256:(s + 1) * 256]).then_inc(S("mg_high"), 1)

            def take(w, n, r, s):
                dve.wait_ge(S("mg_mm"), n * 8 + (4 * r + s + 1))
                dve.tensor_copy(merged_dst(w, n * 2 + (r - 8 * w), s),
                                bank[4 * r + s].rearrange("p (g j b) -> p g j b", g=2, j=8)).then_inc(S("mg_dve"), 1)

            def merge(w, n, last=False):
                for r in range(2):
                    following = (n, 1) if r == 0 else (n + 1, 0)
                    for s in range(4):
                        if not (last and r == 1):
                            high(*following, s)
                        if s % 2 == 1:
                            take(w, n, r, s)
            for s in range(4):
                high(0, 0, s)
            for w in range(2):
                with dve.Fori(4 * w, 4 * w + 4 - w) as n:
                    merge(w, n)
            merge(1, 7, True)
            dve.wait_ge(S("mg_dve"), 32)
            dve.wait_ge(S("mg_act"), 32)

            def ffn_step(t, r):
                if live(t, 0, B):
                    dve.wait_ge(S("f_mm"), t + 1)
                    reuse(dve, S("f_y"), t, 2)
                    for k in (2, 3):
                        ins = dve.tensor_scalar(hbuf[:, r, k, :], bank[2 * r + 1][:, (k - 2) * N:(k - 1) * N], merged_bias(t, k), 0.0, ALU.add, ALU.max)
                    ins.then_inc(S("f_h_dve"), 1)
                if live(t, 1, B):
                    q = (r - 1) % 2
                    dve.wait_ge(S("f_y"), t)
                    dve.scalar_tensor_tensor(sample(xn, t - 1), bank[4 + q][:, 0:N], merged_bias(t - 1, 4), sample(xn, t - 1), ALU.add, ALU.add).then_inc(S("f_res"), 1)
            run_steps(dve, B, 1, ffn_step, 4)
            meet(dve, "lnf")
            ln_dve(dve, "lnf")
            ln_dve(dve, "lna")

            def attn1_step(t, r):
                q = (r - 1) % 2
                if live(t, 2, B):
                    dve.wait_ge(S("b_e_ready"), t * 3 - 3)
                    dve.reciprocal(b_r[:, r, 0:8], b_s[:, r, 0:8]).then_inc(S("b_r1"), 1)
                    dve.reciprocal(b_r[0:HT, r, 8:9], b_s[0:HT, r, 8:9]).then_inc(S("b_r2"), 1)
                    dve.wait_ge(S("b_r1"), t - 1)
                    dve.tensor_tensor(b_ek[:, r, :].rearrange("p (h n) -> p h n", h=H), b_e[:, r, 0:8, P:N], b_r[:, r, 0:8].unsqueeze(2).to_broadcast([P, H, NTAIL]), ALU.mult)
                if live(t, 3, B):
                    dve.wait_ge(S("b_t_done"), t - 2)
                    reuse(dve, S("b_o_done"), t - 3, 2)
                    dve.tensor_copy(b_et[:, q, 4:8, 0:P], bank[6].rearrange("p (h n) -> p h n", h=4))
                    dve.tensor_copy(b_et[:, q, :, P:N], bank[7][:, 0:HT].rearrange("p (h n) -> p h n", h=H))
                    dve.tensor_copy(b_ett[0:HT, q, :], bank[7][0:HT, HT:HT + N]).then_inc(S("b_et_dve"), 1)
                if live(t, 4, B):
                    dve.wait_ge(S("b_y_done"), t - 3)
                    dve.scalar_tensor_tensor(sample(hT, t - 4), bank[1][:, 256:256 + N], V("bpn"), sample(hT, t - 4), ALU.add, ALU.add).then_inc(S("b_h"), 1)
                if live(t, 1, B):
                    for g in range(3):
                        dve.wait_ge(S("b_s_done"), (t - 1) * 3 + (g + 1))
                        dve.tensor_reduce(b_nm[:, q, 3 * g:3 * g + 3], ps3a[:, g, 0:3 * N].rearrange("p (h n) -> p h n", h=3), AX, ALU.max, negate=True).then_inc(S("b_nm_ready"), 1)
                if live(t, 2, B):
                    dve.wait_ge(S("b_v_done"), t - 1)
                    reuse(dve, S("b_o_done"), t - 2, 2)
                    dve.tensor_copy(diagonal(b_v, r), bank[0][:, 0:P].rearrange("p (h d) -> p h d", h=H))
                    dve.tensor_tensor(b_vt[0:HT, r, :], bank[0][0:HT, P:2 * P], C("vmask", HT), ALU.mult).then_inc(S("b_vm_ready"), 1)
                if live(t, 2, B):
                    dve.tensor_tensor(b_e[:, r, 0:8, 0:P], b_e[:, r, 0:8, 0:P], b_r[:, r, 0:8].unsqueeze(2).to_broadcast([P, H, P]), ALU.mult)
                    dve.wait_ge(S("b_r2"), t - 1)
                    dve.tensor_scalar(b_e[0:HT, r, 8, :], b_e[0:HT, r, 8, :], b_r[0:HT, r, 8:9], None, ALU.mult).then_inc(S("b_en_ready"), 1)
                    dve.wait_ge(S("b_en_ready"), t - 1)
                    dve.tensor_tensor(b_tt[0:HT, r, :].rearrange("p (h n) -> p h n", h=H), b_e[0:HT, r, 8, P:N].unsqueeze(1).to_broadcast([HT, H, NTAIL]),
                                      C("tmask", HT).rearrange("p (h n) -> p h n", h=H), ALU.mult).then_inc(S("b_tt_ready"), 1)
                if live(t, 0, B):
                    dve.wait_ge(S("b_q_ready"), t + 1)
                    reuse3(dve, S("b_s_done"), t)
                    dve.tensor_tensor(b_qm[:, r], b_q[:, r, P:N].unsqueeze(1).to_broadcast([P, H, NTAIL]),
                                      C("hmask").unsqueeze(2).to_broadcast([P, H, NTAIL]), ALU.mult).then_inc(S("b_qm_ready"), 1)
                if live(t, 3, B):
                    dve.wait_ge(S("b_o_done"), t - 2)
                    reuse(dve, S("b_y_done"), t - 3, 2)
                    dve.tensor_copy(b_o[:, q, :], bank[1][:, 0:N]).then_inc(S("b_o_ready"), 1)
            dve.wait_ge(S("b_v_zero"), 1)
            run_steps(dve, B, 4, attn1_step, 6)
            dve.wait_ge(S("select_in"), 16)
            dve.tensor_copy(selr[0:KC, :], C("select", KC))
            ln_dve(dve, "lnm")
            dve.wait_ge(S("bias_in"), 16)
            dve.wait_ge(S("r_s"), NCH)
            count = [0]

            def chain(ins):
                count[0] += 1
                ins.then_inc(S("router"), 1)
                dve.wait_ge(S("router"), count[0])
            SB = NCH * NSUB
            s_, b_, one1, one2, tmp = m_s[0:SUB], m_t[0][0:SUB], m_t[1][0:SUB], m_t[2][0:SUB], m_t[3][0:SUB]
            mx = m_1[4][0:SUB, :]

            def wide(v):
                return v.unsqueeze(2).to_broadcast([SUB, SB, E])

            def narrow(v):
                return v.unsqueeze(1).to_broadcast([SUB, SB, E])

            def first_best(onehot, val):
                chain(dve.tensor_reduce(mx, val, AX, ALU.max))
                chain(dve.tensor_tensor(onehot, val, wide(mx), ALU.is_equal))
                chain(dve.tensor_tensor(onehot, onehot, narrow(C("rank", SUB)), ALU.mult))
                chain(dve.tensor_reduce(m_1[3][0:SUB, :], onehot, AX, ALU.max))
                chain(dve.tensor_tensor(onehot, narrow(C("rank", SUB)), wide(m_1[3][0:SUB, :]), ALU.is_equal))

            def without(dst, val, onehot):
                chain(dve.scalar_tensor_tensor(dst, onehot, -BIG, val, ALU.mult, ALU.add))
            a, b, c = (x[0:SUB] for x in m_p)
            dve.tensor_tensor(a[:, :, 0:4], s_[:, :, 0:4], s_[:, :, 4:8], ALU.max)
            dve.tensor_tensor(a[:, :, 4:8], s_[:, :, 0:4], s_[:, :, 4:8], ALU.min).then_inc(S("top"), 1)
            dve.wait_ge(S("top"), 1)
            for n, src, dst in ((2, a, b), (1, b, c)):
                m = 2 * n
                dve.tensor_tensor(dst[:, :, 0:n], src[:, :, 0:n], src[:, :, n:m], ALU.max)
                dve.tensor_tensor(dst[:, :, 4:4 + n], src[:, :, 0:n], src[:, :, n:m], ALU.min)
                dve.tensor_tensor(dst[:, :, 6:6 + n], src[:, :, m:m + n], src[:, :, m + n:2 * m], ALU.max).then_inc(S("top"), 1)
                dve.wait_ge(S("top"), 6 - 2 * n)
                dve.tensor_tensor(dst[:, :, n:m], dst[:, :, 4:4 + n], dst[:, :, 6:6 + n], ALU.max).then_inc(S("top"), 1)
                dve.wait_ge(S("top"), 7 - 2 * n)
            dve.tensor_copy(m_1[0][0:SUB, :], c[:, :, 0])
            dve.tensor_copy(m_1[1][0:SUB, :], c[:, :, 1]).then_inc(S("top_ready"), 1)
            chain(dve.tensor_tensor(b_, s_, narrow(m_bias[0:SUB, :]), ALU.add))
            first_best(one1, b_)
            without(tmp, b_, one1)
            first_best(one2, tmp)
            dve.wait_ge(S("top_exp"), 2)
            w = [m[0:SUB, :] for m in m_1[0:3]]
            dve.tensor_scalar(w[0], w[0], 1.0, None, ALU.add).then_inc(S("share"), 1)
            dve.tensor_scalar(w[1], w[1], 1.0, None, ALU.add).then_inc(S("share"), 1)
            dve.wait_ge(S("share"), 2)
            dve.reciprocal(w[0], w[0]).then_inc(S("share"), 1)
            dve.reciprocal(w[1], w[1]).then_inc(S("share"), 1)
            dve.wait_ge(S("share"), 4)
            dve.tensor_tensor(w[2], w[0], w[1], ALU.add).then_inc(S("share"), 1)
            dve.wait_ge(S("share"), 5)
            dve.reciprocal(w[2], w[2]).then_inc(S("share"), 1)
            dve.wait_ge(S("share"), 6)
            dve.tensor_tensor(w[0], w[0], w[2], ALU.mult).then_inc(S("share"), 1)
            dve.tensor_tensor(w[1], w[1], w[2], ALU.mult).then_inc(S("share"), 1)
            dve.wait_ge(S("share"), 8)
            dve.tensor_tensor(one1, one1, wide(w[0]), ALU.mult).then_inc(S("share"), 1)
            dve.tensor_tensor(one2, one2, wide(w[1]), ALU.mult).then_inc(S("share"), 1)
            dve.wait_ge(S("share"), 10)
            dve.tensor_tensor(tmp, one1, one2, ALU.add).then_inc(S("share"), 1)
            dve.wait_ge(S("share"), 11)
            chi = m_chi[0:SUB]
            dve.tensor_copy(chi, tmp).then_inc(S("c_high"), 1)
            dve.wait_ge(S("c_high"), 1)
            dve.wait_ge(S("c40_zero"), 1)
            dve.tensor_tensor(m_c40[0:SUB, :, 32:32 + E], tmp, chi.bitcast(F32), ALU.subtract).then_inc(S("comb"), 1)
            for c in range(1, NCH, 2):
                dve.wait_ge(S("ct_tr"), c + 1)
                dve.tensor_copy(m_ct[0:KC, c * CH:(c + 1) * CH], bank[c % 8][0:KC, 0:CH]).then_inc(S("ct1"), 1)
            dve.sem_inc(S("m_prod"), 3)
            dve.sem_inc(S("m_f"), 1)
            dve.sem_inc(S("cb_used"), 2)

            def finish(n):
                dve.wait_ge(S("m_y"), n * UN + 3)
                dve.wait_ge(S("m_tr"), n)
                dve.tensor_tensor(m_f[:, :], bank[6][:, 0:CH], hT[:, bass.ds((n - 1) * CH, CH)], ALU.add).then_inc(S("m_f"), 1)

            def chunk_dve(c, first=False):
                for v in range(UN):
                    s, e = v % 3, ORDER[v // 2]
                    if v == 2 and not first:
                        finish(c)
                    dve.wait_ge(S("m_silu"), c * UN + (v + 1))
                    src = m_a[:, s, :]
                    if e < E:
                        if v % 2 == 0:
                            dve.wait_ge(S("cb_taken"), c * E + (e + 2))
                        used_up = "cb_used" if v % 2 == 1 else "cb_half"
                        dve.tensor_tensor(m_g[:, s, :], src, m_cb[:, e % 2, :], ALU.mult).then_inc(S(used_up), 1)
                        dve.wait_ge(S(used_up), c * E + (e + 1 + (2 if v % 2 == 1 else 0)))
                        src = m_g[:, s, :]
                    dve.wait_ge(S("m_lo"), c * UN + (v + 1))
                    dve.tensor_tensor(m_hf[:, s, :], bank[2 * s + 1][:, 0:CH], src, ALU.mult).then_inc(S("m_prod"), 1)
            chunk_dve(0, True)
            with dve.Fori(0, (NCH - 2) // 2) as n:
                for r in range(2):
                    chunk_dve(n * 2 + (r + 1))
            chunk_dve(NCH - 1)
            finish(NCH)


def diagonal(values, r):
    v = values[:, r].rearrange("p h n -> p (h n)")
    return bass.AP(v.tensor, v.offset, [v.ap[0], [P + HD, H], [1, HD]])


_INS = ['x', 'txt', 'L0_tok_W1_w', 'L0_tok_W1_b', 'L0_tok_W1_sw', 'L0_tok_W1_sb', 'L0_tok_W2_w', 'L0_tok_W2_b', 'L0_tok_W2_sw', 'L0_tok_W2_sb', 'L0_tok_W3_w', 'L0_tok_W3_b', 'L0_tok_eps_in1', 'L0_tok_eps_out1', 'L0_tok_eps_in2', 'L0_tok_eps_out2', 'L0_attn_w_qkv', 'L0_attn_w_proj', 'L0_attn_b_proj', 'L0_ffn_gfc1_w', 'L0_ffn_gfc1_b', 'L0_ffn_gfc2_w', 'L0_ffn_gfc2_b', 'L0_ffn_W1', 'L0_ffn_b1', 'L0_ffn_W2', 'L0_ffn_b2', 'L0_ffn_ln_g', 'L0_ffn_ln_b', 'L0_ffn_tv_W1', 'L0_ffn_tv_b1', 'L0_ffn_tv_W2', 'L0_ffn_tv_b2', 'L0_ffn_tv_ln_g', 'L0_ffn_tv_ln_b', 'L1_attn_Wq', 'L1_attn_bq', 'L1_attn_Wk', 'L1_attn_bk', 'L1_attn_Wv', 'L1_attn_bv', 'L1_attn_Wp', 'L1_attn_bp', 'L1_ffn_gate_w', 'L1_ffn_biases', 'L1_ffn_w1', 'L1_ffn_w3', 'L1_ffn_w2', 'L1_ffn_sw1', 'L1_ffn_sw3', 'L1_ffn_sw2']


def shape_constants(np):
    c = np.zeros((P, NCONST), np.float32)

    def put(name, a):
        at, n = CONST[name]
        c[0:a.shape[0], at:at + n] = a
    p = np.arange(P)
    put("ident", np.eye(P))
    put("centre", np.eye(P) - 1.0 / P)
    put("average", np.full((P, P), 1.0 / P))
    pos = np.arange(NP_, dtype=np.float32)[:, None]
    div = np.exp(np.arange(0, D, 2, dtype=np.float32) * np.float32(-np.log(10000.0) / D))
    ang = pos * div
    put("pos", np.stack([np.sin(ang), np.cos(ang)], axis=-1).reshape(NP_, D).T)
    put("jmask", (np.arange(72)[:, None] % 8 == np.arange(8)[None]))
    put("hmask", p[:, None] // HD == np.arange(H)[None])
    ht = np.arange(HT)
    put("vmask", ht[:, None] // NTAIL == p[None] // HD)
    put("tmask", ht[:, None] // NTAIL == ht[None] // NTAIL)
    put("dsel", ht[:, None] % NTAIL == np.arange(NTAIL)[None])
    put("rep", np.arange(E + 1)[:, None] == np.arange(72)[None] // 8)
    row = np.arange(KC)[:, None]
    put("select", ((row < E) | (row >= 32)) & (row % 32 == np.arange(E * P)[None] // P))
    put("rank", np.broadcast_to(E - np.arange(E), (P, E)))
    return c


def build(nc, args, const, out):
    def group(prefix):
        return {n[len(prefix):]: a for n, a in args.items() if n.startswith(prefix)}
    early_fusion(nc, args["x"], args["txt"], group("L0_tok_"), group("L0_attn_"), group("L0_ffn_"),
                 group("L1_attn_"), group("L1_ffn_"), const, out)


def kernel(**inputs):
    import numpy as _np
    import concourse.bacc as _bacc
    from concourse import mybir as _mybir
    from concourse.bass_utils import run_bass_kernel_spmd as _run

    nc = _bacc.Bacc("TRN2", target_bir_lowering=False, num_devices=1)
    arrays, args = {}, {}
    for name in _INS:
        a = _np.ascontiguousarray(inputs[name])
        arrays[f"in_{name}_dram"] = a
        args[name] = nc.dram_tensor(f"in_{name}_dram", a.shape, _mybir.dt.from_np(a.dtype), kind="ExternalInput").ap()
    arrays["shape_constants"] = shape_constants(_np)
    const = nc.dram_tensor("shape_constants", (P, NCONST), F32, kind="ExternalInput").ap()
    out = nc.dram_tensor("out_0_dram", (B, N, D), F32, kind="ExternalOutput").ap()
    build(nc, args, const, out)
    r = _run(nc, [arrays], core_ids=[0])
    return r.results[0]["out_0_dram"]
```
